# Optimizing a Trainium2 kernel written in Bass

```python
import numpy as np
import jax
import jax.numpy as jnp

def _softmax(x, axis=-1):
    return jax.nn.softmax(x, axis=axis)

def _gelu(x):
    return jax.nn.gelu(x, approximate=True)

def _silu(x):
    return jax.nn.silu(x)

def _sigmoid(x):
    return jax.nn.sigmoid(x)

def _layernorm(x, axis=-1, eps=1e-05):
    m = jnp.mean(x, axis=axis, keepdims=True)
    v = jnp.var(x, axis=axis, keepdims=True)
    return (x - m) / jnp.sqrt(v + eps)

def _scatter_add(tgt, idx, src, axis=0):
    return tgt.at[idx].add(src)

def _segment_sum(src, seg, n):
    return jax.ops.segment_sum(src, seg, n)
kernel_name = 'mk_flamingo_gated_d2_seqx_r8_244f69'

def setup_inputs(seed: int=0):
    np.random.seed(seed)
    _w = jnp.asarray

    def _rec_inputs():
        import jax
        import jax.numpy as jnp
        _rk = jax.random.key(seed)
        x = -0.0002928 + 1 * jax.random.normal(jax.random.fold_in(_rk, 1), (32, 128, 128), jnp.float32)
        _lenS = 128 - jax.random.randint(jax.random.fold_in(_rk, 7), (32,), 0, max(1, 128 // 4) + 1, jnp.int32)
        _lenS2 = 128 - jax.random.randint(jax.random.fold_in(_rk, 8), (32,), 0, max(1, 128 // 4) + 1, jnp.int32)
        _ctx_1024P = jax.random.normal(jax.random.fold_in(_rk, 11), (32, 16, 128), jnp.float32)
        _ctx_1024c = jax.random.dirichlet(jax.random.fold_in(_rk, 511), 0.3 * jnp.ones((16,), jnp.float32), (32, 128))
        _ctx_1024t = jnp.einsum('bsk,bkd->bsd', _ctx_1024c, _ctx_1024P)
        _ctx_1024t = _ctx_1024t * jax.lax.rsqrt(jnp.mean(jnp.square(_ctx_1024t)) + 1e-12) * 0.953939
        ctx_1024 = 4.13588e-05 + 0.999923 * (_ctx_1024t + 0.3 * jax.random.normal(jax.random.fold_in(_rk, 611), (32, 128, 128), jnp.float32))
        _validS = jnp.arange(128)[None, :] < _lenS[:, None]
        _validS2 = jnp.arange(128)[None, :] < _lenS2[:, None]
        _causal = jnp.tril(jnp.ones((128, 128), dtype=bool))
        mask_BxSxS2_if1 = jnp.where(jnp.ones((32, 128, 128), dtype=bool), 1, 0).astype(jnp.int32)
        _g = jax.random.normal(jax.random.fold_in(_rk, 9001), (2, 2), jnp.float32)
        _g = jnp.sign(_g) * jnp.maximum(jnp.abs(_g), 1.0) + (_g == 0) * 1.0
        g_xattn = _g[0]
        g_ffn = _g[1]
        return (x, ctx_1024, mask_BxSxS2_if1, g_xattn, g_ffn)
    x, ctx_1024, mask_BxSxS2_if1, g_xattn, g_ffn = _rec_inputs()

    def _L0_xattn_setup():
        import jax, jax.numpy as jnp
        import numpy as np
        HIDDEN = 128
        HEADS = 16
        HEAD_DIM = 64
        key = jax.random.key(seed)
        ks = jax.random.split(key, 7)
        B, Q, K = (2, 256, 512)
        s = 1.0 / np.sqrt(HIDDEN)
        return {'query': jax.random.normal(ks[0], (B, Q, HIDDEN), dtype=jnp.float32), 'key': jax.random.normal(ks[1], (B, K, HIDDEN), dtype=jnp.float32), 'value': jax.random.normal(ks[2], (B, K, HIDDEN), dtype=jnp.float32), 'w_q': jax.random.normal(ks[3], (HIDDEN, HEADS * HEAD_DIM), dtype=jnp.float32) * s, 'w_k': jax.random.normal(ks[4], (HIDDEN, HEADS * HEAD_DIM), dtype=jnp.float32) * s, 'w_v': jax.random.normal(ks[5], (HIDDEN, HEADS * HEAD_DIM), dtype=jnp.float32) * s, 'w_o': jax.random.normal(ks[6], (HEADS * HEAD_DIM, HIDDEN), dtype=jnp.float32) * s}
    _L0_xattn_all = _L0_xattn_setup()
    _L0_xattn_in = {k: v for k, v in _L0_xattn_all.items() if k in ('w_q', 'w_k', 'w_v', 'w_o')}
    del _L0_xattn_all

    def _L0_ffn_setup():
        import jax, jax.numpy as jnp
        import numpy as np
        DIM = 128

        def _reference_tuple_inner(x, W_r, W_k, W_v, mu_r, mu_k):
            B, T, C = x.shape
            x_prev = jnp.concatenate([jnp.zeros((B, 1, C), x.dtype), x[:, :-1, :]], axis=1)
            xr = mu_r * x + (1.0 - mu_r) * x_prev
            xk = mu_k * x + (1.0 - mu_k) * x_prev
            r = jax.nn.sigmoid(jnp.einsum('btc,dc->btd', xr, W_r))
            k = jnp.einsum('btc,dc->btd', xk, W_k)
            k_act = jnp.square(jax.nn.relu(k))
            out = r * jnp.einsum('btc,dc->btd', k_act, W_v)
            new_state = x[:, -1, :]
            return (out, new_state)
        key = jax.random.key(seed)
        ks = jax.random.split(key, 6)
        B, T, C = (8, 256, DIM)
        x = jax.random.normal(ks[0], (B, T, C), dtype=jnp.float32)
        s = 1.0 / np.sqrt(C)
        W_r = jax.random.uniform(ks[1], (C, C), jnp.float32, -s, s)
        W_k = jax.random.uniform(ks[2], (C, C), jnp.float32, -s, s)
        W_v = jax.random.uniform(ks[3], (C, C), jnp.float32, -s, s)
        mu_r = jax.random.uniform(ks[4], (C,), jnp.float32)
        mu_k = jax.random.uniform(ks[5], (C,), jnp.float32)
        return {'x': x, 'W_r': W_r, 'W_k': W_k, 'W_v': W_v, 'mu_r': mu_r, 'mu_k': mu_k}
    _L0_ffn_all = _L0_ffn_setup()
    _L0_ffn_in = {k: v for k, v in _L0_ffn_all.items() if k in ('W_r', 'W_k', 'W_v', 'mu_r', 'mu_k')}
    del _L0_ffn_all

    def _L1_xattn_setup():
        import jax, jax.numpy as jnp
        import numpy as np
        H = 16
        D_MODEL = 128
        D_K = D_MODEL // H
        B, S = (2, 256)

        def _split_heads(x):
            b, s, _ = x.shape
            return x.reshape(b, s, H, D_K).transpose(0, 2, 1, 3)
        key = jax.random.key(seed)
        ks = jax.random.split(key, 8)
        scale = 1.0 / np.sqrt(D_MODEL)
        return {'query': jax.random.normal(ks[0], (B, S, D_MODEL), jnp.float32), 'key': jax.random.normal(ks[1], (B, S, D_MODEL), jnp.float32), 'value': jax.random.normal(ks[2], (B, S, D_MODEL), jnp.float32), 'mask': jnp.ones((B, S, S), jnp.int32), 'Wq': jax.random.normal(ks[3], (D_MODEL, D_MODEL), jnp.float32) * scale, 'bq': jnp.zeros((D_MODEL,), jnp.float32), 'Wk': jax.random.normal(ks[4], (D_MODEL, D_MODEL), jnp.float32) * scale, 'bk': jnp.zeros((D_MODEL,), jnp.float32), 'Wv': jax.random.normal(ks[5], (D_MODEL, D_MODEL), jnp.float32) * scale, 'bv': jnp.zeros((D_MODEL,), jnp.float32), 'Wo': jax.random.normal(ks[6], (D_MODEL, D_MODEL), jnp.float32) * scale, 'bo': jnp.zeros((D_MODEL,), jnp.float32)}
    _L1_xattn_all = _L1_xattn_setup()
    _L1_xattn_in = {k: v for k, v in _L1_xattn_all.items() if k in ('Wq', 'bq', 'Wk', 'bk', 'Wv', 'bv', 'Wo', 'bo')}
    del _L1_xattn_all

    def _L1_ffn_setup():
        import jax, jax.numpy as jnp
        import numpy as np
        DIM = 128
        HID = 256
        E = 8
        K = 2
        R = 16
        B_, S_ = (2, 128)

        def _lora_in(xf, W, b, A, B):
            base = jnp.einsum('td,ehd->teh', xf, W)
            low = jnp.einsum('ter,ehr->teh', jnp.einsum('td,erd->ter', xf, A), B)
            return base + low + b

        def _lora_out(g, W, b, A, B):
            base = jnp.einsum('teh,edh->ted', g, W)
            low = jnp.einsum('ter,edr->ted', jnp.einsum('teh,erh->ter', g, A), B)
            return base + low + b
        key = jax.random.key(seed)
        ks = jax.random.split(key, 14)
        n = lambda k, shape, scale: jax.random.normal(k, shape, jnp.float32) * scale
        inp = {'x': jax.random.normal(ks[0], (B_, S_, DIM), jnp.float32), 'Wg': n(ks[1], (E, DIM), DIM ** (-0.5)), 'W1': n(ks[2], (E, HID, DIM), DIM ** (-0.5)), 'b1': jnp.zeros((E, HID), jnp.float32), 'A1': n(ks[3], (E, R, DIM), DIM ** (-0.5)), 'B1': n(ks[4], (E, HID, R), 0.01), 'W2': n(ks[5], (E, DIM, HID), HID ** (-0.5)), 'b2': jnp.zeros((E, DIM), jnp.float32), 'A2': n(ks[6], (E, R, HID), HID ** (-0.5)), 'B2': n(ks[7], (E, DIM, R), 0.01), 'W3': n(ks[8], (E, HID, DIM), DIM ** (-0.5)), 'b3': jnp.zeros((E, HID), jnp.float32), 'A3': n(ks[9], (E, R, DIM), DIM ** (-0.5)), 'B3': n(ks[10], (E, HID, R), 0.01)}
        return inp
    _L1_ffn_all = _L1_ffn_setup()
    _L1_ffn_in = {k: v for k, v in _L1_ffn_all.items() if k in ('Wg', 'W1', 'b1', 'A1', 'B1', 'W2', 'b2', 'A2', 'B2', 'W3', 'b3', 'A3', 'B3')}
    del _L1_ffn_all
    return {'x': x, 'ctx_1024': ctx_1024, 'mask_BxSxS2_if1': mask_BxSxS2_if1, 'g_xattn': g_xattn, 'g_ffn': g_ffn, 'L0_xattn_w_q': _L0_xattn_in['w_q'], 'L0_xattn_w_k': _L0_xattn_in['w_k'], 'L0_xattn_w_v': _L0_xattn_in['w_v'], 'L0_xattn_w_o': _L0_xattn_in['w_o'], 'L0_ffn_W_r': _L0_ffn_in['W_r'], 'L0_ffn_W_k': _L0_ffn_in['W_k'], 'L0_ffn_W_v': _L0_ffn_in['W_v'], 'L0_ffn_mu_r': _L0_ffn_in['mu_r'], 'L0_ffn_mu_k': _L0_ffn_in['mu_k'], 'L1_xattn_Wq': _L1_xattn_in['Wq'], 'L1_xattn_bq': _L1_xattn_in['bq'], 'L1_xattn_Wk': _L1_xattn_in['Wk'], 'L1_xattn_bk': _L1_xattn_in['bk'], 'L1_xattn_Wv': _L1_xattn_in['Wv'], 'L1_xattn_bv': _L1_xattn_in['bv'], 'L1_xattn_Wo': _L1_xattn_in['Wo'], 'L1_xattn_bo': _L1_xattn_in['bo'], 'L1_ffn_Wg': _L1_ffn_in['Wg'], 'L1_ffn_W1': _L1_ffn_in['W1'], 'L1_ffn_b1': _L1_ffn_in['b1'], 'L1_ffn_A1': _L1_ffn_in['A1'], 'L1_ffn_B1': _L1_ffn_in['B1'], 'L1_ffn_W2': _L1_ffn_in['W2'], 'L1_ffn_b2': _L1_ffn_in['b2'], 'L1_ffn_A2': _L1_ffn_in['A2'], 'L1_ffn_B2': _L1_ffn_in['B2'], 'L1_ffn_W3': _L1_ffn_in['W3'], 'L1_ffn_b3': _L1_ffn_in['b3'], 'L1_ffn_A3': _L1_ffn_in['A3'], 'L1_ffn_B3': _L1_ffn_in['B3']}

def reference(x, ctx_1024, mask_BxSxS2_if1, g_xattn, g_ffn, L0_xattn_w_q, L0_xattn_w_k, L0_xattn_w_v, L0_xattn_w_o, L0_ffn_W_r, L0_ffn_W_k, L0_ffn_W_v, L0_ffn_mu_r, L0_ffn_mu_k, L1_xattn_Wq, L1_xattn_bq, L1_xattn_Wk, L1_xattn_bk, L1_xattn_Wv, L1_xattn_bv, L1_xattn_Wo, L1_xattn_bo, L1_ffn_Wg, L1_ffn_W1, L1_ffn_b1, L1_ffn_A1, L1_ffn_B1, L1_ffn_W2, L1_ffn_b2, L1_ffn_A2, L1_ffn_B2, L1_ffn_W3, L1_ffn_b3, L1_ffn_A3, L1_ffn_B3):
    import jax
    import jax.numpy as jnp

    def _L0_xattn_ref(query, key, value, w_q, w_k, w_v, w_o):
        import jax, jax.numpy as jnp
        import numpy as np
        HIDDEN = 128
        HEADS = 16
        HEAD_DIM = 64
        B, Q, _ = query.shape
        Kl = key.shape[1]
        scale = HEAD_DIM ** (-0.5)
        q = (query @ w_q).reshape(B, Q, HEADS, HEAD_DIM).transpose(0, 2, 1, 3)
        k = (key @ w_k).reshape(B, Kl, HEADS, HEAD_DIM).transpose(0, 2, 1, 3)
        v = (value @ w_v).reshape(B, Kl, HEADS, HEAD_DIM).transpose(0, 2, 1, 3)
        scores = jnp.einsum('bhqd,bhkd->bhqk', q, k) * scale
        attn = jax.nn.softmax(scores, axis=-1)
        out = jnp.einsum('bhqk,bhkd->bhqd', attn, v)
        out = out.transpose(0, 2, 1, 3).reshape(B, Q, HEADS * HEAD_DIM)
        return out @ w_o

    def _L0_ffn_ref(x, W_r, W_k, W_v, mu_r, mu_k):
        import jax, jax.numpy as jnp
        import numpy as np
        DIM = 128

        def _reference_tuple_inner(x, W_r, W_k, W_v, mu_r, mu_k):
            B, T, C = x.shape
            x_prev = jnp.concatenate([jnp.zeros((B, 1, C), x.dtype), x[:, :-1, :]], axis=1)
            xr = mu_r * x + (1.0 - mu_r) * x_prev
            xk = mu_k * x + (1.0 - mu_k) * x_prev
            r = jax.nn.sigmoid(jnp.einsum('btc,dc->btd', xr, W_r))
            k = jnp.einsum('btc,dc->btd', xk, W_k)
            k_act = jnp.square(jax.nn.relu(k))
            out = r * jnp.einsum('btc,dc->btd', k_act, W_v)
            new_state = x[:, -1, :]
            return (out, new_state)
        return _reference_tuple_inner(x, W_r, W_k, W_v, mu_r, mu_k)[0]

    def _L1_xattn_ref(query, key, value, mask, Wq, bq, Wk, bk, Wv, bv, Wo, bo):
        import jax, jax.numpy as jnp
        import numpy as np
        H = 16
        D_MODEL = 128
        D_K = D_MODEL // H
        B, S = (2, 256)

        def _split_heads(x):
            b, s, _ = x.shape
            return x.reshape(b, s, H, D_K).transpose(0, 2, 1, 3)
        qs = _split_heads(query @ Wq + bq)
        ks = _split_heads(key @ Wk + bk)
        vs = _split_heads(value @ Wv + bv)
        scores = jnp.einsum('bhqd,bhkd->bhqk', qs, ks) / jnp.sqrt(jnp.float32(D_K))
        m = mask[:, None, :, :]
        scores = jnp.where(m == 0, -jnp.inf, scores)
        attn = jax.nn.softmax(scores, axis=-1)
        x = jnp.einsum('bhqk,bhkd->bhqd', attn, vs)
        x = x.transpose(0, 2, 1, 3).reshape(query.shape[0], -1, H * D_K)
        return x @ Wo + bo

    def _L1_ffn_ref(x, Wg, W1, b1, A1, B1, W2, b2, A2, B2, W3, b3, A3, B3):
        import jax, jax.numpy as jnp
        import numpy as np
        DIM = 128
        HID = 256
        E = 8
        K = 2
        R = 16
        B_, S_ = (2, 128)

        def _lora_in(xf, W, b, A, B):
            base = jnp.einsum('td,ehd->teh', xf, W)
            low = jnp.einsum('ter,ehr->teh', jnp.einsum('td,erd->ter', xf, A), B)
            return base + low + b

        def _lora_out(g, W, b, A, B):
            base = jnp.einsum('teh,edh->ted', g, W)
            low = jnp.einsum('ter,edr->ted', jnp.einsum('teh,erh->ter', g, A), B)
            return base + low + b
        orig_shape = x.shape
        xf = x.reshape(-1, x.shape[-1])
        scores = jax.nn.softmax(xf @ Wg.T, axis=-1)
        expert_weights, expert_indices = jax.lax.top_k(scores, K)
        expert_weights = expert_weights / expert_weights.sum(-1, keepdims=True)
        gates = (jax.nn.one_hot(expert_indices, E, dtype=xf.dtype) * expert_weights[..., None]).sum(axis=1)
        h1 = _lora_in(xf, W1, b1, A1, B1)
        h3 = _lora_in(xf, W3, b3, A3, B3)
        g = jax.nn.silu(h1) * h3
        y_e = _lora_out(g, W2, b2, A2, B2)
        y = jnp.einsum('te,ted->td', gates, y_e)
        return y.reshape(orig_shape)
    x = x + jnp.tanh(g_xattn[0]) * _L0_xattn_ref(_layernorm(x, axis=-1), ctx_1024, ctx_1024, L0_xattn_w_q, L0_xattn_w_k, L0_xattn_w_v, L0_xattn_w_o)
    x = x + jnp.tanh(g_ffn[0]) * _L0_ffn_ref(_layernorm(x, axis=-1), L0_ffn_W_r, L0_ffn_W_k, L0_ffn_W_v, L0_ffn_mu_r, L0_ffn_mu_k)
    x = x + jnp.tanh(g_xattn[1]) * _L1_xattn_ref(_layernorm(x, axis=-1), ctx_1024, ctx_1024, mask_BxSxS2_if1, L1_xattn_Wq, L1_xattn_bq, L1_xattn_Wk, L1_xattn_bk, L1_xattn_Wv, L1_xattn_bv, L1_xattn_Wo, L1_xattn_bo)
    x = x + jnp.tanh(g_ffn[1]) * _L1_ffn_ref(_layernorm(x, axis=-1), L1_ffn_Wg, L1_ffn_W1, L1_ffn_b1, L1_ffn_A1, L1_ffn_B1, L1_ffn_W2, L1_ffn_b2, L1_ffn_A2, L1_ffn_B2, L1_ffn_W3, L1_ffn_b3, L1_ffn_A3, L1_ffn_B3)
    return x

_drawn_inputs = setup_inputs


def setup_inputs(seed=0):
    import zlib

    import numpy as np

    out = dict(_drawn_inputs(seed))
    spreads = {'g_ffn': (-1.0, 0.6),
     'L1_xattn_bq': (0.0, 0.327),
     'L1_xattn_bk': (0.0, 2.0),
     'L1_xattn_bv': (0.0, 0.1),
     'L1_xattn_bo': (0.0, 0.1),
     'L1_ffn_b1': (0.0, 0.343),
     'L1_ffn_b2': (0.0, 0.425),
     'L1_ffn_b3': (0.0, 0.38)}
    factors = {'L0_ffn_W_r': 2.726,
     'L0_ffn_mu_r': 5.361,
     'L1_ffn_A1': 6.167,
     'L1_ffn_B1': 6.131,
     'L1_ffn_A2': 6.538,
     'L1_ffn_B2': 6.565,
     'L1_ffn_A3': 6.577,
     'L1_ffn_B3': 6.521}
    for name, (base, spread) in spreads.items():
        noise = np.random.default_rng([zlib.crc32(name.encode()), seed]).standard_normal(out[name].shape)
        drawn = base * np.exp(spread * noise) if base else spread * noise
        out[name] = jnp.asarray(drawn.astype(out[name].dtype))
    for name, factor in factors.items():
        out[name] = (out[name] * factor).astype(out[name].dtype)
    return out
```

```python
from contextlib import ExitStack

import concourse.bass as bass
from concourse import mybir

F32 = mybir.dt.float32
F16 = mybir.dt.float16
BF16 = mybir.dt.bfloat16
I32 = mybir.dt.int32
U32 = mybir.dt.uint32
ALU = mybir.AluOpType
ACT = mybir.ActivationFunctionType
AX = mybir.AxisListType

P = 128
EPS = 1e-5
H = 16
D0 = 64
D1 = 8
HG = 4
G = H // HG
E = 8
C = 2
R = 16
TILES = 4
BIG = 1e30


def gated_layers(nc, x, ctx, mask, g_xattn, g_ffn, wq0, wk0, wv0, wo0, w_r, w_k, w_v, mu_r, mu_k,
                 wq1, bq1, wk1, bk1, wv1, bv1, wo1, bo1, wg, w1, b1, a1, bb1, w2, b2, a2, bb2,
                 w3, b3, a3, bb3, out, stages=5):
    B = x.shape[0]
    with ExitStack() as whole:
        def sb(name, shape, dt=F32, to=whole):
            return to.enter_context(nc.sbuf_tensor(name, shape, dt))

        def sem(name):
            return whole.enter_context(nc.semaphore(name))

        bank = [whole.enter_context(nc.psum_tensor(f"bank{i}", [P, 512], F32)) for i in range(8)]

        xs = sb("xs", [P, B, P])
        masks = sb("masks", [P, B, P], I32)
        stat = sb("stat", [P, B, 6])
        mean = sb("mean", [P, B])
        spread = sb("spread", [P, B])
        var = sb("var", [P, B])
        rstd = sb("rstd", [P, B])
        veps = sb("veps", [P, B])
        minus_half = sb("minus_half", [P, B])
        ident = sb("ident", [P, P])
        ident4 = sb("ident4", [P, HG, P], BF16)
        minus_one_at = sb("minus_one_at", [P, H, P], BF16)
        slot_of = sb("slot_of", [P, HG])
        experts = sb("experts", [P, E])
        ones16 = sb("ones16", [1, P], F16)
        gain = sb("gain", [P, 4])
        half_gain = sb("half_gain", [P, 4])
        minus_half_gain = sb("minus_half_gain", [P, 4])
        NCOL = 2 * E * C + 5
        cols = sb("cols", [P, NCOL])
        b1_col, b3_col = cols[:, 0:E * C], cols[:, E * C:2 * E * C]
        bq_col, bk_col, bv_col = (cols[:, 2 * E * C + i:2 * E * C + i + 1] for i in range(3))
        mu = cols[:, NCOL - 2:NCOL]
        b2_row = sb("b2_row", [E, P])
        qk0 = sb("qk0", [P, 2, H, P], F16)
        v0 = sb("v0", [P, 2, H * D0], F16)
        o0 = sb("o0", [P, 2, G * 2, P], F16)
        mix = sb("mix", [P, 2, 5, P], F16)
        att1 = sb("att1", [P, 2, 4, P], F16)
        bias1 = sb("bias1", [1, 2, P], F16)
        router = sb("router", [P, 2, E], F16)
        up1 = sb("up1", [P, 2, E * C, P], F16)
        up3 = sb("up3", [P, 2, E * C, P], F16)
        down = sb("down", [P, 2, E * C, P], F16)

        x_loaded = sem("x_loaded")
        masks_loaded = sem("masks_loaded")
        stats_ready = sem("stats_ready")
        ln_ready = [sem(f"ln_ready{i}") for i in range(4)]

        def product(pe, to, left, right, start=True, stop=True):
            pe.matmul(to, left[0], right[0], start=start, stop=False)
            pe.matmul(to, left[0], right[1], start=False, stop=False)
            return pe.matmul(to, left[1], right[0], start=False, stop=stop)

        def ahead(eng, semaphore, n):
            if not isinstance(n, int) or n > 0:
                eng.wait_ge(semaphore, n)

        moment = sem("moment")
        veps_ready = sem("veps_ready")

        def layer_norm_moments(dve, n):
            before = 5 * n
            even, odd = (stat[:, :, 3 * i + 1] for i in range(2))
            dve.tensor_tensor(mean[:, :], even, odd, ALU.add).then_inc(moment, 1)
            dve.tensor_tensor(spread[:, :], even, odd, ALU.subtract).then_inc(moment, 1)
            dve.tensor_tensor(var[:, :], stat[:, :, 2], stat[:, :, 5], ALU.add).then_inc(moment, 1)
            dve.wait_ge(moment, before + 3)
            dve.tensor_scalar(mean[:, :], mean[:, :], 0.5, None, ALU.mult).then_inc(moment, 1)
            dve.scalar_tensor_tensor(out=spread[:, :], in0=spread[:, :], scalar=0.25, in1=spread[:, :],
                                     op0=ALU.mult, op1=ALU.mult).then_inc(moment, 1)
            dve.wait_ge(moment, before + 5)
            dve.tensor_scalar(var[:, :], var[:, :], 1.0 / P, EPS, ALU.mult, ALU.add).then_inc(var_ready, 1)
            dve.wait_ge(var_ready, n + 1)
            dve.tensor_tensor(veps[:, :], var[:, :], spread[:, :], ALU.add).then_inc(veps_ready, 1)

        def layer_norm_scale(pool, n):
            pool.wait_ge(veps_ready, n + 1)
            pool.tensor_tensor(rstd[:, :], veps[:, :], minus_half[:, :], ALU.pow).then_inc(ln_ready[n], 1)

        var_ready = sem("var_ready")

        with ExitStack() as prep:
            def stage_sb(name, shape, dt=F32):
                return sb(name, shape, dt, prep)

            wq0_s = stage_sb("wq0_s", [P, H * D0])
            wk0_s = stage_sb("wk0_s", [P, H * D0])
            wv0_s = stage_sb("wv0_s", [P, H * D0])
            wo0_s = stage_sb("wo0_s", [P, G * 2, P])
            qT = stage_sb("qT", [P, G * 2, P])
            kT = stage_sb("kT", [P, G * 2, P])
            mix_s = stage_sb("mix_s", [P, 3, P])
            mix_T = stage_sb("mix_T", [P, 3 * P + E])
            rows_s = stage_sb("rows_s", [NCOL, P])
            one_minus_mu = stage_sb("one_minus_mu", [P, 2])
            att1_s = stage_sb("att1_s", [P, 4, P])
            bo_row = stage_sb("bo_row", [1, P])
            bias1_s = stage_sb("bias1_s", [1, 2, P])
            wg_s = stage_sb("wg_s", [E, P])
            gains_in = stage_sb("gains_in", [P, 4])
            w1_s = stage_sb("w1_s", [P, E * C, P])
            w3_s = stage_sb("w3_s", [P, E * C, P])
            w2_s = stage_sb("w2_s", [P, E, C * P])
            a1_s = stage_sb("a1_s", [R, E, P])
            a3_s = stage_sb("a3_s", [R, E, P])
            a2_s = stage_sb("a2_s", [R, E, C * P])
            bb1_s = stage_sb("bb1_s", [P, E * C, R])
            bb3_s = stage_sb("bb3_s", [P, E * C, R])
            bb2_s = stage_sb("bb2_s", [P, E, R])
            bb1_T = stage_sb("bb1_T", [R, E * C, P])
            bb3_T = stage_sb("bb3_T", [R, E * C, P])
            bb2_T = stage_sb("bb2_T", [R, E, P])

            qk_loaded = sem("qk_loaded")
            vo_loaded = sem("vo_loaded")
            small_loaded = sem("small_loaded")
            mats_loaded = sem("mats_loaded")
            lora_loaded = sem("lora_loaded")
            up_loaded = sem("up_loaded")
            SMALL, MATS, LORA, UP = 12 * 16, 7 * 16, 6 * 16, 3 * 16
            ident_ready = sem("ident_ready")
            const_step = sem("const_step")
            turned = sem("turned")
            kept_even = sem("kept_even")
            kept_odd = sem("kept_odd")
            folded = sem("folded")
            folded_hi = sem("folded_hi")
            folded_lo = sem("folded_lo")
            gain_ready = sem("gain_ready")
            scales_ready = sem("scales_ready")
            raw_hi = sem("raw_hi")
            gained_hi = sem("gained_hi")
            prep_end = sem("prep_end")
            bias_done = sem("bias_done")
            bias_step = sem("bias_step")

            def turns():
                for src, dst in ((wq0_s, qT), (wk0_s, kT)):
                    for half in range(2):
                        yield ([src[:, c * P:(c + 1) * P] for c in range(4 * half, 4 * half + 4)],
                               dst[:, 4 * half:4 * half + 4, :].rearrange("p c d -> p (c d)"))
                yield ([mix_s[:, c, :] for c in range(3)] + [wg_s[:, :]], mix_T[:, :])
                yield [rows_s[:, :]], cols[:, :]
                for src, dst, n in ((bb1_s, bb1_T, E * C), (bb3_s, bb3_T, E * C), (bb2_s, bb2_T, E)):
                    for q in range(n // 4):
                        yield ([src[:, c, :] for c in range(4 * q, 4 * q + 4)],
                               dst[:, 4 * q:4 * q + 4, :].rearrange("p c d -> p (c d)"))

            TURNS = list(turns())
            NT = len(TURNS)
            FOLDS = G + 3 * (E * C // 4)

            def fold_target(n, part):
                if n < G:
                    first = 2 * HG * (n // 2) + n % 2
                    return qk0[:, part, first:first + 2 * HG - 1:2, :]
                which, q = divmod(n - G, E * C // 4)
                return (up1, up3, down)[which][:, part, 4 * q:4 * q + 4, :]

            def fold_bank(n):
                return bank[n % 8][:, :].rearrange("p (c d) -> p c d", d=P)

            heads = stage_sb("heads", [P, H])
            block = prep.enter_context(nc.Block())

            @block.sync
            def _(sp):
                sp.dma_start(wq0_s[:, :], wq0).then_inc(qk_loaded, 16)
                sp.dma_start(wk0_s[:, :], wk0).then_inc(qk_loaded, 16)
                for i, w in enumerate((w_r, w_k, w_v)):
                    sp.dma_start(mix_s[:, i, :], w).then_inc(mats_loaded, 16)
                for i, w in enumerate((wq1, wk1, wv1, wo1)):
                    sp.dma_start(att1_s[:, i, :], w).then_inc(mats_loaded, 16)
                sp.dma_start(bb1_s[:, :, :], bb1.rearrange("e (c p) r -> p (e c) r", p=P)).then_inc(lora_loaded, 16)
                sp.dma_start(bb3_s[:, :, :], bb3.rearrange("e (c p) r -> p (e c) r", p=P)).then_inc(lora_loaded, 16)
                sp.dma_start(bb2_s[:, :, :], bb2.rearrange("e d r -> d e r")).then_inc(lora_loaded, 16)
                sp.dma_start(a1_s[:, :, :], a1.rearrange("e r d -> r e d")).then_inc(lora_loaded, 16)
                sp.dma_start(a3_s[:, :, :], a3.rearrange("e r d -> r e d")).then_inc(lora_loaded, 16)
                sp.dma_start(a2_s[:, :, :], a2.rearrange("e r h -> r e h")).then_inc(lora_loaded, 16)
                sp.dma_start(w1_s[:, :, :], w1.rearrange("e (c p) d -> p (e c) d", p=P)).then_inc(up_loaded, 16)
                sp.dma_start(w3_s[:, :, :], w3.rearrange("e (c p) d -> p (e c) d", p=P)).then_inc(up_loaded, 16)
                sp.dma_start(w2_s[:, :, :], w2.rearrange("e d h -> d e h")).then_inc(up_loaded, 16)
                sp.dma_start(masks[:, :, :], mask.rearrange("b q k -> q b k")).then_inc(masks_loaded, 16)

            @block.scalar
            def _(act):
                act.dma_start(gains_in[:, 0:2], g_xattn.rearrange("(a n) -> a n", a=1).broadcast_to([P, 2])).then_inc(small_loaded, 16)
                act.dma_start(gains_in[:, 2:4], g_ffn.rearrange("(a n) -> a n", a=1).broadcast_to([P, 2])).then_inc(small_loaded, 16)
                act.dma_start(wg_s[:, :], wg).then_inc(small_loaded, 16)
                act.dma_start(rows_s[0:E * C, :], b1.rearrange("e (c p) -> (e c) p", p=P)).then_inc(small_loaded, 16)
                act.dma_start(rows_s[E * C:2 * E * C, :], b3.rearrange("e (c p) -> (e c) p", p=P)).then_inc(small_loaded, 16)
                for i, v in enumerate((bq1, bk1, bv1, mu_r, mu_k)):
                    act.dma_start(rows_s[2 * E * C + i:2 * E * C + i + 1, :], v.rearrange("(a n) -> a n", a=1))\
                       .then_inc(small_loaded, 16)
                act.dma_start(xs[:, :, :], x.rearrange("b s d -> s b d")).then_inc(x_loaded, 16)
                act.dma_start(bo_row[:, :], bo1.rearrange("(a n) -> a n", a=1)).then_inc(small_loaded, 16)
                act.dma_start(wv0_s[:, :], wv0).then_inc(vo_loaded, 16)
                act.dma_start(wo0_s[:, :, :], wo0.rearrange("(c p) d -> p c d", p=P)).then_inc(vo_loaded, 16)
                act.dma_start(b2_row[:, :], b2).then_inc(small_loaded, 16)
                for n in range(0, NT, 2):
                    srcs, dst = TURNS[n]
                    act.wait_ge(turned, n + 1)
                    act.activation(dst, bank[n % 8][0:dst.shape[0], 0:dst.shape[1]], ACT.Copy).then_inc(kept_even, 1)
                    if n == 4:
                        act.wait_ge(small_loaded, SMALL)
                        act.activation(gain[:, :], gains_in[:, :], ACT.Tanh).then_inc(gain_ready, 1)
                act.wait_ge(vo_loaded, 32)
                act.activation(v0[:, 0, :], wv0_s[:, :], ACT.Copy).then_inc(raw_hi, 1)
                act.wait_ge(mats_loaded, MATS)
                act.activation(att1[:, 0, 0:3, :], att1_s[:, 0:3, :], ACT.Copy).then_inc(raw_hi, 1)
                act.wait_ge(kept_even, 3)
                act.activation(router[:, 0, :], mix_T[:, 3 * P:3 * P + E], ACT.Copy).then_inc(raw_hi, 1)
                for n in range(FOLDS):
                    act.wait_ge(folded, n + 1)
                    act.activation(fold_target(n, 0), fold_bank(n), ACT.Copy).then_inc(folded_hi, 1)

            @block.gpsimd
            def _(pool):
                pool.memset(ident[:, :], 0.0).then_inc(const_step, 1)
                pool.wait_ge(const_step, 1)
                pool.affine_select(out=ident[:, :], in_=ident[:, :], compare_op=ALU.not_equal, fill=1.0,
                                   base=0, pattern=[[-1, P]], channel_multiplier=1).then_inc(ident_ready, 1)
                pool.memset(minus_half[:, :], -0.5).then_inc(const_step, 1)
                pool.memset(ones16[:, :], 1.0).then_inc(const_step, 1)
                pool.iota(experts[:, :], pattern=[[1, E]], base=0, channel_multiplier=0,
                          allow_small_or_imprecise_dtypes=True).then_inc(const_step, 1)
                pool.memset(minus_one_at[:, :, :], 0.0).then_inc(const_step, 1)
                pool.wait_ge(const_step, 5)
                for n, row in enumerate((0, 32)):
                    pool.wait_ge(const_step, 5 + n)
                    pool.affine_select(out=minus_one_at[:, :, :], in_=minus_one_at[:, :, :],
                                       compare_op=ALU.not_equal, fill=-1.0, base=-row,
                                       pattern=[[-1, H], [0, P]], channel_multiplier=1).then_inc(const_step, 1)
                pool.memset(heads[:, :], 1.0).then_inc(const_step, 1)
                pool.wait_ge(const_step, 8)
                pool.affine_select(out=heads[:, :], in_=heads[:, :], compare_op=ALU.is_ge, fill=0.0,
                                   base=0, pattern=[[-D1, H]], channel_multiplier=1).then_inc(const_step, 1)
                pool.wait_ge(const_step, 9)
                pool.affine_select(out=heads[:, :], in_=heads[:, :], compare_op=ALU.is_ge, fill=0.0,
                                   base=D1 - 1, pattern=[[D1, H]], channel_multiplier=-1).then_inc(const_step, 1)
                layer_norm_scale(pool, 0)

            @block.vector
            def _(dve):
                dve.wait_ge(ident_ready, 1)
                for i in range(HG):
                    last = dve.tensor_copy(ident4[:, i, :], ident[:, :])
                last.then_inc(prep_end, 1)
                for n in range(1, NT, 2):
                    srcs, dst = TURNS[n]
                    dve.wait_ge(turned, n + 1)
                    dve.tensor_copy(dst, bank[n % 8][0:dst.shape[0], 0:dst.shape[1]]).then_inc(kept_odd, 1)
                dve.wait_ge(gain_ready, 1)
                dve.tensor_scalar(half_gain[:, :], gain[:, :], 0.5, None, ALU.mult).then_inc(scales_ready, 1)
                dve.tensor_scalar(minus_half_gain[:, :], gain[:, :], -0.5, None, ALU.mult).then_inc(scales_ready, 1)
                dve.tensor_scalar(one_minus_mu[:, :], mu, -1.0, 1.0, ALU.mult, ALU.add).then_inc(scales_ready, 1)
                dve.wait_ge(const_step, 10)
                dve.tensor_reduce(slot_of[:, :], heads[:, :].rearrange("p (j i) -> p i j", i=HG), AX.X, ALU.add)\
                   .then_inc(scales_ready, 1)
                dve.wait_ge(scales_ready, 4)
                dve.wait_ge(kept_even, 3)
                dve.wait_ge(vo_loaded, 32)
                dve.wait_ge(mats_loaded, MATS)
                scaled = [(mix[:, :, 0, :], mix_T[:, 0:P], mu[:, 0:1]),
                          (mix[:, :, 1, :], mix_T[:, 0:P], one_minus_mu[:, 0:1]),
                          (mix[:, :, 2, :], mix_T[:, P:2 * P], mu[:, 1:2]),
                          (mix[:, :, 3, :], mix_T[:, P:2 * P], one_minus_mu[:, 1:2]),
                          (mix[:, :, 4, :], mix_T[:, 2 * P:3 * P], half_gain[:, 2:3]),
                          (o0[:, :, :, :].rearrange("p a c d -> p a (c d)"),
                           wo0_s[:, :, :].rearrange("p c d -> p (c d)"), gain[:, 0:1]),
                          (att1[:, :, 3, :], att1_s[:, 3, :], gain[:, 1:2])]
                for n, (to, w, by) in enumerate(scaled):
                    dve.tensor_scalar(to[:, 0], w, by, None, ALU.mult).then_inc(gained_hi, 1)
                for n, (to, w, by) in enumerate(scaled):
                    dve.wait_ge(gained_hi, n + 1)
                    dve.scalar_tensor_tensor(out=to[:, 1], in0=w, scalar=by, in1=to[:, 0],
                                             op0=ALU.mult, op1=ALU.subtract).then_inc(prep_end, 1)
                dve.wait_ge(raw_hi, 3)
                dve.tensor_tensor(v0[:, 1, :], wv0_s[:, :], v0[:, 0, :], ALU.subtract).then_inc(prep_end, 1)
                dve.tensor_tensor(att1[:, 1, 0:3, :], att1_s[:, 0:3, :], att1[:, 0, 0:3, :], ALU.subtract).then_inc(prep_end, 1)
                dve.tensor_tensor(router[:, 1, :], mix_T[:, 3 * P:3 * P + E], router[:, 0, :], ALU.subtract).then_inc(prep_end, 1)
                for n in range(FOLDS):
                    dve.wait_ge(folded_hi, n + 1)
                    dve.tensor_tensor(fold_target(n, 1), fold_bank(n), fold_target(n, 0), ALU.subtract)\
                       .then_inc(folded_lo, 1)
                dve.wait_ge(bias_done, 1)
                dve.tensor_tensor(bias1_s[:, 0, :], bank[0][0:1, 0:P], bo_row[:, :], ALU.add).then_inc(bias_step, 1)
                dve.wait_ge(bias_step, 1)
                dve.tensor_scalar(bias1_s[:, 1, :], bias1_s[:, 0, :], gain[0:1, 1:2], None, ALU.mult).then_inc(bias_step, 1)
                dve.wait_ge(bias_step, 2)
                dve.tensor_copy(bias1[:, 0, :], bias1_s[:, 1, :]).then_inc(bias_step, 1)
                dve.wait_ge(bias_step, 3)
                dve.tensor_tensor(bias1[:, 1, :], bias1_s[:, 1, :], bias1[:, 0, :], ALU.subtract).then_inc(prep_end, 1)
                dve.wait_ge(x_loaded, 16)
                with dve.Fori(0, B) as b:
                    dve.bn_stats(stat[:, bass.ds(b, 1), :], xs[:, bass.ds(b, 1), :]).then_inc(stats_ready, 1)
                dve.wait_ge(stats_ready, B)
                layer_norm_moments(dve, 0)

            @block.tensor
            def _(pe):
                pe.wait_ge(ident_ready, 1)
                for n, (srcs, dst) in enumerate(TURNS):
                    if n >= 8:
                        pe.wait_ge(kept_odd if n % 2 else kept_even, (n - 8) // 2 + 1)
                    if n == 0:
                        pe.wait_ge(qk_loaded, 32)
                    if n == 4:
                        pe.wait_ge(mats_loaded, MATS)
                        pe.wait_ge(small_loaded, SMALL)
                    if n == 6:
                        pe.wait_ge(lora_loaded, LORA)
                    for i, s in enumerate(srcs):
                        rows, cols = s.shape
                        last = pe.transpose(bank[n % 8][0:cols, i * P:i * P + rows], s, ident[0:rows, 0:rows])
                    last.then_inc(turned, 1)
                pe.wait_ge(kept_even, (NT + 1) // 2)
                pe.wait_ge(kept_odd, NT // 2)
                pe.wait_ge(up_loaded, UP)
                for n in range(FOLDS):
                    if n >= 8:
                        pe.wait_ge(folded_lo, n - 7)
                    to = bank[n % 8]
                    for i in range(4):
                        where = to[:, i * P:(i + 1) * P]
                        if n < G:
                            h = 2 * HG * (n // 2) + n % 2 + 2 * i
                            rows = slice(D0 * (h % 2), D0 * (h % 2) + D0)
                            last = pe.matmul(where, qT[rows, h // 2, :], kT[rows, h // 2, :], start=True, stop=True)
                            continue
                        which, q = divmod(n - G, E * C // 4)
                        u = 4 * q + i
                        e, c = divmod(u, C)
                        if which == 2:
                            pe.matmul(where, w2_s[:, e, c * P:(c + 1) * P], ident[:, :], start=True, stop=False)
                            last = pe.matmul(where, a2_s[:, e, c * P:(c + 1) * P], bb2_T[:, e, :], start=False, stop=True)
                        else:
                            w, a, bT = ((w1_s, a1_s, bb1_T), (w3_s, a3_s, bb3_T))[which]
                            pe.matmul(where, w[:, u, :], ident[:, :], start=True, stop=False)
                            last = pe.matmul(where, a[:, e, :], bT[:, u, :], start=False, stop=True)
                    last.then_inc(folded, 1)
                pe.wait_ge(folded_lo, FOLDS - 7)
                pe.matmul(bank[0][0:1, 0:P], bv_col, att1_s[:, 3, :], start=True, stop=True).then_inc(bias_done, 1)


        if stages >= 1:
            with ExitStack() as att:
                def a_sb(name, shape, dt=F32):
                    return sb(name, shape, dt, att)

                xn = a_sb("xn", [P, P])
                ctx_in = a_sb("ctx_in", [P, 2, P])
                xcT = a_sb("xcT", [P, 2, 2, 2 * P], F16)
                t_s = a_sb("t_s", [P, 2, 2, H, P], F16)
                v_s = a_sb("v_s", [P, 2, 2, H, D0 + 1], F16)
                peak = a_sb("peak", [P, H])
                peakT = a_sb("peakT", [P, 2, P], BF16)
                prob = a_sb("prob", [P, 2, HG * P])
                prob_hi = a_sb("prob_hi", [P, 2, HG * P], F16)
                prob_lo = a_sb("prob_lo", [P, 2, HG * P], F16)
                inv = a_sb("inv", [P, 2, HG])
                o_s = a_sb("o_s", [P, 2, HG, D0])
                oT = a_sb("oT", [P, 2, G * 2, P], F16)

                ctx_loaded = [sem(f"ctx_loaded{i}") for i in range(2)]
                blanks_ready = sem("blanks_ready")
                xn_ready = sem("xn_ready")
                turn_done = sem("turn_done")
                turn_hi = sem("turn_hi")
                turn_lo = sem("turn_lo")
                proj_done = sem("proj_done")
                proj_hi = sem("proj_hi")
                proj_lo = sem("proj_lo")
                rough_done = sem("rough_done")
                peak_done = sem("peak_done")
                score_done = sem("score_done")
                exp_done = sem("exp_done")
                problo_done = sem("problo_done")
                pv_done = sem("pv_done")
                inv_done = sem("inv_done")
                norm_done = sem("norm_done")
                oturn_done = sem("oturn_done")
                oturn_hi = sem("oturn_hi")
                oturn_lo = sem("oturn_lo")
                out_done = sem("out_done")
                res_done = sem("res_done")
                stat_done = sem("stat_done")

                TURN, OUTB, ROUGH, PVB = bank[0], bank[7], bank[3], bank[6]
                PAIRS = (B - 2) // 2

                def pair(t, part):
                    return [t[:, part, i] for i in range(2)]

                block = att.enter_context(nc.Block())

                @block.sync
                def _(sp):
                    def load(c, par):
                        ahead(sp, turn_done, 2 * c - 3)
                        sp.dma_start(ctx_in[:, par:par + 1, :],
                                     ctx[bass.ds(c, 1), :, :].rearrange("a s d -> s a d")).then_inc(ctx_loaded[par], 16)
                    load(0, 0)
                    load(1, 1)
                    with sp.Fori(0, PAIRS) as i:
                        load(2 * i + 2, 0)
                        load(2 * i + 3, 1)

                @block.gpsimd
                def _(pool):
                    pool.memset(peakT[:, :, :], 0.0).then_inc(blanks_ready, 1)
                    pool.memset(v_s[:, :, 0, :, D0:D0 + 1], 1.0).then_inc(blanks_ready, 1)
                    pool.memset(v_s[:, :, 1, :, D0:D0 + 1], 0.0).then_inc(blanks_ready, 1)

                    def group(n, par):
                        pool.wait_ge(exp_done, n + 1)
                        ahead(pool, pv_done, n - 1)
                        pool.tensor_tensor(prob_lo[:, par, :], prob[:, par, :], prob_hi[:, par, :],
                                           ALU.subtract).then_inc(problo_done, 1)
                    for n in range(G):
                        group(n, n % 2)
                    with pool.Fori(1, B) as b:
                        for g in range(G):
                            group(G * b + g, g % 2)

                @block.scalar
                def _(act):
                    def hi_turned(a, par):
                        act.wait_ge(turn_done, 2 * a + 1)
                        act.activation(xcT[:, par, 0, :], TURN[:, 0:2 * P], ACT.Copy).then_inc(turn_hi, 1)

                    def hi_peak(a, par):
                        act.wait_ge(turn_done, 2 * a + 2)
                        act.activation(peakT[0:H, par, :], TURN[0:H, 0:P], ACT.Copy).then_inc(turn_hi, 1)

                    def hi_t(a, par, g):
                        act.wait_ge(proj_done, 6 * a + g + 1)
                        act.activation(t_s[:, par, 0, HG * g:HG * g + HG, :].rearrange("p h q -> p (h q)"),
                                       bank[1 + g % 2][:, :], ACT.Copy).then_inc(proj_hi, 1)

                    def hi_v(a, par, j):
                        act.wait_ge(proj_done, 6 * a + G + j + 1)
                        act.activation(v_s[:, par, 0, 8 * j:8 * j + 8, 0:D0],
                                       bank[1 + j][:, :].rearrange("p (h d) -> p h d", d=D0), ACT.Copy).then_inc(proj_hi, 1)

                    def exps(b, g):
                        n = G * b + g
                        act.wait_ge(score_done, n + 1)
                        ahead(act, problo_done, n - 1)
                        ahead(act, pv_done, n - 1)
                        act.activation(prob[:, g % 2, :], bank[4 + g % 2][:, :], ACT.Exp, scale=float(D0) ** -0.5)
                        act.activation(prob_hi[:, g % 2, :], bank[4 + g % 2][:, :], ACT.Exp, scale=float(D0) ** -0.5)\
                           .then_inc(exp_done, 1)

                    def hi_o(b, g):
                        act.wait_ge(oturn_done, G * b + g + 1)
                        act.activation(oT[:, 0, 2 * g:2 * g + 2, :].rearrange("p c q -> p (c q)"),
                                       OUTB[:, 0:2 * P], ACT.Copy).then_inc(oturn_hi, 1)

                    def step(b, par, last=False):
                        a, ap = b + 1, 1 - par
                        exps(b, 0)
                        if not last:
                            hi_turned(a, ap)
                        exps(b, 1)
                        if not last:
                            hi_t(a, ap, 0)
                            hi_t(a, ap, 1)
                        exps(b, 2)
                        hi_o(b, 0)
                        if not last:
                            hi_t(a, ap, 2)
                        exps(b, 3)
                        hi_o(b, 1)
                        if not last:
                            hi_t(a, ap, 3)
                        hi_o(b, 2)
                        if not last:
                            hi_v(a, ap, 0)
                            hi_v(a, ap, 1)
                        hi_o(b, 3)
                        if not last:
                            hi_peak(a, ap)

                    act.wait_ge(blanks_ready, 3)
                    hi_turned(0, 0)
                    for g in range(G):
                        hi_t(0, 0, g)
                    hi_v(0, 0, 0)
                    hi_v(0, 0, 1)
                    hi_peak(0, 0)
                    step(0, 0)
                    with act.Fori(0, PAIRS) as i:
                        step(2 * i + 1, 1)
                        step(2 * i + 2, 0)
                    step(B - 1, 1, last=True)

                @block.vector
                def _(dve):
                    def normalize(a):
                        ahead(dve, turn_done, 2 * a - 1)
                        dve.tensor_scalar(xn[:, :], xs[:, bass.ds(a, 1), :].rearrange("p a d -> p (a d)"),
                                          mean[:, bass.ds(a, 1)],
                                          rstd[:, bass.ds(a, 1)], ALU.subtract, ALU.mult).then_inc(xn_ready, 1)

                    def lo_turned(a, par):
                        dve.wait_ge(turn_hi, 2 * a + 1)
                        dve.tensor_tensor(xcT[:, par, 1, :], TURN[:, 0:2 * P], xcT[:, par, 0, :], ALU.subtract)\
                           .then_inc(turn_lo, 1)

                    def lo_peak(a, par):
                        dve.wait_ge(turn_hi, 2 * a + 2)
                        dve.tensor_tensor(peakT[32:32 + H, par, :], TURN[0:H, 0:P], peakT[0:H, par, :], ALU.subtract)\
                           .then_inc(turn_lo, 1)

                    def lo_t(a, par, g):
                        dve.wait_ge(proj_hi, 6 * a + g + 1)
                        hs = slice(HG * g, HG * g + HG)
                        dve.tensor_tensor(t_s[:, par, 1, hs, :].rearrange("p h q -> p (h q)"), bank[1 + g % 2][:, :],
                                          t_s[:, par, 0, hs, :].rearrange("p h q -> p (h q)"), ALU.subtract)\
                           .then_inc(proj_lo, 1)

                    def lo_v(a, par, j):
                        dve.wait_ge(proj_hi, 6 * a + G + j + 1)
                        hs = slice(8 * j, 8 * j + 8)
                        dve.tensor_tensor(v_s[:, par, 1, hs, 0:D0], bank[1 + j][:, :].rearrange("p (h d) -> p h d", d=D0),
                                          v_s[:, par, 0, hs, 0:D0], ALU.subtract).then_inc(proj_lo, 1)

                    def maxima(a, g):
                        dve.wait_ge(rough_done, G * a + g + 1)
                        dve.tensor_reduce(peak[:, HG * g:HG * g + HG], ROUGH[:, :].rearrange("p (h k) -> p h k", k=P),
                                          AX.X, ALU.max).then_inc(peak_done, 1)

                    def norm(b, g):
                        n = G * b + g
                        dve.wait_ge(pv_done, n + 1)
                        o = PVB[:, 0:HG * (D0 + 1)].rearrange("p (h d) -> p h d", d=D0 + 1)
                        dve.reciprocal(inv[:, g % 2, :], o[:, :, D0]).then_inc(inv_done, 1)
                        dve.wait_ge(inv_done, n + 1)
                        ahead(dve, oturn_done, n - 1)
                        dve.tensor_tensor(o_s[:, g % 2, :, :], o[:, :, 0:D0],
                                          inv[:, g % 2, :].unsqueeze(2).broadcast_to([P, HG, D0]), ALU.mult)\
                           .then_inc(norm_done, 1)

                    def lo_o(b, g):
                        dve.wait_ge(oturn_hi, G * b + g + 1)
                        cs = slice(2 * g, 2 * g + 2)
                        dve.tensor_tensor(oT[:, 1, cs, :].rearrange("p c q -> p (c q)"), OUTB[:, 0:2 * P],
                                          oT[:, 0, cs, :].rearrange("p c q -> p (c q)"), ALU.subtract).then_inc(oturn_lo, 1)

                    def residual(b):
                        dve.wait_ge(out_done, b + 1)
                        here = xs[:, bass.ds(b, 1), :].rearrange("p a d -> p (a d)")
                        dve.tensor_tensor(here, OUTB[:, 0:P], here, ALU.add).then_inc(res_done, 1)
                        dve.wait_ge(res_done, b + 1)
                        dve.bn_stats(stat[:, bass.ds(b, 1), :], xs[:, bass.ds(b, 1), :]).then_inc(stat_done, 1)

                    def step(b, par, first=False, last=False):
                        a, ap = b + 1, 1 - par
                        if not last:
                            normalize(a)
                        if not first:
                            residual(b - 1)
                        if not last:
                            lo_turned(a, ap)
                            lo_t(a, ap, 0)
                        norm(b, 0)
                        if not last:
                            lo_t(a, ap, 1)
                            maxima(a, 0)
                        lo_o(b, 0)
                        norm(b, 1)
                        if not last:
                            lo_t(a, ap, 2)
                            maxima(a, 1)
                        lo_o(b, 1)
                        norm(b, 2)
                        if not last:
                            lo_t(a, ap, 3)
                            maxima(a, 2)
                        lo_o(b, 2)
                        if not last:
                            lo_v(a, ap, 0)
                        norm(b, 3)
                        if not last:
                            maxima(a, 3)
                            lo_v(a, ap, 1)
                        lo_o(b, 3)
                        if not last:
                            lo_peak(a, ap)

                    dve.wait_ge(ln_ready[0], 1)
                    dve.wait_ge(blanks_ready, 3)
                    normalize(0)
                    lo_turned(0, 0)
                    for g in range(G):
                        lo_t(0, 0, g)
                    lo_v(0, 0, 0)
                    lo_v(0, 0, 1)
                    for g in range(G):
                        maxima(0, g)
                    lo_peak(0, 0)
                    step(0, 0, first=True)
                    with dve.Fori(0, PAIRS) as i:
                        step(2 * i + 1, 1)
                        step(2 * i + 2, 0)
                    step(B - 1, 1, last=True)
                    residual(B - 1)

                @block.tensor
                def _(pe):
                    def turn(a, par, ctx_count):
                        pe.wait_ge(xn_ready, a + 1)
                        pe.wait_ge(ctx_loaded[par], ctx_count)
                        ahead(pe, turn_lo, 2 * a)
                        pe.transpose(TURN[:, 0:P], xn[:, :], ident[:, :])
                        pe.transpose(TURN[:, P:2 * P], ctx_in[:, par, :], ident[:, :]).then_inc(turn_done, 1)

                    def project_t(a, par, g):
                        ahead(pe, proj_lo, 6 * a + g - 1)
                        if g == 0:
                            pe.wait_ge(turn_lo, 2 * a + 1)
                        for i in range(HG):
                            last = product(pe, bank[1 + g % 2][:, i * P:(i + 1) * P],
                                           [qk0[:, s, HG * g + i, :] for s in range(2)],
                                           [xcT[:, par, s, 0:P] for s in range(2)])
                        last.then_inc(proj_done, 1)

                    def project_v(a, par, j):
                        pe.wait_ge(proj_lo, 6 * a + G + j - 1)
                        product(pe, bank[1 + j][:, :], [xcT[:, par, s, P:2 * P] for s in range(2)],
                                [v0[:, s, 512 * j:512 * j + 512] for s in range(2)]).then_inc(proj_done, 1)

                    def rough(a, par, g):
                        pe.wait_ge(proj_hi, 6 * a + g + 1)
                        ahead(pe, peak_done, G * a + g)
                        for i in range(HG):
                            last = pe.matmul(ROUGH[:, i * P:(i + 1) * P], t_s[:, par, 0, HG * g + i, :],
                                             xcT[:, par, 0, P:2 * P], start=True, stop=True)
                        last.then_inc(rough_done, 1)

                    def turn_peak(a, par):
                        pe.wait_ge(peak_done, G * a + G)
                        pe.wait_ge(turn_lo, 2 * a + 1)
                        pe.transpose(TURN[0:H, 0:P], peak[:, :], ident[:, :]).then_inc(turn_done, 1)

                    def scores(b, par, g):
                        n = G * b + g
                        to = bank[4 + g % 2]
                        pe.wait_ge(proj_lo, 6 * b + g + 1)
                        ahead(pe, exp_done, n - 1)
                        product(pe, to[:, :], [xcT[:, par, s, P:2 * P] for s in range(2)],
                                [t_s[:, par, s, HG * g:HG * g + HG, :].rearrange("p h q -> p (h q)") for s in range(2)],
                                stop=False)
                        pe.wait_ge(turn_lo, 2 * b + 2)
                        for i in range(HG):
                            last = pe.matmul(to[:, i * P:(i + 1) * P], minus_one_at[:, HG * g + i, :],
                                             peakT[:, par, :], start=False, stop=(i == HG - 1))
                        last.then_inc(score_done, 1)

                    def times_v(b, par, g):
                        n = G * b + g
                        pe.wait_ge(exp_done, n + 1)
                        pe.wait_ge(problo_done, n + 1)
                        pe.wait_ge(proj_lo, 6 * b + 6)
                        ahead(pe, norm_done, n)
                        for i in range(HG):
                            last = product(pe, PVB[:, i * (D0 + 1):(i + 1) * (D0 + 1)],
                                           [p[:, g % 2, i * P:(i + 1) * P] for p in (prob_hi, prob_lo)],
                                           [v_s[:, par, s, HG * g + i, :] for s in range(2)])
                        last.then_inc(pv_done, 1)

                    def turn_o(b, g):
                        n = G * b + g
                        pe.wait_ge(norm_done, n + 1)
                        ahead(pe, oturn_lo, n)
                        if g == 0:
                            ahead(pe, res_done, b)
                        o = o_s[:, g % 2, :, :].rearrange("p h d -> p (h d)")
                        pe.transpose(OUTB[:, 0:P], o[:, 0:P], ident[:, :])
                        pe.transpose(OUTB[:, P:2 * P], o[:, P:2 * P], ident[:, :]).then_inc(oturn_done, 1)

                    def output(b):
                        pe.wait_ge(oturn_lo, G * b + G)
                        for c in range(2 * G):
                            last = product(pe, OUTB[:, 0:P], [oT[:, s, c, :] for s in range(2)],
                                           [o0[:, s, c, :] for s in range(2)], start=(c == 0), stop=(c == 2 * G - 1))
                        last.then_inc(out_done, 1)

                    def step(b, par, ctx_count=0, first=False, last=False):
                        a, ap = b + 1, 1 - par
                        scores(b, par, 0)
                        if not first:
                            output(b - 1)
                        if not last:
                            turn(a, ap, ctx_count)
                        scores(b, par, 1)
                        if not last:
                            project_t(a, ap, 0)
                        times_v(b, par, 0)
                        if not last:
                            project_t(a, ap, 1)
                            rough(a, ap, 0)
                        scores(b, par, 2)
                        turn_o(b, 0)
                        times_v(b, par, 1)
                        if not last:
                            project_t(a, ap, 2)
                            rough(a, ap, 1)
                        scores(b, par, 3)
                        turn_o(b, 1)
                        times_v(b, par, 2)
                        if not last:
                            project_t(a, ap, 3)
                            rough(a, ap, 2)
                        turn_o(b, 2)
                        if not last:
                            project_v(a, ap, 0)
                        times_v(b, par, 3)
                        if not last:
                            rough(a, ap, 3)
                            project_v(a, ap, 1)
                        turn_o(b, 3)
                        if not last:
                            turn_peak(a, ap)

                    pe.wait_ge(blanks_ready, 3)
                    turn(0, 0, 16)
                    for g in range(G):
                        project_t(0, 0, g)
                    project_v(0, 0, 0)
                    project_v(0, 0, 1)
                    for g in range(G):
                        rough(0, 0, g)
                    turn_peak(0, 0)
                    step(0, 0, 16, first=True)
                    with pe.Fori(0, PAIRS) as i:
                        step(2 * i + 1, 1, 16 * i + 32)
                        step(2 * i + 2, 0, 16 * i + 32)
                    step(B - 1, 1, last=True)
                    output(B - 1)


        if stages >= 2:
            with ExitStack() as ffn:
                def f_sb(name, shape, dt=F32):
                    return sb(name, shape, dt, ffn)

                f_xn = f_sb("f_xn", [P, P])
                xT = f_sb("xT", [P, 2, 2, P + 1], F16)
                tanh_r = f_sb("tanh_r", [P, 2, P])
                relu_k = f_sb("relu_k", [P, 2, P])
                k_sq = f_sb("k_sq", [P, P])
                k_s = f_sb("k_s", [P, 2, 2, P], F16)
                gated = f_sb("gated", [P, P])

                f_blank = sem("f_blank")
                f_xn_ready = sem("f_xn_ready")
                f_turn = sem("f_turn")
                f_turn_hi = sem("f_turn_hi")
                f_turn_lo = sem("f_turn_lo")
                f_rk = sem("f_rk")
                f_act = sem("f_act")
                f_sq = sem("f_sq")
                f_k_hi = sem("f_k_hi")
                f_k_lo = sem("f_k_lo")
                f_v = sem("f_v")
                f_gated = sem("f_gated")
                f_res = sem("f_res")
                f_stat = sem("f_stat")
                F_PAIRS = (B - 2) // 2

                with nc.Block() as block:
                    @block.gpsimd
                    def _(pool):
                        layer_norm_scale(pool, 1)
                        pool.memset(xT[:, :, :, 0:1], 0.0).then_inc(f_blank, 1)

                    @block.scalar
                    def _(act):
                        def hi_turned(a, par):
                            act.wait_ge(f_turn, a + 1)
                            act.activation(xT[:, par, 0, 1:P + 1], bank[par][:, 0:P], ACT.Copy).then_inc(f_turn_hi, 1)

                        def gates(b, par):
                            act.wait_ge(f_rk, b + 1)
                            ahead(act, f_res, b - 1)
                            act.activation(tanh_r[:, par, :], bank[2 + par][:, 0:P], ACT.Tanh, scale=0.5)
                            act.activation(relu_k[:, par, :], bank[2 + par][:, P:2 * P], ACT.Relu).then_inc(f_act, 1)

                        def hi_k(b, par):
                            act.wait_ge(f_sq, b + 1)
                            act.activation(k_s[:, par, 0, :], k_sq[:, :], ACT.Copy).then_inc(f_k_hi, 1)

                        def step(b, par, last=False):
                            gates(b, par)
                            if not last:
                                hi_turned(b + 1, 1 - par)
                            hi_k(b, par)

                        hi_turned(0, 0)
                        step(0, 0)
                        with act.Fori(0, F_PAIRS) as i:
                            step(2 * i + 1, 1)
                            step(2 * i + 2, 0)
                        step(B - 1, 1, last=True)

                    @block.vector
                    def _(dve):
                        def normalize(a):
                            ahead(dve, f_turn, a)
                            dve.tensor_scalar(f_xn[:, :], xs[:, bass.ds(a, 1), :].rearrange("p a d -> p (a d)"),
                                              mean[:, bass.ds(a, 1)],
                                              rstd[:, bass.ds(a, 1)], ALU.subtract, ALU.mult).then_inc(f_xn_ready, 1)

                        def lo_turned(a, par):
                            dve.wait_ge(f_turn_hi, a + 1)
                            dve.tensor_tensor(xT[:, par, 1, 1:P + 1], bank[par][:, 0:P], xT[:, par, 0, 1:P + 1],
                                              ALU.subtract).then_inc(f_turn_lo, 1)

                        def square(b, par):
                            dve.wait_ge(f_act, b + 1)
                            ahead(dve, f_k_lo, b)
                            dve.tensor_tensor(k_sq[:, :], relu_k[:, par, :], relu_k[:, par, :], ALU.mult).then_inc(f_sq, 1)

                        def lo_k(b, par):
                            dve.wait_ge(f_k_hi, b + 1)
                            dve.tensor_tensor(k_s[:, par, 1, :], k_sq[:, :], k_s[:, par, 0, :], ALU.subtract).then_inc(f_k_lo, 1)

                        def residual(b, par):
                            dve.wait_ge(f_v, b + 1)
                            here = xs[:, bass.ds(b, 1), :].rearrange("p a d -> p (a d)")
                            dve.scalar_tensor_tensor(out=gated[:, :], in0=tanh_r[:, par, :], scalar=1.0,
                                                     in1=bank[4 + par][:, 0:P], op0=ALU.add, op1=ALU.mult).then_inc(f_gated, 1)
                            dve.wait_ge(f_gated, b + 1)
                            dve.tensor_tensor(here, gated[:, :], here, ALU.add).then_inc(f_res, 1)
                            dve.wait_ge(f_res, b + 1)
                            dve.bn_stats(stat[:, bass.ds(b, 1), :], xs[:, bass.ds(b, 1), :]).then_inc(f_stat, 1)

                        def step(b, par, first=False, last=False):
                            if not last:
                                normalize(b + 1)
                            square(b, par)
                            if not last:
                                lo_turned(b + 1, 1 - par)
                            if not first:
                                residual(b - 1, 1 - par)
                            lo_k(b, par)

                        layer_norm_moments(dve, 1)
                        dve.wait_ge(ln_ready[1], 1)
                        dve.wait_ge(f_blank, 1)
                        normalize(0)
                        lo_turned(0, 0)
                        step(0, 0, first=True)
                        with dve.Fori(0, F_PAIRS) as i:
                            step(2 * i + 1, 1)
                            step(2 * i + 2, 0)
                        step(B - 1, 1, last=True)
                        residual(B - 1, 1)

                    @block.tensor
                    def _(pe):
                        def turn(a, par):
                            pe.wait_ge(f_xn_ready, a + 1)
                            ahead(pe, f_turn_lo, a - 1)
                            pe.transpose(bank[par][:, 0:P], f_xn[:, :], ident[:, :]).then_inc(f_turn, 1)

                        def r_and_k(b, par):
                            pe.wait_ge(f_turn_lo, b + 1)
                            ahead(pe, f_act, b - 1)
                            to = bank[2 + par]
                            now = [xT[:, par, s, 1:P + 1] for s in range(2)]
                            before = [xT[:, par, s, 0:P] for s in range(2)]
                            wr, wr_prev, wk, wk_prev = ([mix[:, s, n, :] for s in range(2)] for n in range(4))
                            product(pe, to[:, 0:P], now, wr, stop=False)
                            product(pe, to[:, 0:P], before, wr_prev, start=False)
                            product(pe, to[:, P:2 * P], wk, now, stop=False)
                            product(pe, to[:, P:2 * P], wk_prev, before, start=False).then_inc(f_rk, 1)

                        def times_v(b, par):
                            pe.wait_ge(f_k_lo, b + 1)
                            product(pe, bank[4 + par][:, 0:P], [k_s[:, par, s, :] for s in range(2)],
                                    [mix[:, s, 4, :] for s in range(2)]).then_inc(f_v, 1)

                        def step(b, par, first=False, last=False):
                            r_and_k(b, par)
                            if not last:
                                turn(b + 1, 1 - par)
                            if not first:
                                times_v(b - 1, 1 - par)

                        turn(0, 0)
                        step(0, 0, first=True)
                        with pe.Fori(0, F_PAIRS) as i:
                            step(2 * i + 1, 1)
                            step(2 * i + 2, 0)
                        step(B - 1, 1, last=True)
                        times_v(B - 1, 1)

        if stages >= 3:
            with ExitStack() as att:
                def b_sb(name, shape, dt=F32):
                    return sb(name, shape, dt, att)

                yn = b_sb("yn", [P, P])
                ctx1 = b_sb("ctx1", [P, 2, P])
                ycT = b_sb("ycT", [P, 2, 2 * P], F16)
                qk32 = b_sb("qk32", [P, 2, P])
                qk16 = b_sb("qk16", [P, 2, 2, P], F16)
                q_s = b_sb("q_s", [P, 2, 2, HG, P], F16)
                k_z = b_sb("k_z", [P, 2, G, 2, P], F16)
                v1 = b_sb("v1", [P, 2, 2, H, D1 + 1], F16)
                hide = b_sb("hide", [P, 2, P], BF16)
                peak1 = b_sb("peak1", [P, H])
                peak1c = b_sb("peak1c", [P, H])
                peak1T = b_sb("peak1T", [P, 2, P], BF16)
                pr = b_sb("pr", [P, 2, HG * P])
                pr_hi = b_sb("pr_hi", [P, 2, HG * P], F16)
                pr_lo = b_sb("pr_lo", [P, 2, HG * P], F16)
                inv1 = b_sb("inv1", [P, H])
                o1 = b_sb("o1", [P, H, D1])
                o1T = b_sb("o1T", [P, 2, P], F16)

                c_loaded = [sem(f"c_loaded{i}") for i in range(2)]
                c_blank = sem("c_blank")
                c_xn = sem("c_xn")
                c_turn = sem("c_turn")
                c_turn_hi = sem("c_turn_hi")
                c_turn_lo = sem("c_turn_lo")
                c_qkv = sem("c_qkv")
                c_biased = sem("c_biased")
                c_v_hi = sem("c_v_hi")
                c_v_lo = sem("c_v_lo")
                c_qk_hi = sem("c_qk_hi")
                c_qk_lo = sem("c_qk_lo")
                c_slots = sem("c_slots")
                c_hide = sem("c_hide")
                c_rough = sem("c_rough")
                c_peak = sem("c_peak")
                c_clip = sem("c_clip")
                c_score = sem("c_score")
                c_exp = sem("c_exp")
                c_lo = sem("c_lo")
                c_pv = sem("c_pv")
                c_inv = sem("c_inv")
                c_norm = sem("c_norm")
                c_oturn = sem("c_oturn")
                c_o_hi = sem("c_o_hi")
                c_o_lo = sem("c_o_lo")
                c_out = sem("c_out")
                c_res = sem("c_res")
                c_stat = sem("c_stat")
                TURN1, QKV, ROUGH1, PV1, OUT1 = bank[0], bank[1], bank[2:4], bank[6], bank[7]
                C_PAIRS = (B - 2) // 2
                W = D1 + 1

                with nc.Block() as block:
                    @block.sync
                    def _(sp):
                        def load(c, par):
                            ahead(sp, c_turn, 2 * c - 3)
                            sp.dma_start(ctx1[:, par:par + 1, :],
                                         ctx[bass.ds(c, 1), :, :].rearrange("a s d -> s a d")).then_inc(c_loaded[par], 16)
                        load(0, 0)
                        load(1, 1)
                        with sp.Fori(0, C_PAIRS) as i:
                            load(2 * i + 2, 0)
                            load(2 * i + 3, 1)

                    @block.gpsimd
                    def _(pool):
                        layer_norm_scale(pool, 2)
                        pool.memset(peak1T[:, :, :], 0.0).then_inc(c_blank, 1)
                        pool.memset(k_z[:, :, :, :, :], 0.0).then_inc(c_blank, 1)
                        pool.memset(v1[:, :, 0, :, D1:W], 1.0).then_inc(c_blank, 1)
                        pool.memset(v1[:, :, 1, :, D1:W], 0.0).then_inc(c_blank, 1)

                        def group(n, par):
                            pool.wait_ge(c_exp, n + 1)
                            ahead(pool, c_pv, n - 1)
                            pool.tensor_tensor(pr_lo[:, par, :], pr[:, par, :], pr_hi[:, par, :],
                                               ALU.subtract).then_inc(c_lo, 1)
                        for n in range(G):
                            group(n, n % 2)
                        with pool.Fori(1, B) as b:
                            for g in range(G):
                                group(G * b + g, g % 2)

                    @block.scalar
                    def _(act):
                        def hi_turned(a):
                            act.wait_ge(c_turn, 2 * a + 1)
                            act.activation(ycT[:, 0, :], TURN1[:, 0:2 * P], ACT.Copy).then_inc(c_turn_hi, 1)

                        def hi_peak(a, par):
                            act.wait_ge(c_turn, 2 * a + 2)
                            act.activation(peak1T[0:H, par, :], TURN1[0:H, 0:P], ACT.Copy).then_inc(c_turn_hi, 1)

                        def biased(a, par):
                            act.wait_ge(c_qkv, a + 1)
                            ahead(act, c_qk_lo, a)
                            act.activation(qk32[:, 0, :], QKV[:, 0:P], ACT.Identity, bias=bq_col)
                            act.activation(qk32[:, 1, :], QKV[:, P:2 * P], ACT.Identity, bias=bk_col).then_inc(c_biased, 1)
                            act.activation(v1[:, par, 0, :, 0:D1], QKV[:, 2 * P:3 * P].rearrange("p (h d) -> p h d", d=D1),
                                           ACT.Copy).then_inc(c_v_hi, 1)

                        def exps(b, g):
                            n = G * b + g
                            act.wait_ge(c_score, n + 1)
                            ahead(act, c_lo, n - 1)
                            ahead(act, c_pv, n - 1)
                            act.activation(pr[:, g % 2, :], bank[4 + g % 2][:, :], ACT.Exp, scale=float(D1) ** -0.5)
                            act.activation(pr_hi[:, g % 2, :], bank[4 + g % 2][:, :], ACT.Exp, scale=float(D1) ** -0.5)\
                               .then_inc(c_exp, 1)

                        def hi_o(b):
                            act.wait_ge(c_oturn, b + 1)
                            act.activation(o1T[:, 0, :], OUT1[:, 0:P], ACT.Copy).then_inc(c_o_hi, 1)

                        def step(b, par, first=False, last=False):
                            a, ap = b + 1, 1 - par
                            exps(b, 0)
                            if not last:
                                hi_turned(a)
                            if not first:
                                hi_o(b - 1)
                            exps(b, 1)
                            if not last:
                                biased(a, ap)
                            exps(b, 2)
                            exps(b, 3)
                            if not last:
                                hi_peak(a, ap)

                        act.wait_ge(c_blank, 4)
                        hi_turned(0)
                        biased(0, 0)
                        hi_peak(0, 0)
                        step(0, 0, first=True)
                        with act.Fori(0, C_PAIRS) as i:
                            step(2 * i + 1, 1)
                            step(2 * i + 2, 0)
                        step(B - 1, 1, last=True)
                        hi_o(B - 1)

                    @block.vector
                    def _(dve):
                        def normalize(a, par):
                            ahead(dve, c_turn, 2 * a - 1)
                            dve.tensor_scalar(yn[:, :], xs[:, bass.ds(a, 1), :].rearrange("p a d -> p (a d)"),
                                              mean[:, bass.ds(a, 1)],
                                              rstd[:, bass.ds(a, 1)], ALU.subtract, ALU.mult).then_inc(c_xn, 1)
                            ahead(dve, c_score, G * (a - 1))
                            dve.tensor_scalar(hide[:, par, :], masks[:, bass.ds(a, 1), :].rearrange("p a k -> p (a k)"),
                                              0, -BIG, ALU.is_equal, ALU.mult).then_inc(c_hide, 1)

                        def lo_turned(a):
                            dve.wait_ge(c_turn_hi, 2 * a + 1)
                            dve.tensor_tensor(ycT[:, 1, :], TURN1[:, 0:2 * P], ycT[:, 0, :], ALU.subtract).then_inc(c_turn_lo, 1)

                        def lo_peak(a, par):
                            dve.wait_ge(c_turn_hi, 2 * a + 2)
                            dve.tensor_tensor(peak1T[32:32 + H, par, :], TURN1[0:H, 0:P], peak1T[0:H, par, :],
                                              ALU.subtract).then_inc(c_turn_lo, 1)

                        def slots(a, par):
                            dve.wait_ge(c_biased, a + 1)
                            ahead(dve, c_slots, a)
                            dve.tensor_copy(qk16[:, :, 0, :], qk32[:, :, :]).then_inc(c_qk_hi, 1)
                            dve.wait_ge(c_v_hi, a + 1)
                            dve.tensor_tensor(v1[:, par, 1, :, 0:D1], QKV[:, 2 * P:3 * P].rearrange("p (h d) -> p h d", d=D1),
                                              v1[:, par, 0, :, 0:D1], ALU.subtract).then_inc(c_v_lo, 1)
                            dve.wait_ge(c_qk_hi, a + 1)
                            dve.tensor_tensor(qk16[:, :, 1, :], qk32[:, :, :], qk16[:, :, 0, :], ALU.subtract).then_inc(c_qk_lo, 1)
                            dve.wait_ge(c_qk_lo, a + 1)
                            for i in range(HG):
                                dve.tensor_scalar(q_s[:, par, :, i, :], qk16[:, 0, :, :], slot_of[:, i:i + 1], None, ALU.mult)
                            for j in range(G):
                                rows = slice(32 * j, 32 * j + 32)
                                last = dve.tensor_copy(k_z[rows, par, j, :, :], qk16[rows, 1, :, :])
                            last.then_inc(c_slots, 1)

                        def maxima(a, g):
                            dve.wait_ge(c_rough, G * a + g + 1)
                            dve.tensor_reduce(peak1[:, HG * g:HG * g + HG],
                                              ROUGH1[g % 2][:, :].rearrange("p (h k) -> p h k", k=P),
                                              AX.X, ALU.max).then_inc(c_peak, 1)

                        def clip(a):
                            dve.wait_ge(c_peak, G * a + G)
                            dve.tensor_scalar(peak1c[:, :], peak1[:, :], -BIG / 16, None, ALU.max).then_inc(c_clip, 1)

                        def norm(b):
                            dve.wait_ge(c_pv, G * b + G)
                            o = PV1[:, 0:H * W].rearrange("p (h d) -> p h d", d=W)
                            dve.reciprocal(inv1[:, :], o[:, :, D1]).then_inc(c_inv, 1)
                            dve.wait_ge(c_inv, b + 1)
                            ahead(dve, c_oturn, b)
                            dve.tensor_tensor(o1[:, :, :], o[:, :, 0:D1],
                                              inv1[:, :].unsqueeze(2).broadcast_to([P, H, D1]), ALU.mult).then_inc(c_norm, 1)

                        def lo_o(b):
                            dve.wait_ge(c_o_hi, b + 1)
                            dve.tensor_tensor(o1T[:, 1, :], OUT1[:, 0:P], o1T[:, 0, :], ALU.subtract).then_inc(c_o_lo, 1)

                        def residual(b):
                            dve.wait_ge(c_out, b + 1)
                            here = xs[:, bass.ds(b, 1), :].rearrange("p a d -> p (a d)")
                            dve.tensor_tensor(here, OUT1[:, 0:P], here, ALU.add).then_inc(c_res, 1)
                            dve.wait_ge(c_res, b + 1)
                            dve.bn_stats(stat[:, bass.ds(b, 1), :], xs[:, bass.ds(b, 1), :]).then_inc(c_stat, 1)

                        def step(b, par, first=False, last=False):
                            a, ap = b + 1, 1 - par
                            if not last:
                                normalize(a, ap)
                                lo_turned(a)
                            if not first:
                                lo_o(b - 1)
                            if not last:
                                slots(a, ap)
                            if not first:
                                residual(b - 1)
                            if not last:
                                for g in range(G):
                                    maxima(a, g)
                                clip(a)
                                lo_peak(a, ap)
                            norm(b)

                        layer_norm_moments(dve, 2)
                        dve.wait_ge(ln_ready[2], 1)
                        dve.wait_ge(c_blank, 4)
                        dve.wait_ge(masks_loaded, 16)
                        normalize(0, 0)
                        lo_turned(0)
                        slots(0, 0)
                        for g in range(G):
                            maxima(0, g)
                        clip(0)
                        lo_peak(0, 0)
                        step(0, 0, first=True)
                        with dve.Fori(0, C_PAIRS) as i:
                            step(2 * i + 1, 1)
                            step(2 * i + 2, 0)
                        step(B - 1, 1, last=True)
                        lo_o(B - 1)
                        residual(B - 1)

                    @block.tensor
                    def _(pe):
                        def turn(a, par, ctx_count):
                            pe.wait_ge(c_xn, a + 1)
                            pe.wait_ge(c_loaded[par], ctx_count)
                            ahead(pe, c_turn_lo, 2 * a)
                            pe.transpose(TURN1[:, 0:P], yn[:, :], ident[:, :])
                            pe.transpose(TURN1[:, P:2 * P], ctx1[:, par, :], ident[:, :]).then_inc(c_turn, 1)

                        def project(a):
                            pe.wait_ge(c_turn_lo, 2 * a + 1)
                            ahead(pe, c_v_lo, a)
                            xT_, cT_ = ([ycT[:, s, w * P:(w + 1) * P] for s in range(2)] for w in range(2))
                            wq, wk, wv = ([att1[:, s, n, :] for s in range(2)] for n in range(3))
                            product(pe, QKV[:, 0:P], wq, xT_)
                            product(pe, QKV[:, P:2 * P], wk, cT_)
                            product(pe, QKV[:, 2 * P:3 * P], cT_, wv).then_inc(c_qkv, 1)

                        def rough(a, par, g):
                            pe.wait_ge(c_slots, a + 1)
                            pe.wait_ge(c_hide, a + 1)
                            ahead(pe, c_peak, G * a + g - 1)
                            to = ROUGH1[g % 2]
                            pe.matmul(to[:, :].rearrange("p (h k) -> p h k", k=P), ident4[:, 0, :],
                                      hide[:, par, :].unsqueeze(1).broadcast_to([P, HG, P]), start=True, stop=False)
                            for i in range(HG):
                                last = pe.matmul(to[:, i * P:(i + 1) * P], q_s[:, par, 0, i, :], k_z[:, par, g, 0, :],
                                                 start=False, stop=(i == HG - 1))
                            last.then_inc(c_rough, 1)

                        def turn_peak(a):
                            pe.wait_ge(c_clip, a + 1)
                            pe.transpose(TURN1[0:H, 0:P], peak1c[:, :], ident[:, :]).then_inc(c_turn, 1)

                        def scores(b, par, g):
                            n = G * b + g
                            to = bank[4 + g % 2]
                            ahead(pe, c_exp, n - 1)
                            product(pe, to[:, :], [k_z[:, par, g, s, :] for s in range(2)],
                                    [q_s[:, par, s, :, :].rearrange("p i q -> p (i q)") for s in range(2)], stop=False)
                            pe.matmul(to[:, :], hide[:, par, :], ident4[:, :, :].rearrange("p i q -> p (i q)"),
                                      start=False, stop=False)
                            pe.wait_ge(c_turn_lo, 2 * b + 2)
                            for i in range(HG):
                                last = pe.matmul(to[:, i * P:(i + 1) * P], minus_one_at[:, HG * g + i, :],
                                                 peak1T[:, par, :], start=False, stop=(i == HG - 1))
                            last.then_inc(c_score, 1)

                        def times_v(b, par, g):
                            n = G * b + g
                            pe.wait_ge(c_exp, n + 1)
                            pe.wait_ge(c_lo, n + 1)
                            if g == 0:
                                ahead(pe, c_norm, b)
                            for i in range(HG):
                                h = HG * g + i
                                last = product(pe, PV1[:, h * W:(h + 1) * W],
                                               [p[:, g % 2, i * P:(i + 1) * P] for p in (pr_hi, pr_lo)],
                                               [v1[:, par, s, h, :] for s in range(2)])
                            last.then_inc(c_pv, 1)

                        def turn_o(b):
                            pe.wait_ge(c_norm, b + 1)
                            ahead(pe, c_res, b)
                            pe.transpose(OUT1[:, 0:P], o1[:, :, :].rearrange("p h d -> p (h d)"), ident[:, :]).then_inc(c_oturn, 1)

                        def output(b):
                            pe.wait_ge(c_o_lo, b + 1)
                            product(pe, OUT1[:, 0:P], [o1T[:, s, :] for s in range(2)], [att1[:, s, 3, :] for s in range(2)],
                                    stop=False)
                            pe.matmul(OUT1[:, 0:P], ones16[:, :], bias1[:, 0, :], start=False, stop=False)
                            pe.matmul(OUT1[:, 0:P], ones16[:, :], bias1[:, 1, :], start=False, stop=True).then_inc(c_out, 1)

                        def step(b, par, ctx_count=0, first=False, last=False):
                            a, ap = b + 1, 1 - par
                            if not last:
                                turn(a, ap, ctx_count)
                            scores(b, par, 0)
                            if not first:
                                turn_o(b - 1)
                            if not last:
                                project(a)
                            scores(b, par, 1)
                            if not first:
                                output(b - 1)
                            times_v(b, par, 0)
                            scores(b, par, 2)
                            if not last:
                                rough(a, ap, 0)
                                rough(a, ap, 1)
                            times_v(b, par, 1)
                            scores(b, par, 3)
                            if not last:
                                rough(a, ap, 2)
                            times_v(b, par, 2)
                            if not last:
                                rough(a, ap, 3)
                                turn_peak(a)
                            times_v(b, par, 3)

                        pe.wait_ge(c_blank, 4)
                        turn(0, 0, 16)
                        project(0)
                        for g in range(G):
                            rough(0, 0, g)
                        turn_peak(0)
                        step(0, 0, 16, first=True)
                        with pe.Fori(0, C_PAIRS) as i:
                            step(2 * i + 1, 1, 16 * i + 32)
                            step(2 * i + 2, 0, 16 * i + 32)
                        step(B - 1, 1, last=True)
                        turn_o(B - 1)
                        output(B - 1)


        if stages >= 4:
            with ExitStack() as moe:
                def m_sb(name, shape, dt=F32):
                    return sb(name, shape, dt, moe)

                T = TILES
                SETS = B // T
                zn = m_sb("zn", [P, T, P])
                zT = m_sb("zT", [P, 2, 2, T * P], F16)
                logits = m_sb("logits", [P, T, E])
                top = m_sb("top", [P, T, 8])
                top_at = m_sb("top_at", [P, T, 8], U32)
                two_at = m_sb("two_at", [P, T, 2])
                lead = m_sb("lead", [P, T])
                tanh_lead = m_sb("tanh_lead", [P, T])
                two_gates = m_sb("two_gates", [P, T, 2])
                picked = m_sb("picked", [P, T, 2, E])
                picked_gate = m_sb("picked_gate", [P, T, 2, E])
                gate = m_sb("gate", [P, 2, T, E])
                gateT = m_sb("gateT", [E, T * P])
                silu = m_sb("silu", [P, C, T * P])
                g32 = m_sb("g32", [P, C, T * P])
                g_s = m_sb("g_s", [P, 2, C, 2, T * P], F16)
                acc = m_sb("acc", [P, 2, T, P])

                z_norm = sem("z_norm")
                z_turn = sem("z_turn")
                z_hi = sem("z_hi")
                z_lo = sem("z_lo")
                z_logits = sem("z_logits")
                z_kept = sem("z_kept")
                z_ranked = sem("z_ranked")
                z_top = sem("z_top")
                z_at = sem("z_at")
                z_lead = sem("z_lead")
                z_tanh = sem("z_tanh")
                z_two = sem("z_two")
                z_picked = sem("z_picked")
                z_pgate = sem("z_pgate")
                z_gate = sem("z_gate")
                z_gturn = sem("z_gturn")
                z_gateT = sem("z_gateT")
                z_b2 = sem("z_b2")
                z_start = sem("z_start")
                h1_done = sem("h1_done")
                h3_done = sem("h3_done")
                silu_done = sem("silu_done")
                g_done = sem("g_done")
                g_hi = sem("g_hi")
                g_lo = sem("g_lo")
                y_done = sem("y_done")
                acc_done = sem("acc_done")
                set_stored = [sem(f"set_stored{i}") for i in range(2)]
                H1B, H3B, YB, TURNB, SMALLB = bank[0:2], bank[2:4], bank[4:6], bank[6], bank[7]
                S_PAIRS = (SETS - 2) // 2

                with nc.Block() as block:
                    @block.sync
                    def _(sp):
                        def store(s, par):
                            sp.wait_ge(acc_done, T * E * (s + 1))
                            sp.dma_start(out[bass.ds(T * s, T), :, :].rearrange("b s d -> s b d"), acc[:, par, :, :])\
                              .then_inc(set_stored[par], 16)
                        with sp.Fori(0, SETS // 2) as i:
                            store(2 * i, 0)
                            store(2 * i + 1, 1)
                        for par in range(2):
                            sp.wait_ge(set_stored[par], 16 * (SETS // 2))

                    @block.gpsimd
                    def _(pool):
                        layer_norm_scale(pool, 3)

                        def lo_g(s, e):
                            for c in range(C):
                                v = E * C * s + C * e + c
                                pool.wait_ge(g_hi, v + 1)
                                ahead(pool, y_done, E * s + e - 1)
                                pool.tensor_tensor(g_s[:, e % 2, c, 1, :], g32[:, c, :], g_s[:, e % 2, c, 0, :],
                                                   ALU.subtract).then_inc(g_lo, 1)
                        for e in range(E):
                            lo_g(0, e)
                        with pool.Fori(1, SETS) as s:
                            for e in range(E):
                                lo_g(s, e)

                    @block.scalar
                    def _(act):
                        def hi_turned(a, par):
                            act.wait_ge(z_turn, a + 1)
                            act.activation(zT[:, par, 0, :], TURNB[:, :], ACT.Copy).then_inc(z_hi, 1)

                        def tanh(a):
                            act.wait_ge(z_lead, a + 1)
                            act.activation(tanh_lead[:, :], lead[:, :], ACT.Tanh, scale=0.5).then_inc(z_tanh, 1)

                        def keep_gateT(a):
                            act.wait_ge(z_gturn, a + 1)
                            act.activation(gateT[:, :], SMALLB[0:E, :], ACT.Copy).then_inc(z_gateT, 1)

                        def expert(s, e):
                            for c in range(C):
                                v = E * C * s + C * e + c
                                act.wait_ge(h1_done, v + 1)
                                ahead(act, g_done, v - 1)
                                act.activation(silu[:, c, :], H1B[c][:, :], ACT.Silu,
                                               bias=b1_col[:, C * e + c:C * e + c + 1]).then_inc(silu_done, 1)
                                act.wait_ge(g_done, v + 1)
                                ahead(act, y_done, E * s + e - 1)
                                act.activation(g_s[:, e % 2, c, 0, :], g32[:, c, :], ACT.Copy).then_inc(g_hi, 1)

                        def step(s, par, last=False):
                            for e in range(E):
                                expert(s, e)
                                if not last:
                                    if e == 1:
                                        hi_turned(s + 1, 1 - par)
                                    if e == 4:
                                        tanh(s + 1)
                                    if e == 5:
                                        keep_gateT(s + 1)

                        hi_turned(0, 0)
                        tanh(0)
                        keep_gateT(0)
                        step(0, 0)
                        with act.Fori(0, S_PAIRS) as i:
                            step(2 * i + 1, 1)
                            step(2 * i + 2, 0)
                        step(SETS - 1, 1, last=True)

                    @block.vector
                    def _(dve):
                        def normalize(a):
                            ahead(dve, z_turn, a)
                            for t in range(T):
                                last = dve.tensor_scalar(zn[:, t, :], xs[:, bass.ds(T * a + t, 1), :].rearrange("p a d -> p (a d)"),
                                                         mean[:, bass.ds(T * a + t, 1)],
                                                         rstd[:, bass.ds(T * a + t, 1)], ALU.subtract, ALU.mult)
                            last.then_inc(z_norm, 1)

                        def lo_turned(a, par):
                            dve.wait_ge(z_hi, a + 1)
                            dve.tensor_tensor(zT[:, par, 1, :], TURNB[:, :], zT[:, par, 0, :], ALU.subtract).then_inc(z_lo, 1)

                        def rank(a):
                            dve.wait_ge(z_logits, a + 1)
                            ahead(dve, z_top, a)
                            dve.tensor_copy(logits[:, :, :].rearrange("p t e -> p (t e)"), SMALLB[:, 0:T * E]).then_inc(z_kept, 1)
                            dve.wait_ge(ln_ready[3], 1)
                            dve.wait_ge(z_kept, a + 1)
                            ahead(dve, z_pgate, a)
                            for t in range(T):
                                dve.max(top[:, t, :], logits[:, t, :]).then_inc(z_ranked, 1)
                            dve.wait_ge(z_ranked, T * (a + 1))
                            dve.tensor_tensor(lead[:, :], top[:, :, 0], top[:, :, 1], ALU.subtract).then_inc(z_lead, 1)
                            for t in range(T):
                                last = dve.max_index(top_at[:, t, :], top[:, t, :], logits[:, t, :])
                            last.then_inc(z_top, 1)
                            dve.wait_ge(z_top, a + 1)
                            ahead(dve, z_picked, a)
                            dve.tensor_copy(two_at[:, :, :], top_at[:, :, 0:2]).then_inc(z_at, 1)

                        def route(a, par):
                            dve.wait_ge(z_tanh, a + 1)
                            ahead(dve, z_pgate, a)
                            dve.tensor_scalar(two_gates[:, :, 0], tanh_lead[:, :], half_gain[:, 3:4], half_gain[:, 3:4],
                                              ALU.mult, ALU.add)
                            dve.tensor_scalar(two_gates[:, :, 1], tanh_lead[:, :], minus_half_gain[:, 3:4], half_gain[:, 3:4],
                                              ALU.mult, ALU.add).then_inc(z_two, 1)
                            dve.wait_ge(z_at, a + 1)
                            dve.tensor_tensor(picked[:, :, :, :],
                                              experts[:, :].unsqueeze(1).unsqueeze(1).broadcast_to([P, T, 2, E]),
                                              two_at[:, :, :].unsqueeze(3).broadcast_to([P, T, 2, E]), ALU.is_equal)\
                               .then_inc(z_picked, 1)
                            dve.wait_ge(z_two, a + 1)
                            dve.wait_ge(z_picked, a + 1)
                            ahead(dve, z_gate, a)
                            dve.tensor_tensor(picked_gate[:, :, :, :], picked[:, :, :, :],
                                              two_gates[:, :, :].unsqueeze(3).broadcast_to([P, T, 2, E]), ALU.mult)\
                               .then_inc(z_pgate, 1)
                            dve.wait_ge(z_pgate, a + 1)
                            ahead(dve, acc_done, T * E * (a - 1))
                            dve.tensor_tensor(gate[:, par, :, :], picked_gate[:, :, 0, :], picked_gate[:, :, 1, :], ALU.add)\
                               .then_inc(z_gate, 1)

                        def begin(a, par, stores):
                            dve.wait_ge(z_b2, a + 1)
                            ahead(dve, set_stored[par], stores)
                            dve.tensor_tensor(acc[:, par, :, :].rearrange("p t d -> p (t d)"), SMALLB[:, :],
                                              xs[:, bass.ds(T * a, T), :].rearrange("p t d -> p (t d)"), ALU.add)\
                               .then_inc(z_start, 1)

                        def gated(s, e):
                            for c in range(C):
                                v = E * C * s + C * e + c
                                dve.wait_ge(h3_done, v + 1)
                                dve.wait_ge(silu_done, v + 1)
                                ahead(dve, g_lo, v - 1)
                                dve.scalar_tensor_tensor(out=g32[:, c, :], in0=H3B[c][:, :],
                                                         scalar=b3_col[:, C * e + c:C * e + c + 1], in1=silu[:, c, :],
                                                         op0=ALU.add, op1=ALU.mult).then_inc(g_done, 1)

                        def accumulate(s, par, e):
                            u = E * s + e
                            dve.wait_ge(y_done, u + 1)
                            dve.wait_ge(z_start, s + 1)
                            ahead(dve, acc_done, T * u)
                            for t in range(T):
                                dve.scalar_tensor_tensor(out=acc[:, par, t, :], in0=YB[e % 2][:, t * P:(t + 1) * P],
                                                         scalar=gate[:, par, t, e:e + 1], in1=acc[:, par, t, :],
                                                         op0=ALU.mult, op1=ALU.add).then_inc(acc_done, 1)

                        def step(s, par, stores=0, first=False, last=False):
                            for e in range(E):
                                gated(s, e)
                                if e > 0:
                                    accumulate(s, par, e - 1)
                                elif not first:
                                    accumulate(s - 1, 1 - par, E - 1)
                                if not last:
                                    if e == 0:
                                        normalize(s + 1)
                                    if e == 2:
                                        lo_turned(s + 1, 1 - par)
                                    if e == 4:
                                        rank(s + 1)
                                    if e == 5:
                                        route(s + 1, 1 - par)
                                    if e == 7:
                                        begin(s + 1, 1 - par, stores)

                        layer_norm_moments(dve, 3)
                        dve.wait_ge(ln_ready[3], 1)
                        normalize(0)
                        lo_turned(0, 0)
                        rank(0)
                        route(0, 0)
                        begin(0, 0, 0)
                        step(0, 0, 0, first=True)
                        with dve.Fori(0, S_PAIRS) as i:
                            step(2 * i + 1, 1, 16 * i + 16)
                            step(2 * i + 2, 0, 16 * i + 16)
                        step(SETS - 1, 1, last=True)
                        accumulate(SETS - 1, 1, E - 1)

                    @block.tensor
                    def _(pe):
                        def turn(a):
                            pe.wait_ge(z_norm, a + 1)
                            ahead(pe, z_lo, a)
                            for t in range(T):
                                last = pe.transpose(TURNB[:, t * P:(t + 1) * P], zn[:, t, :], ident[:, :])
                            last.then_inc(z_turn, 1)

                        def score_experts(a, par):
                            pe.wait_ge(z_lo, a + 1)
                            ahead(pe, z_start, a)
                            for t in range(T):
                                last = product(pe, SMALLB[:, t * E:(t + 1) * E],
                                               [zT[:, par, w, t * P:(t + 1) * P] for w in range(2)],
                                               [router[:, w, :] for w in range(2)])
                            last.then_inc(z_logits, 1)

                        def turn_gates(a, par):
                            pe.wait_ge(z_gate, a + 1)
                            for t in range(T):
                                last = pe.transpose(SMALLB[0:E, t * P:(t + 1) * P], gate[:, par, t, :], ident[:, :])
                            last.then_inc(z_gturn, 1)

                        def gates_b2(a):
                            pe.wait_ge(z_gateT, a + 1)
                            for t in range(T):
                                last = pe.matmul(SMALLB[:, t * P:(t + 1) * P], gateT[:, t * P:(t + 1) * P], b2_row[:, :],
                                                 start=True, stop=True)
                            last.then_inc(z_b2, 1)

                        def hidden(s, par, e):
                            for c in range(C):
                                v = E * C * s + C * e + c
                                z = [zT[:, par, w, :] for w in range(2)]
                                if c == 0 and e == 0:
                                    pe.wait_ge(z_lo, s + 1)
                                ahead(pe, silu_done, v - 1)
                                product(pe, H1B[c][:, :], [up1[:, w, C * e + c, :] for w in range(2)], z).then_inc(h1_done, 1)
                                ahead(pe, g_done, v - 1)
                                product(pe, H3B[c][:, :], [up3[:, w, C * e + c, :] for w in range(2)], z).then_inc(h3_done, 1)

                        def down_project(s, e):
                            u = E * s + e
                            pe.wait_ge(g_lo, C * (u + 1))
                            ahead(pe, acc_done, T * (u - 1))
                            for t in range(T):
                                for c in range(C):
                                    last = product(pe, YB[e % 2][:, t * P:(t + 1) * P],
                                                   [g_s[:, e % 2, c, w, t * P:(t + 1) * P] for w in range(2)],
                                                   [down[:, w, C * e + c, :] for w in range(2)],
                                                   start=(c == 0), stop=(c == C - 1))
                            last.then_inc(y_done, 1)

                        def step(s, par, first=False, last=False):
                            for e in range(E):
                                hidden(s, par, e)
                                if e > 0:
                                    down_project(s, e - 1)
                                elif not first:
                                    down_project(s - 1, E - 1)
                                if not last:
                                    if e == 1:
                                        turn(s + 1)
                                    if e == 3:
                                        score_experts(s + 1, 1 - par)
                                    if e == 5:
                                        turn_gates(s + 1, 1 - par)
                                    if e == 6:
                                        gates_b2(s + 1)

                        turn(0)
                        score_experts(0, 0)
                        turn_gates(0, 0)
                        gates_b2(0)
                        step(0, 0, first=True)
                        with pe.Fori(0, S_PAIRS) as i:
                            step(2 * i + 1, 1)
                            step(2 * i + 2, 0)
                        step(SETS - 1, 1, last=True)
                        down_project(SETS - 1, E - 1)


        if stages < 4:
            with nc.Block() as block:
                stored = sem("stored")

                @block.sync
                def _(sp):
                    sp.dma_start(out.rearrange("b s d -> s b d"), xs[:, :, :]).then_inc(stored, 16)
                    sp.wait_ge(stored, 16)


_INS = ["x", "ctx_1024", "mask_BxSxS2_if1", "g_xattn", "g_ffn",
        "L0_xattn_w_q", "L0_xattn_w_k", "L0_xattn_w_v", "L0_xattn_w_o",
        "L0_ffn_W_r", "L0_ffn_W_k", "L0_ffn_W_v", "L0_ffn_mu_r", "L0_ffn_mu_k",
        "L1_xattn_Wq", "L1_xattn_bq", "L1_xattn_Wk", "L1_xattn_bk", "L1_xattn_Wv", "L1_xattn_bv",
        "L1_xattn_Wo", "L1_xattn_bo", "L1_ffn_Wg", "L1_ffn_W1", "L1_ffn_b1", "L1_ffn_A1", "L1_ffn_B1",
        "L1_ffn_W2", "L1_ffn_b2", "L1_ffn_A2", "L1_ffn_B2", "L1_ffn_W3", "L1_ffn_b3", "L1_ffn_A3",
        "L1_ffn_B3"]


def kernel(**inputs):
    import numpy as np
    import concourse.bacc as bacc
    from concourse.bass_utils import run_bass_kernel_spmd

    nc = bacc.Bacc("TRN2", target_bir_lowering=False, num_devices=1)
    arrays, args = {}, []
    for name in _INS:
        a = np.ascontiguousarray(inputs[name])
        arrays[name] = a
        args.append(nc.dram_tensor(name, a.shape, mybir.dt.from_np(a.dtype), kind="ExternalInput").ap())
    args.append(nc.dram_tensor("x_out", arrays["x"].shape, F32, kind="ExternalOutput").ap())
    gated_layers(nc, *args)
    result = run_bass_kernel_spmd(nc, [arrays], core_ids=[0])
    return result.results[0]["x_out"]
```

```python
from contextlib import ExitStack

import concourse.bass as bass
from concourse import mybir

F32 = mybir.dt.float32
F16 = mybir.dt.float16
BF16 = mybir.dt.bfloat16
I32 = mybir.dt.int32
U32 = mybir.dt.uint32
ALU = mybir.AluOpType
ACT = mybir.ActivationFunctionType
AX = mybir.AxisListType

P = 128
EPS = 1e-5
H = 16
D0 = 64
D1 = 8
HG = 4
G = H // HG
E = 8
C = 2
R = 16
TILES = 4
BIG = 1e30


def gated_layers(nc, x, ctx, mask, g_xattn, g_ffn, wq0, wk0, wv0, wo0, w_r, w_k, w_v, mu_r, mu_k,
                 wq1, bq1, wk1, bk1, wv1, bv1, wo1, bo1, wg, w1, b1, a1, bb1, w2, b2, a2, bb2,
                 w3, b3, a3, bb3, out, stages=5):
    B = x.shape[0]
    with ExitStack() as whole:
        def sb(name, shape, dt=F32, to=whole):
            return to.enter_context(nc.sbuf_tensor(name, shape, dt))

        def sem(name):
            return whole.enter_context(nc.semaphore(name))

        bank = [whole.enter_context(nc.psum_tensor(f"bank{i}", [P, 512], F32)) for i in range(8)]

        xs = sb("xs", [P, B, P])
        masks = sb("masks", [P, B, P], I32)
        stat = sb("stat", [P, B, 6])
        mean = sb("mean", [P, B])
        spread = sb("spread", [P, B])
        var = sb("var", [P, B])
        rstd = sb("rstd", [P, B])
        veps = sb("veps", [P, B])
        minus_half = sb("minus_half", [P, B])
        ident = sb("ident", [P, P])
        ident4 = sb("ident4", [P, HG, P], BF16)
        minus_one_at = sb("minus_one_at", [P, H, P], BF16)
        slot_of = sb("slot_of", [P, HG])
        experts = sb("experts", [P, E])
        ones16 = sb("ones16", [1, P], F16)
        gain = sb("gain", [P, 4])
        half_gain = sb("half_gain", [P, 4])
        minus_half_gain = sb("minus_half_gain", [P, 4])
        NCOL = 2 * E * C + 5
        cols = sb("cols", [P, NCOL])
        b1_col, b3_col = cols[:, 0:E * C], cols[:, E * C:2 * E * C]
        bq_col, bk_col, bv_col = (cols[:, 2 * E * C + i:2 * E * C + i + 1] for i in range(3))
        mu = cols[:, NCOL - 2:NCOL]
        b2_row = sb("b2_row", [E, P])
        qk0 = sb("qk0", [P, 2, H, P], F16)
        v0 = sb("v0", [P, 2, H * D0], F16)
        o0 = sb("o0", [P, 2, G * 2, P], F16)
        mix = sb("mix", [P, 2, 5, P], F16)
        att1 = sb("att1", [P, 2, 4, P], F16)
        bias1 = sb("bias1", [1, 2, P], F16)
        router = sb("router", [P, 2, E], F16)
        up1 = sb("up1", [P, 2, E * C, P], F16)
        up3 = sb("up3", [P, 2, E * C, P], F16)
        down = sb("down", [P, 2, E * C, P], F16)

        x_loaded = sem("x_loaded")
        masks_loaded = sem("masks_loaded")
        stats_ready = sem("stats_ready")
        ln_ready = [sem(f"ln_ready{i}") for i in range(4)]

        def product(pe, to, left, right, start=True, stop=True):
            pe.matmul(to, left[0], right[0], start=start, stop=False)
            pe.matmul(to, left[0], right[1], start=False, stop=False)
            return pe.matmul(to, left[1], right[0], start=False, stop=stop)

        def ahead(eng, semaphore, n):
            if not isinstance(n, int) or n > 0:
                eng.wait_ge(semaphore, n)

        moment = sem("moment")
        veps_ready = sem("veps_ready")

        def layer_norm_moments(dve, n):
            before = 5 * n
            even, odd = (stat[:, :, 3 * i + 1] for i in range(2))
            dve.tensor_tensor(mean[:, :], even, odd, ALU.add).then_inc(moment, 1)
            dve.tensor_tensor(spread[:, :], even, odd, ALU.subtract).then_inc(moment, 1)
            dve.tensor_tensor(var[:, :], stat[:, :, 2], stat[:, :, 5], ALU.add).then_inc(moment, 1)
            dve.wait_ge(moment, before + 3)
            dve.tensor_scalar(mean[:, :], mean[:, :], 0.5, None, ALU.mult).then_inc(moment, 1)
            dve.scalar_tensor_tensor(out=spread[:, :], in0=spread[:, :], scalar=0.25, in1=spread[:, :],
                                     op0=ALU.mult, op1=ALU.mult).then_inc(moment, 1)
            dve.wait_ge(moment, before + 5)
            dve.tensor_scalar(var[:, :], var[:, :], 1.0 / P, EPS, ALU.mult, ALU.add).then_inc(var_ready, 1)
            dve.wait_ge(var_ready, n + 1)
            dve.tensor_tensor(veps[:, :], var[:, :], spread[:, :], ALU.add).then_inc(veps_ready, 1)

        def layer_norm_scale(pool, n):
            pool.wait_ge(veps_ready, n + 1)
            pool.tensor_tensor(rstd[:, :], veps[:, :], minus_half[:, :], ALU.pow).then_inc(ln_ready[n], 1)

        var_ready = sem("var_ready")

        with ExitStack() as prep:
            def stage_sb(name, shape, dt=F32):
                return sb(name, shape, dt, prep)

            wq0_s = stage_sb("wq0_s", [P, H * D0])
            wk0_s = stage_sb("wk0_s", [P, H * D0])
            wv0_s = stage_sb("wv0_s", [P, H * D0])
            wo0_s = stage_sb("wo0_s", [P, G * 2, P])
            qT = stage_sb("qT", [P, G * 2, P])
            kT = stage_sb("kT", [P, G * 2, P])
            mix_s = stage_sb("mix_s", [P, 3, P])
            mix_T = stage_sb("mix_T", [P, 3 * P + E])
            rows_s = stage_sb("rows_s", [NCOL, P])
            one_minus_mu = stage_sb("one_minus_mu", [P, 2])
            att1_s = stage_sb("att1_s", [P, 4, P])
            bo_row = stage_sb("bo_row", [1, P])
            bias1_s = stage_sb("bias1_s", [1, 2, P])
            wg_s = stage_sb("wg_s", [E, P])
            gains_in = stage_sb("gains_in", [P, 4])
            w1_s = stage_sb("w1_s", [P, E * C, P])
            w3_s = stage_sb("w3_s", [P, E * C, P])
            w2_s = stage_sb("w2_s", [P, E, C * P])
            a1_s = stage_sb("a1_s", [R, E, P])
            a3_s = stage_sb("a3_s", [R, E, P])
            a2_s = stage_sb("a2_s", [R, E, C * P])
            bb1_s = stage_sb("bb1_s", [P, E * C, R])
            bb3_s = stage_sb("bb3_s", [P, E * C, R])
            bb2_s = stage_sb("bb2_s", [P, E, R])
            bb1_T = stage_sb("bb1_T", [R, E * C, P])
            bb3_T = stage_sb("bb3_T", [R, E * C, P])
            bb2_T = stage_sb("bb2_T", [R, E, P])

            qk_loaded = sem("qk_loaded")
            vo_loaded = sem("vo_loaded")
            small_loaded = sem("small_loaded")
            mats_loaded = sem("mats_loaded")
            lora_loaded = sem("lora_loaded")
            up_loaded = sem("up_loaded")
            SMALL, MATS, LORA, UP = 12 * 16, 7 * 16, 6 * 16, 3 * 16
            ident_ready = sem("ident_ready")
            const_step = sem("const_step")
            turned = sem("turned")
            kept_even = sem("kept_even")
            kept_odd = sem("kept_odd")
            folded = sem("folded")
            folded_hi = sem("folded_hi")
            folded_lo = sem("folded_lo")
            gain_ready = sem("gain_ready")
            scales_ready = sem("scales_ready")
            raw_hi = sem("raw_hi")
            gained_hi = sem("gained_hi")
            prep_end = sem("prep_end")
            bias_done = sem("bias_done")
            bias_step = sem("bias_step")

            def turns():
                for src, dst in ((wq0_s, qT), (wk0_s, kT)):
                    for half in range(2):
                        yield ([src[:, c * P:(c + 1) * P] for c in range(4 * half, 4 * half + 4)],
                               dst[:, 4 * half:4 * half + 4, :].rearrange("p c d -> p (c d)"))
                yield ([mix_s[:, c, :] for c in range(3)] + [wg_s[:, :]], mix_T[:, :])
                yield [rows_s[:, :]], cols[:, :]
                for src, dst, n in ((bb1_s, bb1_T, E * C), (bb3_s, bb3_T, E * C), (bb2_s, bb2_T, E)):
                    for q in range(n // 4):
                        yield ([src[:, c, :] for c in range(4 * q, 4 * q + 4)],
                               dst[:, 4 * q:4 * q + 4, :].rearrange("p c d -> p (c d)"))

            TURNS = list(turns())
            NT = len(TURNS)
            FOLDS = G + 3 * (E * C // 4)

            def fold_target(n, part):
                if n < G:
                    first = 2 * HG * (n // 2) + n % 2
                    return qk0[:, part, first:first + 2 * HG - 1:2, :]
                which, q = divmod(n - G, E * C // 4)
                return (up1, up3, down)[which][:, part, 4 * q:4 * q + 4, :]

            def fold_bank(n):
                return bank[n % 8][:, :].rearrange("p (c d) -> p c d", d=P)

            heads = stage_sb("heads", [P, H])
            block = prep.enter_context(nc.Block())

            @block.sync
            def _(sp):
                sp.dma_start(wq0_s[:, :], wq0).then_inc(qk_loaded, 16)
                sp.dma_start(wk0_s[:, :], wk0).then_inc(qk_loaded, 16)
                for i, w in enumerate((w_r, w_k, w_v)):
                    sp.dma_start(mix_s[:, i, :], w).then_inc(mats_loaded, 16)
                for i, w in enumerate((wq1, wk1, wv1, wo1)):
                    sp.dma_start(att1_s[:, i, :], w).then_inc(mats_loaded, 16)
                sp.dma_start(bb1_s[:, :, :], bb1.rearrange("e (c p) r -> p (e c) r", p=P)).then_inc(lora_loaded, 16)
                sp.dma_start(bb3_s[:, :, :], bb3.rearrange("e (c p) r -> p (e c) r", p=P)).then_inc(lora_loaded, 16)
                sp.dma_start(bb2_s[:, :, :], bb2.rearrange("e d r -> d e r")).then_inc(lora_loaded, 16)
                sp.dma_start(a1_s[:, :, :], a1.rearrange("e r d -> r e d")).then_inc(lora_loaded, 16)
                sp.dma_start(a3_s[:, :, :], a3.rearrange("e r d -> r e d")).then_inc(lora_loaded, 16)
                sp.dma_start(a2_s[:, :, :], a2.rearrange("e r h -> r e h")).then_inc(lora_loaded, 16)
                sp.dma_start(w1_s[:, :, :], w1.rearrange("e (c p) d -> p (e c) d", p=P)).then_inc(up_loaded, 16)
                sp.dma_start(w3_s[:, :, :], w3.rearrange("e (c p) d -> p (e c) d", p=P)).then_inc(up_loaded, 16)
                sp.dma_start(w2_s[:, :, :], w2.rearrange("e d h -> d e h")).then_inc(up_loaded, 16)
                sp.dma_start(masks[:, :, :], mask.rearrange("b q k -> q b k")).then_inc(masks_loaded, 16)

            @block.scalar
            def _(act):
                act.dma_start(gains_in[:, 0:2], g_xattn.rearrange("(a n) -> a n", a=1).broadcast_to([P, 2])).then_inc(small_loaded, 16)
                act.dma_start(gains_in[:, 2:4], g_ffn.rearrange("(a n) -> a n", a=1).broadcast_to([P, 2])).then_inc(small_loaded, 16)
                act.dma_start(wg_s[:, :], wg).then_inc(small_loaded, 16)
                act.dma_start(rows_s[0:E * C, :], b1.rearrange("e (c p) -> (e c) p", p=P)).then_inc(small_loaded, 16)
                act.dma_start(rows_s[E * C:2 * E * C, :], b3.rearrange("e (c p) -> (e c) p", p=P)).then_inc(small_loaded, 16)
                for i, v in enumerate((bq1, bk1, bv1, mu_r, mu_k)):
                    act.dma_start(rows_s[2 * E * C + i:2 * E * C + i + 1, :], v.rearrange("(a n) -> a n", a=1))\
                       .then_inc(small_loaded, 16)
                act.dma_start(xs[:, :, :], x.rearrange("b s d -> s b d")).then_inc(x_loaded, 16)
                act.dma_start(bo_row[:, :], bo1.rearrange("(a n) -> a n", a=1)).then_inc(small_loaded, 16)
                act.dma_start(wv0_s[:, :], wv0).then_inc(vo_loaded, 16)
                act.dma_start(wo0_s[:, :, :], wo0.rearrange("(c p) d -> p c d", p=P)).then_inc(vo_loaded, 16)
                act.dma_start(b2_row[:, :], b2).then_inc(small_loaded, 16)
                for n in range(0, NT, 2):
                    srcs, dst = TURNS[n]
                    act.wait_ge(turned, n + 1)
                    act.activation(dst, bank[n % 8][0:dst.shape[0], 0:dst.shape[1]], ACT.Copy).then_inc(kept_even, 1)
                    if n == 4:
                        act.wait_ge(small_loaded, SMALL)
                        act.activation(gain[:, :], gains_in[:, :], ACT.Tanh).then_inc(gain_ready, 1)
                act.wait_ge(vo_loaded, 32)
                act.activation(v0[:, 0, :], wv0_s[:, :], ACT.Copy).then_inc(raw_hi, 1)
                act.wait_ge(mats_loaded, MATS)
                act.activation(att1[:, 0, 0:3, :], att1_s[:, 0:3, :], ACT.Copy).then_inc(raw_hi, 1)
                act.wait_ge(kept_even, 3)
                act.activation(router[:, 0, :], mix_T[:, 3 * P:3 * P + E], ACT.Copy).then_inc(raw_hi, 1)
                for n in range(FOLDS):
                    act.wait_ge(folded, n + 1)
                    act.activation(fold_target(n, 0), fold_bank(n), ACT.Copy).then_inc(folded_hi, 1)

            @block.gpsimd
            def _(pool):
                pool.memset(ident[:, :], 0.0).then_inc(const_step, 1)
                pool.wait_ge(const_step, 1)
                pool.affine_select(out=ident[:, :], in_=ident[:, :], compare_op=ALU.not_equal, fill=1.0,
                                   base=0, pattern=[[-1, P]], channel_multiplier=1).then_inc(ident_ready, 1)
                pool.memset(minus_half[:, :], -0.5).then_inc(const_step, 1)
                pool.memset(ones16[:, :], 1.0).then_inc(const_step, 1)
                pool.iota(experts[:, :], pattern=[[1, E]], base=0, channel_multiplier=0,
                          allow_small_or_imprecise_dtypes=True).then_inc(const_step, 1)
                pool.memset(minus_one_at[:, :, :], 0.0).then_inc(const_step, 1)
                pool.wait_ge(const_step, 5)
                for n, row in enumerate((0, 32)):
                    pool.wait_ge(const_step, 5 + n)
                    pool.affine_select(out=minus_one_at[:, :, :], in_=minus_one_at[:, :, :],
                                       compare_op=ALU.not_equal, fill=-1.0, base=-row,
                                       pattern=[[-1, H], [0, P]], channel_multiplier=1).then_inc(const_step, 1)
                pool.memset(heads[:, :], 1.0).then_inc(const_step, 1)
                pool.wait_ge(const_step, 8)
                pool.affine_select(out=heads[:, :], in_=heads[:, :], compare_op=ALU.is_ge, fill=0.0,
                                   base=0, pattern=[[-D1, H]], channel_multiplier=1).then_inc(const_step, 1)
                pool.wait_ge(const_step, 9)
                pool.affine_select(out=heads[:, :], in_=heads[:, :], compare_op=ALU.is_ge, fill=0.0,
                                   base=D1 - 1, pattern=[[D1, H]], channel_multiplier=-1).then_inc(const_step, 1)
                layer_norm_scale(pool, 0)

            @block.vector
            def _(dve):
                dve.wait_ge(ident_ready, 1)
                for i in range(HG):
                    last = dve.tensor_copy(ident4[:, i, :], ident[:, :])
                last.then_inc(prep_end, 1)
                for n in range(1, NT, 2):
                    srcs, dst = TURNS[n]
                    dve.wait_ge(turned, n + 1)
                    dve.tensor_copy(dst, bank[n % 8][0:dst.shape[0], 0:dst.shape[1]]).then_inc(kept_odd, 1)
                dve.wait_ge(gain_ready, 1)
                dve.tensor_scalar(half_gain[:, :], gain[:, :], 0.5, None, ALU.mult).then_inc(scales_ready, 1)
                dve.tensor_scalar(minus_half_gain[:, :], gain[:, :], -0.5, None, ALU.mult).then_inc(scales_ready, 1)
                dve.tensor_scalar(one_minus_mu[:, :], mu, -1.0, 1.0, ALU.mult, ALU.add).then_inc(scales_ready, 1)
                dve.wait_ge(const_step, 10)
                dve.tensor_reduce(slot_of[:, :], heads[:, :].rearrange("p (j i) -> p i j", i=HG), AX.X, ALU.add)\
                   .then_inc(scales_ready, 1)
                dve.wait_ge(scales_ready, 4)
                dve.wait_ge(kept_even, 3)
                dve.wait_ge(vo_loaded, 32)
                dve.wait_ge(mats_loaded, MATS)
                scaled = [(mix[:, :, 0, :], mix_T[:, 0:P], mu[:, 0:1]),
                          (mix[:, :, 1, :], mix_T[:, 0:P], one_minus_mu[:, 0:1]),
                          (mix[:, :, 2, :], mix_T[:, P:2 * P], mu[:, 1:2]),
                          (mix[:, :, 3, :], mix_T[:, P:2 * P], one_minus_mu[:, 1:2]),
                          (mix[:, :, 4, :], mix_T[:, 2 * P:3 * P], half_gain[:, 2:3]),
                          (o0[:, :, :, :].rearrange("p a c d -> p a (c d)"),
                           wo0_s[:, :, :].rearrange("p c d -> p (c d)"), gain[:, 0:1]),
                          (att1[:, :, 3, :], att1_s[:, 3, :], gain[:, 1:2])]
                for n, (to, w, by) in enumerate(scaled):
                    dve.tensor_scalar(to[:, 0], w, by, None, ALU.mult).then_inc(gained_hi, 1)
                for n, (to, w, by) in enumerate(scaled):
                    dve.wait_ge(gained_hi, n + 1)
                    dve.scalar_tensor_tensor(out=to[:, 1], in0=w, scalar=by, in1=to[:, 0],
                                             op0=ALU.mult, op1=ALU.subtract).then_inc(prep_end, 1)
                dve.wait_ge(raw_hi, 3)
                dve.tensor_tensor(v0[:, 1, :], wv0_s[:, :], v0[:, 0, :], ALU.subtract).then_inc(prep_end, 1)
                dve.tensor_tensor(att1[:, 1, 0:3, :], att1_s[:, 0:3, :], att1[:, 0, 0:3, :], ALU.subtract).then_inc(prep_end, 1)
                dve.tensor_tensor(router[:, 1, :], mix_T[:, 3 * P:3 * P + E], router[:, 0, :], ALU.subtract).then_inc(prep_end, 1)
                for n in range(FOLDS):
                    dve.wait_ge(folded_hi, n + 1)
                    dve.tensor_tensor(fold_target(n, 1), fold_bank(n), fold_target(n, 0), ALU.subtract)\
                       .then_inc(folded_lo, 1)
                dve.wait_ge(bias_done, 1)
                dve.tensor_tensor(bias1_s[:, 0, :], bank[0][0:1, 0:P], bo_row[:, :], ALU.add).then_inc(bias_step, 1)
                dve.wait_ge(bias_step, 1)
                dve.tensor_scalar(bias1_s[:, 1, :], bias1_s[:, 0, :], gain[0:1, 1:2], None, ALU.mult).then_inc(bias_step, 1)
                dve.wait_ge(bias_step, 2)
                dve.tensor_copy(bias1[:, 0, :], bias1_s[:, 1, :]).then_inc(bias_step, 1)
                dve.wait_ge(bias_step, 3)
                dve.tensor_tensor(bias1[:, 1, :], bias1_s[:, 1, :], bias1[:, 0, :], ALU.subtract).then_inc(prep_end, 1)
                dve.wait_ge(x_loaded, 16)
                with dve.Fori(0, B) as b:
                    dve.bn_stats(stat[:, bass.ds(b, 1), :], xs[:, bass.ds(b, 1), :]).then_inc(stats_ready, 1)
                dve.wait_ge(stats_ready, B)
                layer_norm_moments(dve, 0)

            @block.tensor
            def _(pe):
                pe.wait_ge(ident_ready, 1)
                for n, (srcs, dst) in enumerate(TURNS):
                    if n >= 8:
                        pe.wait_ge(kept_odd if n % 2 else kept_even, (n - 8) // 2 + 1)
                    if n == 0:
                        pe.wait_ge(qk_loaded, 32)
                    if n == 4:
                        pe.wait_ge(mats_loaded, MATS)
                        pe.wait_ge(small_loaded, SMALL)
                    if n == 6:
                        pe.wait_ge(lora_loaded, LORA)
                    for i, s in enumerate(srcs):
                        rows, cols = s.shape
                        last = pe.transpose(bank[n % 8][0:cols, i * P:i * P + rows], s, ident[0:rows, 0:rows])
                    last.then_inc(turned, 1)
                pe.wait_ge(kept_even, (NT + 1) // 2)
                pe.wait_ge(kept_odd, NT // 2)
                pe.wait_ge(up_loaded, UP)
                for n in range(FOLDS):
                    if n >= 8:
                        pe.wait_ge(folded_lo, n - 7)
                    to = bank[n % 8]
                    for i in range(4):
                        where = to[:, i * P:(i + 1) * P]
                        if n < G:
                            h = 2 * HG * (n // 2) + n % 2 + 2 * i
                            rows = slice(D0 * (h % 2), D0 * (h % 2) + D0)
                            last = pe.matmul(where, qT[rows, h // 2, :], kT[rows, h // 2, :], start=True, stop=True)
                            continue
                        which, q = divmod(n - G, E * C // 4)
                        u = 4 * q + i
                        e, c = divmod(u, C)
                        if which == 2:
                            pe.matmul(where, w2_s[:, e, c * P:(c + 1) * P], ident[:, :], start=True, stop=False)
                            last = pe.matmul(where, a2_s[:, e, c * P:(c + 1) * P], bb2_T[:, e, :], start=False, stop=True)
                        else:
                            w, a, bT = ((w1_s, a1_s, bb1_T), (w3_s, a3_s, bb3_T))[which]
                            pe.matmul(where, w[:, u, :], ident[:, :], start=True, stop=False)
                            last = pe.matmul(where, a[:, e, :], bT[:, u, :], start=False, stop=True)
                    last.then_inc(folded, 1)
                pe.wait_ge(folded_lo, FOLDS - 7)
                pe.matmul(bank[0][0:1, 0:P], bv_col, att1_s[:, 3, :], start=True, stop=True).then_inc(bias_done, 1)


        if stages >= 1:
            with ExitStack() as att:
                def a_sb(name, shape, dt=F32):
                    return sb(name, shape, dt, att)

                xn = a_sb("xn", [P, P])
                ctx_in = a_sb("ctx_in", [P, 2, P])
                xcT = a_sb("xcT", [P, 2, 2, 2 * P], F16)
                t_s = a_sb("t_s", [P, 2, 2, H, P], F16)
                v_s = a_sb("v_s", [P, 2, 2, H, D0 + 1], F16)
                peak = a_sb("peak", [P, H])
                peakT = a_sb("peakT", [P, 2, P], BF16)
                prob = a_sb("prob", [P, 2, HG * P])
                prob_hi = a_sb("prob_hi", [P, 2, HG * P], F16)
                prob_lo = a_sb("prob_lo", [P, 2, HG * P], F16)
                inv = a_sb("inv", [P, 2, HG])
                o_s = a_sb("o_s", [P, 2, HG, D0])
                oT = a_sb("oT", [P, 2, G * 2, P], F16)

                ctx_loaded = [sem(f"ctx_loaded{i}") for i in range(2)]
                blanks_ready = sem("blanks_ready")
                xn_ready = sem("xn_ready")
                turn_done = sem("turn_done")
                turn_hi = sem("turn_hi")
                turn_lo = sem("turn_lo")
                proj_done = sem("proj_done")
                proj_hi = sem("proj_hi")
                proj_lo = sem("proj_lo")
                rough_done = sem("rough_done")
                peak_done = sem("peak_done")
                peak_turned = sem("peak_turned")
                peakT_hi = sem("peakT_hi")
                peakT_lo = sem("peakT_lo")
                score_done = sem("score_done")
                exp_done = sem("exp_done")
                problo_done = sem("problo_done")
                pv_done = sem("pv_done")
                inv_done = sem("inv_done")
                norm_done = sem("norm_done")
                oturn_done = sem("oturn_done")
                oturn_hi = sem("oturn_hi")
                oturn_lo = sem("oturn_lo")
                out_done = sem("out_done")
                res_done = sem("res_done")
                stat_done = sem("stat_done")

                TURN, OUTB, ROUGH, PVB = bank[0], bank[7], bank[3], bank[6]
                PAIRS = (B - 4) // 2

                def pair(t, part):
                    return [t[:, part, i] for i in range(2)]

                block = att.enter_context(nc.Block())

                @block.sync
                def _(sp):
                    def load(c, par):
                        ahead(sp, turn_done, c - 1)
                        sp.dma_start(ctx_in[:, par:par + 1, :],
                                     ctx[bass.ds(c, 1), :, :].rearrange("a s d -> s a d")).then_inc(ctx_loaded[par], 16)
                    load(0, 0)
                    load(1, 1)
                    with sp.Fori(0, B // 2 - 1) as i:
                        load(2 * i + 2, 0)
                        load(2 * i + 3, 1)

                @block.gpsimd
                def _(pool):
                    pool.memset(peakT[:, :, :], 0.0).then_inc(blanks_ready, 1)
                    pool.memset(v_s[:, :, 0, :, D0:D0 + 1], 1.0).then_inc(blanks_ready, 1)
                    pool.memset(v_s[:, :, 1, :, D0:D0 + 1], 0.0).then_inc(blanks_ready, 1)

                    def group(n, par):
                        pool.wait_ge(exp_done, n + 1)
                        ahead(pool, pv_done, n - 1)
                        pool.tensor_tensor(prob_lo[:, par, :], prob[:, par, :], prob_hi[:, par, :],
                                           ALU.subtract).then_inc(problo_done, 1)
                    for n in range(G):
                        group(n, n % 2)
                    with pool.Fori(1, B) as b:
                        for g in range(G):
                            group(G * b + g, g % 2)

                @block.scalar
                def _(act):
                    def hi_turned(a, par):
                        act.wait_ge(turn_done, a + 1)
                        act.activation(xcT[:, par, 0, :], TURN[:, 0:2 * P], ACT.Copy).then_inc(turn_hi, 1)

                    def hi_peak(a, par):
                        act.wait_ge(peak_turned, a + 1)
                        act.activation(peakT[0:H, par, :], TURN[0:H, 0:P], ACT.Copy).then_inc(peakT_hi, 1)

                    def hi_t(a, par, g):
                        act.wait_ge(proj_done, 6 * a + g + 1)
                        act.activation(t_s[:, par, 0, HG * g:HG * g + HG, :].rearrange("p h q -> p (h q)"),
                                       bank[1 + g % 2][:, :], ACT.Copy).then_inc(proj_hi, 1)

                    def hi_v(a, par, j):
                        act.wait_ge(proj_done, 6 * a + G + j + 1)
                        act.activation(v_s[:, par, 0, 8 * j:8 * j + 8, 0:D0],
                                       bank[1 + j][:, :].rearrange("p (h d) -> p h d", d=D0), ACT.Copy).then_inc(proj_hi, 1)

                    def exps(b, g):
                        n = G * b + g
                        act.wait_ge(score_done, n + 1)
                        ahead(act, problo_done, n - 1)
                        ahead(act, pv_done, n - 1)
                        act.activation(prob[:, g % 2, :], bank[4 + g % 2][:, :], ACT.Exp, scale=float(D0) ** -0.5)
                        act.activation(prob_hi[:, g % 2, :], bank[4 + g % 2][:, :], ACT.Exp, scale=float(D0) ** -0.5)\
                           .then_inc(exp_done, 1)

                    def hi_o(b, g):
                        act.wait_ge(oturn_done, G * b + g + 1)
                        act.activation(oT[:, 0, 2 * g:2 * g + 2, :].rearrange("p c q -> p (c q)"),
                                       OUTB[:, 0:2 * P], ACT.Copy).then_inc(oturn_hi, 1)

                    def step(b, par, first=False, after=2):
                        a, ap = b + 1, 1 - par
                        if after >= 1:
                            hi_t(a, ap, 0)
                        if not first:
                            hi_o(b - 1, 2)
                        exps(b, 0)
                        if not first:
                            hi_o(b - 1, 3)
                        if after >= 1:
                            hi_t(a, ap, 1)
                        exps(b, 1)
                        if after >= 1:
                            hi_t(a, ap, 2)
                        exps(b, 2)
                        hi_o(b, 0)
                        if after >= 1:
                            hi_t(a, ap, 3)
                        exps(b, 3)
                        if after >= 2:
                            hi_turned(b + 2, par)
                        if after >= 1:
                            hi_v(a, ap, 0)
                        hi_o(b, 1)
                        if after >= 1:
                            hi_peak(a, ap)
                            hi_v(a, ap, 1)

                    act.wait_ge(blanks_ready, 3)
                    hi_turned(0, 0)
                    for g in range(G):
                        hi_t(0, 0, g)
                    hi_v(0, 0, 0)
                    hi_v(0, 0, 1)
                    hi_turned(1, 1)
                    hi_peak(0, 0)
                    step(0, 0, first=True)
                    with act.Fori(0, PAIRS) as i:
                        step(2 * i + 1, 1)
                        step(2 * i + 2, 0)
                    step(B - 3, 1)
                    step(B - 2, 0, after=1)
                    step(B - 1, 1, after=0)
                    hi_o(B - 1, 2)
                    hi_o(B - 1, 3)

                @block.vector
                def _(dve):
                    def normalize(a):
                        ahead(dve, turn_done, a)
                        dve.tensor_scalar(xn[:, :], xs[:, bass.ds(a, 1), :].rearrange("p a d -> p (a d)"),
                                          mean[:, bass.ds(a, 1)],
                                          rstd[:, bass.ds(a, 1)], ALU.subtract, ALU.mult).then_inc(xn_ready, 1)

                    def lo_turned(a, par):
                        dve.wait_ge(turn_hi, a + 1)
                        dve.tensor_tensor(xcT[:, par, 1, :], TURN[:, 0:2 * P], xcT[:, par, 0, :], ALU.subtract)\
                           .then_inc(turn_lo, 1)

                    def lo_peak(a, par):
                        dve.wait_ge(peakT_hi, a + 1)
                        dve.tensor_tensor(peakT[32:32 + H, par, :], TURN[0:H, 0:P], peakT[0:H, par, :], ALU.subtract)\
                           .then_inc(peakT_lo, 1)

                    def lo_t(a, par, g):
                        dve.wait_ge(proj_hi, 6 * a + g + 1)
                        hs = slice(HG * g, HG * g + HG)
                        dve.tensor_tensor(t_s[:, par, 1, hs, :].rearrange("p h q -> p (h q)"), bank[1 + g % 2][:, :],
                                          t_s[:, par, 0, hs, :].rearrange("p h q -> p (h q)"), ALU.subtract)\
                           .then_inc(proj_lo, 1)

                    def lo_v(a, par, j):
                        dve.wait_ge(proj_hi, 6 * a + G + j + 1)
                        hs = slice(8 * j, 8 * j + 8)
                        dve.tensor_tensor(v_s[:, par, 1, hs, 0:D0], bank[1 + j][:, :].rearrange("p (h d) -> p h d", d=D0),
                                          v_s[:, par, 0, hs, 0:D0], ALU.subtract).then_inc(proj_lo, 1)

                    def maxima(a, g):
                        dve.wait_ge(rough_done, G * a + g + 1)
                        dve.tensor_reduce(peak[:, HG * g:HG * g + HG], ROUGH[:, :].rearrange("p (h k) -> p h k", k=P),
                                          AX.X, ALU.max).then_inc(peak_done, 1)

                    def norm(b, g):
                        n = G * b + g
                        dve.wait_ge(pv_done, n + 1)
                        o = PVB[:, 0:HG * (D0 + 1)].rearrange("p (h d) -> p h d", d=D0 + 1)
                        dve.reciprocal(inv[:, g % 2, :], o[:, :, D0]).then_inc(inv_done, 1)
                        dve.wait_ge(inv_done, n + 1)
                        ahead(dve, oturn_done, n - 1)
                        dve.tensor_tensor(o_s[:, g % 2, :, :], o[:, :, 0:D0],
                                          inv[:, g % 2, :].unsqueeze(2).broadcast_to([P, HG, D0]), ALU.mult)\
                           .then_inc(norm_done, 1)

                    def lo_o(b, g):
                        dve.wait_ge(oturn_hi, G * b + g + 1)
                        cs = slice(2 * g, 2 * g + 2)
                        dve.tensor_tensor(oT[:, 1, cs, :].rearrange("p c q -> p (c q)"), OUTB[:, 0:2 * P],
                                          oT[:, 0, cs, :].rearrange("p c q -> p (c q)"), ALU.subtract).then_inc(oturn_lo, 1)

                    def residual(b):
                        dve.wait_ge(out_done, b + 1)
                        here = xs[:, bass.ds(b, 1), :].rearrange("p a d -> p (a d)")
                        dve.tensor_tensor(here, OUTB[:, 0:P], here, ALU.add).then_inc(res_done, 1)

                    def statistics(b):
                        dve.wait_ge(res_done, b + 1)
                        dve.bn_stats(stat[:, bass.ds(b, 1), :], xs[:, bass.ds(b, 1), :]).then_inc(stat_done, 1)

                    def step(b, par, first=False, after=2):
                        a, ap = b + 1, 1 - par
                        if after >= 2:
                            normalize(b + 2)
                        if after >= 1:
                            lo_t(a, ap, 0)
                        if not first:
                            norm(b - 1, 3)
                            lo_o(b - 1, 2)
                        if not first:
                            lo_o(b - 1, 3)
                        if after >= 1:
                            maxima(a, 0)
                            lo_t(a, ap, 1)
                        if not first:
                            residual(b - 1)
                        norm(b, 0)
                        if not first:
                            statistics(b - 1)
                        if after >= 1:
                            maxima(a, 1)
                            lo_t(a, ap, 2)
                        norm(b, 1)
                        if after >= 1:
                            maxima(a, 2)
                        lo_o(b, 0)
                        if after >= 1:
                            lo_t(a, ap, 3)
                            maxima(a, 3)
                        if after >= 2:
                            lo_turned(b + 2, par)
                        if after >= 1:
                            lo_v(a, ap, 0)
                        lo_o(b, 1)
                        norm(b, 2)
                        if after >= 1:
                            lo_peak(a, ap)
                            lo_v(a, ap, 1)

                    dve.wait_ge(ln_ready[0], 1)
                    dve.wait_ge(blanks_ready, 3)
                    normalize(0)
                    lo_turned(0, 0)
                    normalize(1)
                    for g in range(G):
                        lo_t(0, 0, g)
                    lo_v(0, 0, 0)
                    lo_v(0, 0, 1)
                    lo_turned(1, 1)
                    for g in range(G):
                        maxima(0, g)
                    lo_peak(0, 0)
                    step(0, 0, first=True)
                    with dve.Fori(0, PAIRS) as i:
                        step(2 * i + 1, 1)
                        step(2 * i + 2, 0)
                    step(B - 3, 1)
                    step(B - 2, 0, after=1)
                    step(B - 1, 1, after=0)
                    norm(B - 1, 3)
                    lo_o(B - 1, 2)
                    lo_o(B - 1, 3)
                    residual(B - 1)
                    statistics(B - 1)

                @block.tensor
                def _(pe):
                    def turn(a, par, ctx_count):
                        pe.wait_ge(xn_ready, a + 1)
                        pe.wait_ge(ctx_loaded[par], ctx_count)
                        ahead(pe, peakT_lo, a - 1)
                        pe.transpose(TURN[:, 0:P], xn[:, :], ident[:, :])
                        pe.transpose(TURN[:, P:2 * P], ctx_in[:, par, :], ident[:, :]).then_inc(turn_done, 1)

                    def project_t(a, par, g):
                        ahead(pe, proj_lo, 6 * a + g - 1)
                        if g == 0:
                            pe.wait_ge(turn_lo, a + 1)
                        for i in range(HG):
                            last = product(pe, bank[1 + g % 2][:, i * P:(i + 1) * P],
                                           [qk0[:, s, HG * g + i, :] for s in range(2)],
                                           [xcT[:, par, s, 0:P] for s in range(2)])
                        last.then_inc(proj_done, 1)

                    def project_v(a, par, j):
                        pe.wait_ge(proj_lo, 6 * a + G + j - 1)
                        product(pe, bank[1 + j][:, :], [xcT[:, par, s, P:2 * P] for s in range(2)],
                                [v0[:, s, 512 * j:512 * j + 512] for s in range(2)]).then_inc(proj_done, 1)

                    def rough(a, par, g):
                        pe.wait_ge(proj_hi, 6 * a + g + 1)
                        ahead(pe, peak_done, G * a + g)
                        for i in range(HG):
                            last = pe.matmul(ROUGH[:, i * P:(i + 1) * P], t_s[:, par, 0, HG * g + i, :],
                                             xcT[:, par, 0, P:2 * P], start=True, stop=True)
                        last.then_inc(rough_done, 1)

                    def turn_peak(a, split):
                        pe.wait_ge(peak_done, G * a + G)
                        pe.wait_ge(turn_lo, split)
                        pe.transpose(TURN[0:H, 0:P], peak[:, :], ident[:, :]).then_inc(peak_turned, 1)

                    def scores(b, par, g):
                        n = G * b + g
                        to = bank[4 + g % 2]
                        pe.wait_ge(proj_lo, 6 * b + g + 1)
                        ahead(pe, exp_done, n - 1)
                        product(pe, to[:, :], [xcT[:, par, s, P:2 * P] for s in range(2)],
                                [t_s[:, par, s, HG * g:HG * g + HG, :].rearrange("p h q -> p (h q)") for s in range(2)],
                                stop=False)
                        pe.wait_ge(peakT_lo, b + 1)
                        for i in range(HG):
                            last = pe.matmul(to[:, i * P:(i + 1) * P], minus_one_at[:, HG * g + i, :],
                                             peakT[:, par, :], start=False, stop=(i == HG - 1))
                        last.then_inc(score_done, 1)

                    def times_v(b, par, g):
                        n = G * b + g
                        pe.wait_ge(exp_done, n + 1)
                        pe.wait_ge(problo_done, n + 1)
                        pe.wait_ge(proj_lo, 6 * b + 6)
                        ahead(pe, norm_done, n)
                        for i in range(HG):
                            last = product(pe, PVB[:, i * (D0 + 1):(i + 1) * (D0 + 1)],
                                           [p[:, g % 2, i * P:(i + 1) * P] for p in (prob_hi, prob_lo)],
                                           [v_s[:, par, s, HG * g + i, :] for s in range(2)])
                        last.then_inc(pv_done, 1)

                    def turn_o(b, g):
                        n = G * b + g
                        pe.wait_ge(norm_done, n + 1)
                        ahead(pe, oturn_lo, n)
                        if g == 0:
                            ahead(pe, res_done, b)
                        o = o_s[:, g % 2, :, :].rearrange("p h d -> p (h d)")
                        pe.transpose(OUTB[:, 0:P], o[:, 0:P], ident[:, :])
                        pe.transpose(OUTB[:, P:2 * P], o[:, P:2 * P], ident[:, :]).then_inc(oturn_done, 1)

                    def output(b):
                        pe.wait_ge(oturn_lo, G * b + G)
                        for c in range(2 * G):
                            last = product(pe, OUTB[:, 0:P], [oT[:, s, c, :] for s in range(2)],
                                           [o0[:, s, c, :] for s in range(2)], start=(c == 0), stop=(c == 2 * G - 1))
                        last.then_inc(out_done, 1)

                    def step(b, par, ctx_count=0, first=False, after=2):
                        a, ap = b + 1, 1 - par
                        if after >= 1:
                            project_t(a, ap, 0)
                        if not first:
                            turn_o(b - 1, 2)
                            times_v(b - 1, ap, 3)
                        scores(b, par, 0)
                        if after >= 1:
                            project_t(a, ap, 1)
                            rough(a, ap, 0)
                        if not first:
                            turn_o(b - 1, 3)
                        scores(b, par, 1)
                        if after >= 1:
                            project_t(a, ap, 2)
                        if not first:
                            output(b - 1)
                        times_v(b, par, 0)
                        if after >= 1:
                            rough(a, ap, 1)
                        scores(b, par, 2)
                        turn_o(b, 0)
                        times_v(b, par, 1)
                        if after >= 1:
                            project_t(a, ap, 3)
                            rough(a, ap, 2)
                        scores(b, par, 3)
                        if after >= 2:
                            turn(b + 2, par, ctx_count)
                        if after >= 1:
                            rough(a, ap, 3)
                            project_v(a, ap, 0)
                        turn_o(b, 1)
                        times_v(b, par, 2)
                        if after >= 1:
                            project_v(a, ap, 1)
                            turn_peak(a, b + 3 if after >= 2 else B)

                    pe.wait_ge(blanks_ready, 3)
                    turn(0, 0, 16)
                    for g in range(G):
                        project_t(0, 0, g)
                    project_v(0, 0, 0)
                    project_v(0, 0, 1)
                    turn(1, 1, 16)
                    for g in range(G):
                        rough(0, 0, g)
                    turn_peak(0, 2)
                    step(0, 0, 32, first=True)
                    with pe.Fori(0, PAIRS) as i:
                        step(2 * i + 1, 1, 16 * i + 32)
                        step(2 * i + 2, 0, 16 * i + 48)
                    step(B - 3, 1, 16 * (B // 2))
                    step(B - 2, 0, after=1)
                    step(B - 1, 1, after=0)
                    turn_o(B - 1, 2)
                    times_v(B - 1, 1, 3)
                    turn_o(B - 1, 3)
                    output(B - 1)


        if stages >= 2:
            with ExitStack() as ffn:
                def f_sb(name, shape, dt=F32):
                    return sb(name, shape, dt, ffn)

                f_xn = f_sb("f_xn", [P, P])
                xT = f_sb("xT", [P, 2, 2, P + 1], F16)
                tanh_r = f_sb("tanh_r", [P, 2, P])
                relu_k = f_sb("relu_k", [P, 2, P])
                k_sq = f_sb("k_sq", [P, P])
                k_s = f_sb("k_s", [P, 2, 2, P], F16)
                gated = f_sb("gated", [P, P])

                f_blank = sem("f_blank")
                f_xn_ready = sem("f_xn_ready")
                f_turn = sem("f_turn")
                f_turn_hi = sem("f_turn_hi")
                f_turn_lo = sem("f_turn_lo")
                f_rk = sem("f_rk")
                f_act = sem("f_act")
                f_sq = sem("f_sq")
                f_k_hi = sem("f_k_hi")
                f_k_lo = sem("f_k_lo")
                f_v = sem("f_v")
                f_gated = sem("f_gated")
                f_res = sem("f_res")
                f_stat = sem("f_stat")
                F_PAIRS = (B - 2) // 2

                with nc.Block() as block:
                    @block.gpsimd
                    def _(pool):
                        layer_norm_scale(pool, 1)
                        pool.memset(xT[:, :, :, 0:1], 0.0).then_inc(f_blank, 1)

                    @block.scalar
                    def _(act):
                        def hi_turned(a, par):
                            act.wait_ge(f_turn, a + 1)
                            act.activation(xT[:, par, 0, 1:P + 1], bank[par][:, 0:P], ACT.Copy).then_inc(f_turn_hi, 1)

                        def gates(b, par):
                            act.wait_ge(f_rk, b + 1)
                            ahead(act, f_res, b - 1)
                            act.activation(tanh_r[:, par, :], bank[2 + par][:, 0:P], ACT.Tanh, scale=0.5)
                            act.activation(relu_k[:, par, :], bank[2 + par][:, P:2 * P], ACT.Relu).then_inc(f_act, 1)

                        def hi_k(b, par):
                            act.wait_ge(f_sq, b + 1)
                            act.activation(k_s[:, par, 0, :], k_sq[:, :], ACT.Copy).then_inc(f_k_hi, 1)

                        def step(b, par, last=False):
                            gates(b, par)
                            if not last:
                                hi_turned(b + 1, 1 - par)
                            hi_k(b, par)

                        hi_turned(0, 0)
                        step(0, 0)
                        with act.Fori(0, F_PAIRS) as i:
                            step(2 * i + 1, 1)
                            step(2 * i + 2, 0)
                        step(B - 1, 1, last=True)

                    @block.vector
                    def _(dve):
                        def normalize(a):
                            ahead(dve, f_turn, a)
                            dve.tensor_scalar(f_xn[:, :], xs[:, bass.ds(a, 1), :].rearrange("p a d -> p (a d)"),
                                              mean[:, bass.ds(a, 1)],
                                              rstd[:, bass.ds(a, 1)], ALU.subtract, ALU.mult).then_inc(f_xn_ready, 1)

                        def lo_turned(a, par):
                            dve.wait_ge(f_turn_hi, a + 1)
                            dve.tensor_tensor(xT[:, par, 1, 1:P + 1], bank[par][:, 0:P], xT[:, par, 0, 1:P + 1],
                                              ALU.subtract).then_inc(f_turn_lo, 1)

                        def square(b, par):
                            dve.wait_ge(f_act, b + 1)
                            ahead(dve, f_k_lo, b)
                            dve.tensor_tensor(k_sq[:, :], relu_k[:, par, :], relu_k[:, par, :], ALU.mult).then_inc(f_sq, 1)

                        def lo_k(b, par):
                            dve.wait_ge(f_k_hi, b + 1)
                            dve.tensor_tensor(k_s[:, par, 1, :], k_sq[:, :], k_s[:, par, 0, :], ALU.subtract).then_inc(f_k_lo, 1)

                        def residual(b, par):
                            dve.wait_ge(f_v, b + 1)
                            here = xs[:, bass.ds(b, 1), :].rearrange("p a d -> p (a d)")
                            dve.scalar_tensor_tensor(out=gated[:, :], in0=tanh_r[:, par, :], scalar=1.0,
                                                     in1=bank[4 + par][:, 0:P], op0=ALU.add, op1=ALU.mult).then_inc(f_gated, 1)
                            dve.wait_ge(f_gated, b + 1)
                            dve.tensor_tensor(here, gated[:, :], here, ALU.add).then_inc(f_res, 1)
                            dve.wait_ge(f_res, b + 1)
                            dve.bn_stats(stat[:, bass.ds(b, 1), :], xs[:, bass.ds(b, 1), :]).then_inc(f_stat, 1)

                        def step(b, par, first=False, last=False):
                            if not last:
                                normalize(b + 1)
                            square(b, par)
                            if not last:
                                lo_turned(b + 1, 1 - par)
                            if not first:
                                residual(b - 1, 1 - par)
                            lo_k(b, par)

                        layer_norm_moments(dve, 1)
                        dve.wait_ge(ln_ready[1], 1)
                        dve.wait_ge(f_blank, 1)
                        normalize(0)
                        lo_turned(0, 0)
                        step(0, 0, first=True)
                        with dve.Fori(0, F_PAIRS) as i:
                            step(2 * i + 1, 1)
                            step(2 * i + 2, 0)
                        step(B - 1, 1, last=True)
                        residual(B - 1, 1)

                    @block.tensor
                    def _(pe):
                        def turn(a, par):
                            pe.wait_ge(f_xn_ready, a + 1)
                            ahead(pe, f_turn_lo, a - 1)
                            pe.transpose(bank[par][:, 0:P], f_xn[:, :], ident[:, :]).then_inc(f_turn, 1)

                        def r_and_k(b, par):
                            pe.wait_ge(f_turn_lo, b + 1)
                            ahead(pe, f_act, b - 1)
                            to = bank[2 + par]
                            now = [xT[:, par, s, 1:P + 1] for s in range(2)]
                            before = [xT[:, par, s, 0:P] for s in range(2)]
                            wr, wr_prev, wk, wk_prev = ([mix[:, s, n, :] for s in range(2)] for n in range(4))
                            product(pe, to[:, 0:P], now, wr, stop=False)
                            product(pe, to[:, 0:P], before, wr_prev, start=False)
                            product(pe, to[:, P:2 * P], wk, now, stop=False)
                            product(pe, to[:, P:2 * P], wk_prev, before, start=False).then_inc(f_rk, 1)

                        def times_v(b, par):
                            pe.wait_ge(f_k_lo, b + 1)
                            product(pe, bank[4 + par][:, 0:P], [k_s[:, par, s, :] for s in range(2)],
                                    [mix[:, s, 4, :] for s in range(2)]).then_inc(f_v, 1)

                        def step(b, par, first=False, last=False):
                            r_and_k(b, par)
                            if not last:
                                turn(b + 1, 1 - par)
                            if not first:
                                times_v(b - 1, 1 - par)

                        turn(0, 0)
                        step(0, 0, first=True)
                        with pe.Fori(0, F_PAIRS) as i:
                            step(2 * i + 1, 1)
                            step(2 * i + 2, 0)
                        step(B - 1, 1, last=True)
                        times_v(B - 1, 1)

        if stages >= 3:
            with ExitStack() as att:
                def b_sb(name, shape, dt=F32):
                    return sb(name, shape, dt, att)

                yn = b_sb("yn", [P, P])
                ctx1 = b_sb("ctx1", [P, 2, P])
                ycT = b_sb("ycT", [P, 2, 2, 2 * P], F16)
                qk32 = b_sb("qk32", [P, 2, P])
                qk16 = b_sb("qk16", [P, 2, 2, P], F16)
                q_s = b_sb("q_s", [P, 2, 2, HG, P], F16)
                k_z = b_sb("k_z", [P, 2, G, 2, P], F16)
                v1 = b_sb("v1", [P, 2, 2, H, D1 + 1], F16)
                hide = b_sb("hide", [P, 2, P], BF16)
                peak1 = b_sb("peak1", [P, H])
                peak1c = b_sb("peak1c", [P, H])
                peak1T = b_sb("peak1T", [P, 2, P], BF16)
                pr = b_sb("pr", [P, 2, HG * P])
                pr_hi = b_sb("pr_hi", [P, 2, HG * P], F16)
                pr_lo = b_sb("pr_lo", [P, 2, HG * P], F16)
                inv1 = b_sb("inv1", [P, H])
                o1 = b_sb("o1", [P, H, D1])
                o1T = b_sb("o1T", [P, 2, P], F16)

                c_loaded = [sem(f"c_loaded{i}") for i in range(2)]
                c_blank = sem("c_blank")
                c_xn = sem("c_xn")
                c_turn = sem("c_turn")
                c_turn_hi = sem("c_turn_hi")
                c_turn_lo = sem("c_turn_lo")
                c_qkv = sem("c_qkv")
                c_biased = sem("c_biased")
                c_v_hi = sem("c_v_hi")
                c_v_lo = sem("c_v_lo")
                c_qk_hi = sem("c_qk_hi")
                c_qk_lo = sem("c_qk_lo")
                c_slots = sem("c_slots")
                c_hide = sem("c_hide")
                c_rough = sem("c_rough")
                c_peak = sem("c_peak")
                c_peak_turn = sem("c_peak_turn")
                c_peak_hi = sem("c_peak_hi")
                c_peak_lo = sem("c_peak_lo")
                c_clip = sem("c_clip")
                c_score = sem("c_score")
                c_exp = sem("c_exp")
                c_lo = sem("c_lo")
                c_pv = sem("c_pv")
                c_inv = sem("c_inv")
                c_norm = sem("c_norm")
                c_oturn = sem("c_oturn")
                c_o_hi = sem("c_o_hi")
                c_o_lo = sem("c_o_lo")
                c_out = sem("c_out")
                c_res = sem("c_res")
                c_stat = sem("c_stat")
                TURN1, QKV, ROUGH1, PV1, OUT1 = bank[0], bank[1], bank[2:4], bank[6], bank[7]
                C_PAIRS = (B - 4) // 2
                W = D1 + 1

                with nc.Block() as block:
                    @block.sync
                    def _(sp):
                        def load(c, par):
                            ahead(sp, c_turn, c - 1)
                            sp.dma_start(ctx1[:, par:par + 1, :],
                                         ctx[bass.ds(c, 1), :, :].rearrange("a s d -> s a d")).then_inc(c_loaded[par], 16)
                        load(0, 0)
                        load(1, 1)
                        with sp.Fori(0, B // 2 - 1) as i:
                            load(2 * i + 2, 0)
                            load(2 * i + 3, 1)

                    @block.gpsimd
                    def _(pool):
                        layer_norm_scale(pool, 2)
                        pool.memset(peak1T[:, :, :], 0.0).then_inc(c_blank, 1)
                        pool.memset(k_z[:, :, :, :, :], 0.0).then_inc(c_blank, 1)
                        pool.memset(v1[:, :, 0, :, D1:W], 1.0).then_inc(c_blank, 1)
                        pool.memset(v1[:, :, 1, :, D1:W], 0.0).then_inc(c_blank, 1)

                        def group(n, par):
                            pool.wait_ge(c_exp, n + 1)
                            ahead(pool, c_pv, n - 1)
                            pool.tensor_tensor(pr_lo[:, par, :], pr[:, par, :], pr_hi[:, par, :],
                                               ALU.subtract).then_inc(c_lo, 1)
                        for n in range(G):
                            group(n, n % 2)
                        with pool.Fori(1, B) as b:
                            for g in range(G):
                                group(G * b + g, g % 2)

                    @block.scalar
                    def _(act):
                        def hi_turned(n, par):
                            act.wait_ge(c_turn, n + 1)
                            act.activation(ycT[:, par, 0, :], TURN1[:, 0:2 * P], ACT.Copy).then_inc(c_turn_hi, 1)

                        def hi_peak(a, par):
                            act.wait_ge(c_peak_turn, a + 1)
                            act.activation(peak1T[0:H, par, :], TURN1[0:H, 0:P], ACT.Copy).then_inc(c_peak_hi, 1)

                        def biased(a):
                            act.wait_ge(c_qkv, a + 1)
                            ahead(act, c_qk_lo, a)
                            act.activation(qk32[:, 0, :], QKV[:, 0:P], ACT.Identity, bias=bq_col)
                            act.activation(qk32[:, 1, :], QKV[:, P:2 * P], ACT.Identity, bias=bk_col).then_inc(c_biased, 1)

                        def hi_v(a, par):
                            act.wait_ge(c_qkv, a + 1)
                            ahead(act, c_pv, G * (a - 1))
                            act.activation(v1[:, par, 0, :, 0:D1], QKV[:, 2 * P:3 * P].rearrange("p (h d) -> p h d", d=D1),
                                           ACT.Copy).then_inc(c_v_hi, 1)

                        def exps(b, g):
                            n = G * b + g
                            act.wait_ge(c_score, n + 1)
                            ahead(act, c_lo, n - 1)
                            ahead(act, c_pv, n - 1)
                            act.activation(pr[:, g % 2, :], bank[4 + g % 2][:, :], ACT.Exp, scale=float(D1) ** -0.5)
                            act.activation(pr_hi[:, g % 2, :], bank[4 + g % 2][:, :], ACT.Exp, scale=float(D1) ** -0.5)\
                               .then_inc(c_exp, 1)

                        def hi_o(b):
                            act.wait_ge(c_oturn, b + 1)
                            act.activation(o1T[:, 0, :], OUT1[:, 0:P], ACT.Copy).then_inc(c_o_hi, 1)

                        def step(b, par, first=False, after=2):
                            a, ap = b + 1, 1 - par
                            if after >= 1:
                                biased(a)
                            exps(b, 0)
                            if after >= 1:
                                hi_v(a, ap)
                            exps(b, 1)
                            if after >= 2:
                                hi_turned(b + 2, par)
                            if not first:
                                hi_o(b - 1)
                            exps(b, 2)
                            exps(b, 3)
                            if after >= 1:
                                hi_peak(a, ap)

                        act.wait_ge(c_blank, 4)
                        hi_turned(0, 0)
                        biased(0)
                        hi_v(0, 0)
                        hi_turned(1, 1)
                        hi_peak(0, 0)
                        step(0, 0, first=True)
                        with act.Fori(0, C_PAIRS) as i:
                            step(2 * i + 1, 1)
                            step(2 * i + 2, 0)
                        step(B - 3, 1)
                        step(B - 2, 0, after=1)
                        step(B - 1, 1, after=0)
                        hi_o(B - 1)

                    @block.vector
                    def _(dve):
                        def normalize(a):
                            ahead(dve, c_turn, a)
                            dve.tensor_scalar(yn[:, :], xs[:, bass.ds(a, 1), :].rearrange("p a d -> p (a d)"),
                                              mean[:, bass.ds(a, 1)],
                                              rstd[:, bass.ds(a, 1)], ALU.subtract, ALU.mult).then_inc(c_xn, 1)

                        def hide_masked(a, par):
                            ahead(dve, c_score, G * (a - 1))
                            dve.tensor_scalar(hide[:, par, :], masks[:, bass.ds(a, 1), :].rearrange("p a k -> p (a k)"),
                                              0, -BIG, ALU.is_equal, ALU.mult).then_inc(c_hide, 1)

                        def lo_turned(n, par):
                            dve.wait_ge(c_turn_hi, n + 1)
                            dve.tensor_tensor(ycT[:, par, 1, :], TURN1[:, 0:2 * P], ycT[:, par, 0, :], ALU.subtract).then_inc(c_turn_lo, 1)

                        def lo_peak(a, par):
                            dve.wait_ge(c_peak_hi, a + 1)
                            dve.tensor_tensor(peak1T[32:32 + H, par, :], TURN1[0:H, 0:P], peak1T[0:H, par, :],
                                              ALU.subtract).then_inc(c_peak_lo, 1)

                        def split_qk(a):
                            dve.wait_ge(c_biased, a + 1)
                            ahead(dve, c_slots, a)
                            dve.tensor_copy(qk16[:, :, 0, :], qk32[:, :, :]).then_inc(c_qk_hi, 1)

                        def split_qk_lo(a):
                            dve.wait_ge(c_qk_hi, a + 1)
                            dve.tensor_tensor(qk16[:, :, 1, :], qk32[:, :, :], qk16[:, :, 0, :], ALU.subtract).then_inc(c_qk_lo, 1)

                        def q_slots(a, par):
                            dve.wait_ge(c_qk_lo, a + 1)
                            for i in range(HG):
                                dve.tensor_scalar(q_s[:, par, :, i, :], qk16[:, 0, :, :], slot_of[:, i:i + 1], None, ALU.mult)

                        def k_slots(par):
                            for j in range(G):
                                rows = slice(32 * j, 32 * j + 32)
                                last = dve.tensor_copy(k_z[rows, par, j, :, :], qk16[rows, 1, :, :])
                            last.then_inc(c_slots, 1)

                        def lo_v(a, par):
                            dve.wait_ge(c_v_hi, a + 1)
                            dve.tensor_tensor(v1[:, par, 1, :, 0:D1], QKV[:, 2 * P:3 * P].rearrange("p (h d) -> p h d", d=D1),
                                              v1[:, par, 0, :, 0:D1], ALU.subtract).then_inc(c_v_lo, 1)

                        def maxima(a, g):
                            dve.wait_ge(c_rough, G * a + g + 1)
                            dve.tensor_reduce(peak1[:, HG * g:HG * g + HG],
                                              ROUGH1[g % 2][:, :].rearrange("p (h k) -> p h k", k=P),
                                              AX.X, ALU.max).then_inc(c_peak, 1)

                        def clip(a):
                            dve.wait_ge(c_peak, G * a + G)
                            dve.tensor_scalar(peak1c[:, :], peak1[:, :], -BIG / 16, None, ALU.max).then_inc(c_clip, 1)

                        def norm(b):
                            dve.wait_ge(c_pv, G * b + G)
                            o = PV1[:, 0:H * W].rearrange("p (h d) -> p h d", d=W)
                            dve.reciprocal(inv1[:, :], o[:, :, D1]).then_inc(c_inv, 1)
                            dve.wait_ge(c_inv, b + 1)
                            ahead(dve, c_oturn, b)
                            dve.tensor_tensor(o1[:, :, :], o[:, :, 0:D1],
                                              inv1[:, :].unsqueeze(2).broadcast_to([P, H, D1]), ALU.mult).then_inc(c_norm, 1)

                        def lo_o(b):
                            dve.wait_ge(c_o_hi, b + 1)
                            dve.tensor_tensor(o1T[:, 1, :], OUT1[:, 0:P], o1T[:, 0, :], ALU.subtract).then_inc(c_o_lo, 1)

                        def residual(b):
                            dve.wait_ge(c_out, b + 1)
                            here = xs[:, bass.ds(b, 1), :].rearrange("p a d -> p (a d)")
                            dve.tensor_tensor(here, OUT1[:, 0:P], here, ALU.add).then_inc(c_res, 1)
                            dve.wait_ge(c_res, b + 1)
                            dve.bn_stats(stat[:, bass.ds(b, 1), :], xs[:, bass.ds(b, 1), :]).then_inc(c_stat, 1)

                        def step(b, par, first=False, after=2):
                            a, ap = b + 1, 1 - par
                            if after >= 1:
                                split_qk(a)
                                split_qk_lo(a)
                                q_slots(a, ap)
                            if not first:
                                norm(b - 1)
                            if after >= 1:
                                k_slots(ap)
                                lo_v(a, ap)
                            if after >= 2:
                                lo_turned(b + 2, par)
                            if not first:
                                lo_o(b - 1)
                            if after >= 3:
                                normalize(b + 3)
                            if after >= 1:
                                for g in range(G):
                                    maxima(a, g)
                                clip(a)
                            if not first:
                                residual(b - 1)
                            if after >= 1:
                                lo_peak(a, ap)
                            if after >= 2:
                                hide_masked(b + 2, par)

                        layer_norm_moments(dve, 2)
                        dve.wait_ge(ln_ready[2], 1)
                        dve.wait_ge(c_blank, 4)
                        dve.wait_ge(masks_loaded, 16)
                        normalize(0)
                        hide_masked(0, 0)
                        lo_turned(0, 0)
                        normalize(1)
                        split_qk(0)
                        split_qk_lo(0)
                        q_slots(0, 0)
                        k_slots(0)
                        lo_v(0, 0)
                        lo_turned(1, 1)
                        hide_masked(1, 1)
                        normalize(2)
                        for g in range(G):
                            maxima(0, g)
                        clip(0)
                        lo_peak(0, 0)
                        step(0, 0, first=True, after=3)
                        with dve.Fori(0, C_PAIRS) as i:
                            step(2 * i + 1, 1, after=3)
                            step(2 * i + 2, 0, after=3)
                        step(B - 3, 1)
                        step(B - 2, 0, after=1)
                        step(B - 1, 1, after=0)
                        norm(B - 1)
                        lo_o(B - 1)
                        residual(B - 1)

                    @block.tensor
                    def _(pe):
                        def turn(a, par, ctx_count):
                            pe.wait_ge(c_xn, a + 1)
                            pe.wait_ge(c_loaded[par], ctx_count)
                            ahead(pe, c_peak_lo, a - 1)
                            pe.transpose(TURN1[:, 0:P], yn[:, :], ident[:, :])
                            pe.transpose(TURN1[:, P:2 * P], ctx1[:, par, :], ident[:, :]).then_inc(c_turn, 1)

                        def project(a, par):
                            pe.wait_ge(c_turn_lo, a + 1)
                            ahead(pe, c_v_lo, a)
                            xT_, cT_ = ([ycT[:, par, s, w * P:(w + 1) * P] for s in range(2)] for w in range(2))
                            wq, wk, wv = ([att1[:, s, n, :] for s in range(2)] for n in range(3))
                            product(pe, QKV[:, 0:P], wq, xT_)
                            product(pe, QKV[:, P:2 * P], wk, cT_)
                            product(pe, QKV[:, 2 * P:3 * P], cT_, wv).then_inc(c_qkv, 1)

                        def rough(a, par, g):
                            pe.wait_ge(c_slots, a + 1)
                            pe.wait_ge(c_hide, a + 1)
                            ahead(pe, c_peak, G * a + g - 1)
                            to = ROUGH1[g % 2]
                            pe.matmul(to[:, :].rearrange("p (h k) -> p h k", k=P), ident4[:, 0, :],
                                      hide[:, par, :].unsqueeze(1).broadcast_to([P, HG, P]), start=True, stop=False)
                            for i in range(HG):
                                last = pe.matmul(to[:, i * P:(i + 1) * P], q_s[:, par, 0, i, :], k_z[:, par, g, 0, :],
                                                 start=False, stop=(i == HG - 1))
                            last.then_inc(c_rough, 1)

                        def turn_peak(a, turned):
                            pe.wait_ge(c_clip, a + 1)
                            pe.wait_ge(c_turn_lo, turned)
                            pe.transpose(TURN1[0:H, 0:P], peak1c[:, :], ident[:, :]).then_inc(c_peak_turn, 1)

                        def scores(b, par, g):
                            n = G * b + g
                            to = bank[4 + g % 2]
                            ahead(pe, c_exp, n - 1)
                            product(pe, to[:, :], [k_z[:, par, g, s, :] for s in range(2)],
                                    [q_s[:, par, s, :, :].rearrange("p i q -> p (i q)") for s in range(2)], stop=False)
                            pe.matmul(to[:, :], hide[:, par, :], ident4[:, :, :].rearrange("p i q -> p (i q)"),
                                      start=False, stop=False)
                            pe.wait_ge(c_peak_lo, b + 1)
                            for i in range(HG):
                                last = pe.matmul(to[:, i * P:(i + 1) * P], minus_one_at[:, HG * g + i, :],
                                                 peak1T[:, par, :], start=False, stop=(i == HG - 1))
                            last.then_inc(c_score, 1)

                        def times_v(b, par, g):
                            n = G * b + g
                            pe.wait_ge(c_exp, n + 1)
                            pe.wait_ge(c_lo, n + 1)
                            if g == 0:
                                ahead(pe, c_norm, b)
                            for i in range(HG):
                                h = HG * g + i
                                last = product(pe, PV1[:, h * W:(h + 1) * W],
                                               [p[:, g % 2, i * P:(i + 1) * P] for p in (pr_hi, pr_lo)],
                                               [v1[:, par, s, h, :] for s in range(2)])
                            last.then_inc(c_pv, 1)

                        def turn_o(b):
                            pe.wait_ge(c_norm, b + 1)
                            ahead(pe, c_res, b)
                            pe.transpose(OUT1[:, 0:P], o1[:, :, :].rearrange("p h d -> p (h d)"), ident[:, :]).then_inc(c_oturn, 1)

                        def output(b):
                            pe.wait_ge(c_o_lo, b + 1)
                            product(pe, OUT1[:, 0:P], [o1T[:, s, :] for s in range(2)], [att1[:, s, 3, :] for s in range(2)],
                                    stop=False)
                            pe.matmul(OUT1[:, 0:P], ones16[:, :], bias1[:, 0, :], start=False, stop=False)
                            pe.matmul(OUT1[:, 0:P], ones16[:, :], bias1[:, 1, :], start=False, stop=True).then_inc(c_out, 1)

                        def step(b, par, ctx_count=0, first=False, after=2):
                            a, ap = b + 1, 1 - par
                            if after >= 1:
                                project(a, ap)
                            scores(b, par, 0)
                            scores(b, par, 1)
                            if not first:
                                times_v(b - 1, ap, 3)
                            if after >= 2:
                                turn(b + 2, par, ctx_count)
                            scores(b, par, 2)
                            if not first:
                                turn_o(b - 1)
                            times_v(b, par, 0)
                            if after >= 1:
                                rough(a, ap, 0)
                                rough(a, ap, 1)
                            if not first:
                                output(b - 1)
                            times_v(b, par, 1)
                            if after >= 1:
                                rough(a, ap, 2)
                                rough(a, ap, 3)
                            scores(b, par, 3)
                            if after >= 1:
                                turn_peak(a, b + 3 if after >= 2 else B)
                            times_v(b, par, 2)

                        pe.wait_ge(c_blank, 4)
                        turn(0, 0, 16)
                        project(0, 0)
                        turn(1, 1, 16)
                        for g in range(G):
                            rough(0, 0, g)
                        turn_peak(0, 2)
                        step(0, 0, 32, first=True)
                        with pe.Fori(0, C_PAIRS) as i:
                            step(2 * i + 1, 1, 16 * i + 32)
                            step(2 * i + 2, 0, 16 * i + 48)
                        step(B - 3, 1, 16 * (B // 2))
                        step(B - 2, 0, after=1)
                        step(B - 1, 1, after=0)
                        times_v(B - 1, 1, 3)
                        turn_o(B - 1)
                        output(B - 1)


        if stages >= 4:
            with ExitStack() as moe:
                def m_sb(name, shape, dt=F32):
                    return sb(name, shape, dt, moe)

                T = TILES
                SETS = B // T
                zn = m_sb("zn", [P, T, P])
                zT = m_sb("zT", [P, 2, 2, T * P], F16)
                logits = m_sb("logits", [P, T, E])
                top = m_sb("top", [P, T, 8])
                top_at = m_sb("top_at", [P, T, 8], U32)
                two_at = m_sb("two_at", [P, T, 2])
                lead = m_sb("lead", [P, T])
                tanh_lead = m_sb("tanh_lead", [P, T])
                two_gates = m_sb("two_gates", [P, T, 2])
                picked = m_sb("picked", [P, T, 2, E])
                picked_gate = m_sb("picked_gate", [P, T, 2, E])
                gate = m_sb("gate", [P, 2, T, E])
                gateT = m_sb("gateT", [E, T * P])
                silu = m_sb("silu", [P, C, T * P])
                g32 = m_sb("g32", [P, C, T * P])
                g_s = m_sb("g_s", [P, 2, C, 2, T * P], F16)
                acc = m_sb("acc", [P, 2, T, P])

                z_norm = sem("z_norm")
                z_turn = sem("z_turn")
                z_hi = sem("z_hi")
                z_lo = sem("z_lo")
                z_logits = sem("z_logits")
                z_kept = sem("z_kept")
                z_ranked = sem("z_ranked")
                z_top = sem("z_top")
                z_at = sem("z_at")
                z_lead = sem("z_lead")
                z_tanh = sem("z_tanh")
                z_two = sem("z_two")
                z_picked = sem("z_picked")
                z_pgate = sem("z_pgate")
                z_gate = sem("z_gate")
                z_gturn = sem("z_gturn")
                z_gateT = sem("z_gateT")
                z_b2 = sem("z_b2")
                z_start = sem("z_start")
                h1_done = sem("h1_done")
                h3_done = sem("h3_done")
                silu_done = sem("silu_done")
                g_done = sem("g_done")
                g_hi = sem("g_hi")
                g_lo = sem("g_lo")
                y_done = sem("y_done")
                acc_done = sem("acc_done")
                set_stored = [sem(f"set_stored{i}") for i in range(2)]
                H1B, H3B, YB, TURNB, SMALLB = bank[0:2], bank[2:4], bank[4:6], bank[6], bank[7]
                S_PAIRS = (SETS - 2) // 2

                with nc.Block() as block:
                    @block.sync
                    def _(sp):
                        def store(s, par):
                            sp.wait_ge(acc_done, T * E * (s + 1))
                            sp.dma_start(out[bass.ds(T * s, T), :, :].rearrange("b s d -> s b d"), acc[:, par, :, :])\
                              .then_inc(set_stored[par], 16)
                        with sp.Fori(0, SETS // 2) as i:
                            store(2 * i, 0)
                            store(2 * i + 1, 1)
                        for par in range(2):
                            sp.wait_ge(set_stored[par], 16 * (SETS // 2))

                    @block.gpsimd
                    def _(pool):
                        layer_norm_scale(pool, 3)

                        def lo_g(s, e):
                            for c in range(C):
                                v = E * C * s + C * e + c
                                pool.wait_ge(g_hi, v + 1)
                                ahead(pool, y_done, E * s + e - 1)
                                pool.tensor_tensor(g_s[:, e % 2, c, 1, :], g32[:, c, :], g_s[:, e % 2, c, 0, :],
                                                   ALU.subtract).then_inc(g_lo, 1)
                        for e in range(E):
                            lo_g(0, e)
                        with pool.Fori(1, SETS) as s:
                            for e in range(E):
                                lo_g(s, e)

                    @block.scalar
                    def _(act):
                        def hi_turned(a, par):
                            act.wait_ge(z_turn, a + 1)
                            act.activation(zT[:, par, 0, :], TURNB[:, :], ACT.Copy).then_inc(z_hi, 1)

                        def tanh(a):
                            act.wait_ge(z_lead, a + 1)
                            act.activation(tanh_lead[:, :], lead[:, :], ACT.Tanh, scale=0.5).then_inc(z_tanh, 1)

                        def keep_gateT(a):
                            act.wait_ge(z_gturn, a + 1)
                            act.activation(gateT[:, :], SMALLB[0:E, :], ACT.Copy).then_inc(z_gateT, 1)

                        def silu_h1(s, e, c):
                            v = E * C * s + C * e + c
                            act.wait_ge(h1_done, v + 1)
                            ahead(act, g_done, v - 1)
                            act.activation(silu[:, c, :], H1B[c][:, :], ACT.Silu,
                                           bias=b1_col[:, C * e + c:C * e + c + 1]).then_inc(silu_done, 1)

                        def hi_g(s, e, c):
                            v = E * C * s + C * e + c
                            act.wait_ge(g_done, v + 1)
                            ahead(act, y_done, E * s + e - 1)
                            act.activation(g_s[:, e % 2, c, 0, :], g32[:, c, :], ACT.Copy).then_inc(g_hi, 1)

                        def step(s, par, last=False):
                            for e in range(E):
                                silu_h1(s, e, 0)
                                silu_h1(s, e, 1)
                                hi_g(s, e, 0)
                                hi_g(s, e, 1)
                                if not last:
                                    if e == 1:
                                        hi_turned(s + 1, 1 - par)
                                    if e == 3:
                                        tanh(s + 1)
                                    if e == 5:
                                        keep_gateT(s + 1)

                        hi_turned(0, 0)
                        tanh(0)
                        keep_gateT(0)
                        step(0, 0)
                        with act.Fori(0, S_PAIRS) as i:
                            step(2 * i + 1, 1)
                            step(2 * i + 2, 0)
                        step(SETS - 1, 1, last=True)

                    @block.vector
                    def _(dve):
                        def normalize(a):
                            ahead(dve, z_turn, a)
                            for t in range(T):
                                last = dve.tensor_scalar(zn[:, t, :], xs[:, bass.ds(T * a + t, 1), :].rearrange("p a d -> p (a d)"),
                                                         mean[:, bass.ds(T * a + t, 1)],
                                                         rstd[:, bass.ds(T * a + t, 1)], ALU.subtract, ALU.mult)
                            last.then_inc(z_norm, 1)

                        def lo_turned(a, par):
                            dve.wait_ge(z_hi, a + 1)
                            dve.tensor_tensor(zT[:, par, 1, :], TURNB[:, :], zT[:, par, 0, :], ALU.subtract).then_inc(z_lo, 1)

                        def rank(a):
                            dve.wait_ge(z_logits, a + 1)
                            ahead(dve, z_top, a)
                            dve.tensor_copy(logits[:, :, :].rearrange("p t e -> p (t e)"), SMALLB[:, 0:T * E]).then_inc(z_kept, 1)
                            dve.wait_ge(ln_ready[3], 1)
                            dve.wait_ge(z_kept, a + 1)
                            ahead(dve, z_pgate, a)
                            for t in range(T):
                                dve.max(top[:, t, :], logits[:, t, :]).then_inc(z_ranked, 1)
                            dve.wait_ge(z_ranked, T * (a + 1))
                            dve.tensor_tensor(lead[:, :], top[:, :, 0], top[:, :, 1], ALU.subtract).then_inc(z_lead, 1)
                            for t in range(T):
                                last = dve.max_index(top_at[:, t, :], top[:, t, :], logits[:, t, :])
                            last.then_inc(z_top, 1)
                            dve.wait_ge(z_top, a + 1)
                            ahead(dve, z_picked, a)
                            dve.tensor_copy(two_at[:, :, :], top_at[:, :, 0:2]).then_inc(z_at, 1)

                        def route(a, par):
                            dve.wait_ge(z_tanh, a + 1)
                            ahead(dve, z_pgate, a)
                            dve.tensor_scalar(two_gates[:, :, 0], tanh_lead[:, :], half_gain[:, 3:4], half_gain[:, 3:4],
                                              ALU.mult, ALU.add)
                            dve.tensor_scalar(two_gates[:, :, 1], tanh_lead[:, :], minus_half_gain[:, 3:4], half_gain[:, 3:4],
                                              ALU.mult, ALU.add).then_inc(z_two, 1)
                            dve.wait_ge(z_at, a + 1)
                            dve.tensor_tensor(picked[:, :, :, :],
                                              experts[:, :].unsqueeze(1).unsqueeze(1).broadcast_to([P, T, 2, E]),
                                              two_at[:, :, :].unsqueeze(3).broadcast_to([P, T, 2, E]), ALU.is_equal)\
                               .then_inc(z_picked, 1)
                            dve.wait_ge(z_two, a + 1)
                            dve.wait_ge(z_picked, a + 1)
                            ahead(dve, z_gate, a)
                            dve.tensor_tensor(picked_gate[:, :, :, :], picked[:, :, :, :],
                                              two_gates[:, :, :].unsqueeze(3).broadcast_to([P, T, 2, E]), ALU.mult)\
                               .then_inc(z_pgate, 1)
                            dve.wait_ge(z_pgate, a + 1)
                            ahead(dve, acc_done, T * E * (a - 1))
                            dve.tensor_tensor(gate[:, par, :, :], picked_gate[:, :, 0, :], picked_gate[:, :, 1, :], ALU.add)\
                               .then_inc(z_gate, 1)

                        def begin(a, par, stores):
                            dve.wait_ge(z_b2, a + 1)
                            ahead(dve, set_stored[par], stores)
                            dve.tensor_tensor(acc[:, par, :, :].rearrange("p t d -> p (t d)"), SMALLB[:, :],
                                              xs[:, bass.ds(T * a, T), :].rearrange("p t d -> p (t d)"), ALU.add)\
                               .then_inc(z_start, 1)

                        def gated(s, e):
                            for c in range(C):
                                v = E * C * s + C * e + c
                                dve.wait_ge(h3_done, v + 1)
                                dve.wait_ge(silu_done, v + 1)
                                ahead(dve, g_lo, v - 1)
                                dve.scalar_tensor_tensor(out=g32[:, c, :], in0=H3B[c][:, :],
                                                         scalar=b3_col[:, C * e + c:C * e + c + 1], in1=silu[:, c, :],
                                                         op0=ALU.add, op1=ALU.mult).then_inc(g_done, 1)

                        def accumulate(s, par, e):
                            u = E * s + e
                            dve.wait_ge(y_done, u + 1)
                            dve.wait_ge(z_start, s + 1)
                            ahead(dve, acc_done, T * u)
                            for t in range(T):
                                dve.scalar_tensor_tensor(out=acc[:, par, t, :], in0=YB[e % 2][:, t * P:(t + 1) * P],
                                                         scalar=gate[:, par, t, e:e + 1], in1=acc[:, par, t, :],
                                                         op0=ALU.mult, op1=ALU.add).then_inc(acc_done, 1)

                        def step(s, par, stores=0, first=False, last=False):
                            for e in range(E):
                                gated(s, e)
                                if e > 0:
                                    accumulate(s, par, e - 1)
                                elif not first:
                                    accumulate(s - 1, 1 - par, E - 1)
                                if not last:
                                    if e == 0:
                                        normalize(s + 1)
                                    if e == 2:
                                        lo_turned(s + 1, 1 - par)
                                    if e == 3:
                                        rank(s + 1)
                                    if e == 4:
                                        route(s + 1, 1 - par)
                                    if e == 7:
                                        begin(s + 1, 1 - par, stores)

                        layer_norm_moments(dve, 3)
                        dve.wait_ge(ln_ready[3], 1)
                        normalize(0)
                        lo_turned(0, 0)
                        rank(0)
                        route(0, 0)
                        begin(0, 0, 0)
                        step(0, 0, 0, first=True)
                        with dve.Fori(0, S_PAIRS) as i:
                            step(2 * i + 1, 1, 16 * i + 16)
                            step(2 * i + 2, 0, 16 * i + 16)
                        step(SETS - 1, 1, last=True)
                        accumulate(SETS - 1, 1, E - 1)

                    @block.tensor
                    def _(pe):
                        def turn(a):
                            pe.wait_ge(z_norm, a + 1)
                            ahead(pe, z_lo, a)
                            for t in range(T):
                                last = pe.transpose(TURNB[:, t * P:(t + 1) * P], zn[:, t, :], ident[:, :])
                            last.then_inc(z_turn, 1)

                        def score_experts(a, par):
                            pe.wait_ge(z_lo, a + 1)
                            ahead(pe, z_start, a)
                            for t in range(T):
                                last = product(pe, SMALLB[:, t * E:(t + 1) * E],
                                               [zT[:, par, w, t * P:(t + 1) * P] for w in range(2)],
                                               [router[:, w, :] for w in range(2)])
                            last.then_inc(z_logits, 1)

                        def turn_gates(a, par):
                            pe.wait_ge(z_gate, a + 1)
                            for t in range(T):
                                last = pe.transpose(SMALLB[0:E, t * P:(t + 1) * P], gate[:, par, t, :], ident[:, :])
                            last.then_inc(z_gturn, 1)

                        def gates_b2(a):
                            pe.wait_ge(z_gateT, a + 1)
                            for t in range(T):
                                last = pe.matmul(SMALLB[:, t * P:(t + 1) * P], gateT[:, t * P:(t + 1) * P], b2_row[:, :],
                                                 start=True, stop=True)
                            last.then_inc(z_b2, 1)

                        def hidden(s, par, e):
                            for c in range(C):
                                v = E * C * s + C * e + c
                                z = [zT[:, par, w, :] for w in range(2)]
                                if c == 0 and e == 0:
                                    pe.wait_ge(z_lo, s + 1)
                                ahead(pe, silu_done, v - 1)
                                product(pe, H1B[c][:, :], [up1[:, w, C * e + c, :] for w in range(2)], z).then_inc(h1_done, 1)
                                ahead(pe, g_done, v - 1)
                                product(pe, H3B[c][:, :], [up3[:, w, C * e + c, :] for w in range(2)], z).then_inc(h3_done, 1)

                        def down_project(s, e):
                            u = E * s + e
                            pe.wait_ge(g_lo, C * (u + 1))
                            ahead(pe, acc_done, T * (u - 1))
                            for c in range(C):
                                for t in range(T):
                                    last = product(pe, YB[e % 2][:, t * P:(t + 1) * P],
                                                   [g_s[:, e % 2, c, w, t * P:(t + 1) * P] for w in range(2)],
                                                   [down[:, w, C * e + c, :] for w in range(2)],
                                                   start=(c == 0 and t == 0), stop=(c == C - 1 and t == T - 1))
                            last.then_inc(y_done, 1)

                        def step(s, par, first=False, last=False):
                            for e in range(E):
                                hidden(s, par, e)
                                if e > 0:
                                    down_project(s, e - 1)
                                elif not first:
                                    down_project(s - 1, E - 1)
                                if not last:
                                    if e == 1:
                                        turn(s + 1)
                                    if e == 3:
                                        score_experts(s + 1, 1 - par)
                                    if e == 5:
                                        turn_gates(s + 1, 1 - par)
                                    if e == 6:
                                        gates_b2(s + 1)

                        turn(0)
                        score_experts(0, 0)
                        turn_gates(0, 0)
                        gates_b2(0)
                        step(0, 0, first=True)
                        with pe.Fori(0, S_PAIRS) as i:
                            step(2 * i + 1, 1)
                            step(2 * i + 2, 0)
                        step(SETS - 1, 1, last=True)
                        down_project(SETS - 1, E - 1)


        if stages < 4:
            with nc.Block() as block:
                stored = sem("stored")

                @block.sync
                def _(sp):
                    sp.dma_start(out.rearrange("b s d -> s b d"), xs[:, :, :]).then_inc(stored, 16)
                    sp.wait_ge(stored, 16)


_INS = ["x", "ctx_1024", "mask_BxSxS2_if1", "g_xattn", "g_ffn",
        "L0_xattn_w_q", "L0_xattn_w_k", "L0_xattn_w_v", "L0_xattn_w_o",
        "L0_ffn_W_r", "L0_ffn_W_k", "L0_ffn_W_v", "L0_ffn_mu_r", "L0_ffn_mu_k",
        "L1_xattn_Wq", "L1_xattn_bq", "L1_xattn_Wk", "L1_xattn_bk", "L1_xattn_Wv", "L1_xattn_bv",
        "L1_xattn_Wo", "L1_xattn_bo", "L1_ffn_Wg", "L1_ffn_W1", "L1_ffn_b1", "L1_ffn_A1", "L1_ffn_B1",
        "L1_ffn_W2", "L1_ffn_b2", "L1_ffn_A2", "L1_ffn_B2", "L1_ffn_W3", "L1_ffn_b3", "L1_ffn_A3",
        "L1_ffn_B3"]


def kernel(**inputs):
    import numpy as np
    import concourse.bacc as bacc
    from concourse.bass_utils import run_bass_kernel_spmd

    nc = bacc.Bacc("TRN2", target_bir_lowering=False, num_devices=1)
    arrays, args = {}, []
    for name in _INS:
        a = np.ascontiguousarray(inputs[name])
        arrays[name] = a
        args.append(nc.dram_tensor(name, a.shape, mybir.dt.from_np(a.dtype), kind="ExternalInput").ap())
    args.append(nc.dram_tensor("x_out", arrays["x"].shape, F32, kind="ExternalOutput").ap())
    gated_layers(nc, *args)
    result = run_bass_kernel_spmd(nc, [arrays], core_ids=[0])
    return result.results[0]["x_out"]
```

```python
from contextlib import ExitStack

import concourse.bass as bass
from concourse import mybir

F32 = mybir.dt.float32
F16 = mybir.dt.float16
BF16 = mybir.dt.bfloat16
I32 = mybir.dt.int32
U32 = mybir.dt.uint32
ALU = mybir.AluOpType
ACT = mybir.ActivationFunctionType
AX = mybir.AxisListType

P = 128
EPS = 1e-5
H = 16
D0 = 64
D1 = 8
HG = 4
G = H // HG
E = 8
C = 2
R = 16
TILES = 4
BIG = 1e30


def gated_layers(nc, x, ctx, mask, g_xattn, g_ffn, wq0, wk0, wv0, wo0, w_r, w_k, w_v, mu_r, mu_k,
                 wq1, bq1, wk1, bk1, wv1, bv1, wo1, bo1, wg, w1, b1, a1, bb1, w2, b2, a2, bb2,
                 w3, b3, a3, bb3, out):
    B = x.shape[0]
    with ExitStack() as whole:
        def sb(name, shape, dt=F32, to=whole):
            return to.enter_context(nc.sbuf_tensor(name, shape, dt))

        def sem(name):
            return whole.enter_context(nc.semaphore(name))

        bank = [whole.enter_context(nc.psum_tensor(f"bank{i}", [P, 512], F32)) for i in range(8)]

        xs = sb("xs", [P, B, P])
        stat = sb("stat", [P, B, 6])
        mean = sb("mean", [P, B])
        spread = sb("spread", [P, B])
        var = sb("var", [P, B])
        rstd = sb("rstd", [P, B])
        spread_sq = sb("spread_sq", [P, B])
        total_var = sb("total_var", [P, B])
        minus_half = sb("minus_half", [P, B])
        half = sb("half", [P, B])
        one_in_p = sb("one_in_p", [P, B])
        eps = sb("eps", [P, B])
        ident = sb("ident", [P, P])
        ident4 = sb("ident4", [P, HG, P], BF16)
        minus_one_at = sb("minus_one_at", [P, H, P], BF16)
        slot_of = sb("slot_of", [P, HG])
        experts = sb("experts", [P, E])
        ones16 = sb("ones16", [1, P], F16)
        gain = sb("gain", [P, 4])
        half_gain = sb("half_gain", [P, 4])
        minus_half_gain = sb("minus_half_gain", [P, 4])
        NCOL = 2 * E * C + 5
        cols = sb("cols", [P, NCOL])
        b1_col, b3_col = cols[:, 0:E * C], cols[:, E * C:2 * E * C]
        bq_col, bk_col, bv_col = (cols[:, 2 * E * C + i:2 * E * C + i + 1] for i in range(3))
        mu = cols[:, NCOL - 2:NCOL]
        b2_row = sb("b2_row", [E, P])
        qk0 = sb("qk0", [P, 2, H, P], F16)
        v0 = sb("v0", [P, 2, H * D0], F16)
        o0 = sb("o0", [P, 2, G * 2, P], F16)
        mix = sb("mix", [P, 2, 5, P], F16)
        att1 = sb("att1", [P, 2, 4, P], F16)
        bias1 = sb("bias1", [1, 2, P], F16)
        router = sb("router", [P, 2, E], F16)
        up1 = sb("up1", [P, 2, E * C, P], F16)
        up3 = sb("up3", [P, 2, E * C, P], F16)
        down = sb("down", [P, 2, E * C, P], F16)

        ctx_in = sb("ctx_in", [P, 2, P])
        ctx1 = sb("ctx1", [P, 2, P])

        ctx_loaded = [sem(f"ctx_loaded{i}") for i in range(2)]
        c_loaded = [sem(f"c_loaded{i}") for i in range(2)]
        x_loaded = sem("x_loaded")
        masks_loaded = sem("masks_loaded")
        stats_ready = sem("stats_ready")
        ln_ready = [sem(f"ln_ready{i}") for i in range(4)]

        def load_ctx(sp, to, c, par, loaded):
            sp.dma_start(to[:, par:par + 1, :],
                         ctx[bass.ds(c, 1), :, :].rearrange("a s d -> s a d")).then_inc(loaded[par], 16)

        def product(pe, to, left, right, start=True, stop=True):
            pe.matmul(to, left[0], right[0], start=start, stop=False)
            pe.matmul(to, left[0], right[1], start=False, stop=False)
            return pe.matmul(to, left[1], right[0], start=False, stop=stop)

        def ahead(eng, semaphore, n):
            if not isinstance(n, int) or n > 0:
                eng.wait_ge(semaphore, n)

        sums_ready, scaled_ready, parts_ready, var_ready = (
            [sem(f"{step}{i}") for i in range(4)]
            for step in ("sums_ready", "scaled_ready", "parts_ready", "var_ready"))

        def wait_beside(pool, semaphore, n):
            pool.wait_ge(const_step, 1)
            pool.wait_ge(semaphore, n)

        def layer_norm_moments(pool, n, k, first, count):
            at = bass.ds(first, count)
            even, odd = (stat[:, at, 3 * i + 1] for i in range(2))
            const = slice(0, count)
            pool.tensor_tensor(mean[:, at], even, odd, ALU.add)
            pool.tensor_tensor(spread[:, at], even, odd, ALU.subtract)
            pool.tensor_tensor(var[:, at], stat[:, at, 2], stat[:, at, 5], ALU.add).then_inc(sums_ready[n], 1)
            wait_beside(pool, sums_ready[n], k + 1)
            pool.tensor_tensor(mean[:, at], mean[:, at], half[:, const], ALU.mult)
            pool.tensor_tensor(spread[:, at], spread[:, at], half[:, const], ALU.mult)
            pool.tensor_tensor(var[:, at], var[:, at], one_in_p[:, const], ALU.mult).then_inc(scaled_ready[n], 1)
            wait_beside(pool, scaled_ready[n], k + 1)
            pool.tensor_tensor(spread_sq[:, at], spread[:, at], spread[:, at], ALU.mult)
            pool.tensor_tensor(var[:, at], var[:, at], eps[:, const], ALU.add).then_inc(parts_ready[n], 1)

        def layer_norm_scale(pool, n, k, first, count):
            at = bass.ds(first, count)
            wait_beside(pool, parts_ready[n], k + 1)
            pool.tensor_tensor(total_var[:, at], spread_sq[:, at], var[:, at], ALU.add).then_inc(var_ready[n], 1)
            wait_beside(pool, var_ready[n], k + 1)
            pool.tensor_tensor(rstd[:, at], total_var[:, at], minus_half[:, 0:count], ALU.pow).then_inc(ln_ready[n], 1)

        def layer_norm(pool, n, k, first, count):
            layer_norm_moments(pool, n, k, first, count)
            layer_norm_scale(pool, n, k, first, count)

        with ExitStack() as prep:
            def stage_sb(name, shape, dt=F32):
                return sb(name, shape, dt, prep)

            wq0_s = stage_sb("wq0_s", [P, H * D0])
            wk0_s = stage_sb("wk0_s", [P, H * D0])
            wv0_s = stage_sb("wv0_s", [P, H * D0])
            wo0_s = stage_sb("wo0_s", [P, G * 2, P])
            qT = stage_sb("qT", [P, G * 2, P])
            kT = stage_sb("kT", [P, G * 2, P])
            mix_s = stage_sb("mix_s", [P, 3, P])
            mix_T = stage_sb("mix_T", [P, 3 * P + E])
            rows_s = stage_sb("rows_s", [NCOL, P])
            one_minus_mu = stage_sb("one_minus_mu", [P, 2])
            att1_s = stage_sb("att1_s", [P, 4, P])
            bo_row = stage_sb("bo_row", [1, P])
            bias1_s = stage_sb("bias1_s", [1, 2, P])
            wg_s = stage_sb("wg_s", [E, P])
            gains_in = stage_sb("gains_in", [P, 4])
            w1_s = stage_sb("w1_s", [P, E * C, P])
            w3_s = stage_sb("w3_s", [P, E * C, P])
            w2_s = stage_sb("w2_s", [P, E, C * P])
            a1_s = stage_sb("a1_s", [R, E, P])
            a3_s = stage_sb("a3_s", [R, E, P])
            a2_s = stage_sb("a2_s", [R, E, C * P])
            bb1_s = stage_sb("bb1_s", [P, E * C, R])
            bb3_s = stage_sb("bb3_s", [P, E * C, R])
            bb2_s = stage_sb("bb2_s", [P, E, R])
            bb1_T = stage_sb("bb1_T", [P, 2, E * C, P], F16)
            bb3_T = stage_sb("bb3_T", [P, 2, E * C, P], F16)
            bb2_T = stage_sb("bb2_T", [P, 2, E, P], F16)
            a1_p = stage_sb("a1_p", [P, 2, E, P], F16)
            a3_p = stage_sb("a3_p", [P, 2, E, P], F16)
            a2_p = stage_sb("a2_p", [P, 2, E, C * P], F16)
            w1_p = stage_sb("w1_p", [P, 2, E * C, P], F16)
            w3_p = stage_sb("w3_p", [P, 2, E * C, P], F16)
            w2_p = stage_sb("w2_p", [P, 2, E, C * P], F16)
            ident16 = stage_sb("ident16", [P, P], F16)

            qk_loaded = sem("qk_loaded")
            vo_loaded = sem("vo_loaded")
            small_loaded = sem("small_loaded")
            mats_loaded = sem("mats_loaded")
            lora_loaded = sem("lora_loaded")
            up_loaded = sem("up_loaded")
            SMALL, MATS, LORA, UP = 12 * 16, 7 * 16, 6 * 16, 3 * 16
            ident_ready = sem("ident_ready")
            const_step = sem("const_step")
            filled = sem("filled")
            taken_hi = sem("taken_hi")
            taken_lo = sem("taken_lo")
            padded = sem("padded")
            w_hi = sem("w_hi")
            a_hi = sem("a_hi")
            a_lo = sem("a_lo")
            w_lo = sem("w_lo")
            gain_ready = sem("gain_ready")
            scales_ready = sem("scales_ready")
            raw_hi = sem("raw_hi")
            gained_hi = sem("gained_hi")
            prep_end = sem("prep_end")
            bias_done = sem("bias_done")
            bias_step = sem("bias_step")

            def flat(t):
                return t.rearrange("p c d -> p (c d)")

            def turns():
                for src, dst in ((wq0_s, qT), (wk0_s, kT)):
                    for half_ in range(2):
                        cs = range(4 * half_, 4 * half_ + 4)
                        yield [src[:, c * P:(c + 1) * P] for c in cs], flat(dst[:, 4 * half_:4 * half_ + 4, :])
                for src, dst, n in ((bb1_s, bb1_T, E * C), (bb3_s, bb3_T, E * C), (bb2_s, bb2_T, E)):
                    for q in range(n // 4):
                        yield ([src[:, c, :] for c in range(4 * q, 4 * q + 4)],
                               [flat(dst[0:R, w, 4 * q:4 * q + 4, :]) for w in range(2)])
                yield ([mix_s[:, c, :] for c in range(3)] + [wg_s[:, :]], mix_T[:, :])
                yield [rows_s[:, :]], cols[:, :]

            TURNS = list(turns())
            NT = len(TURNS)
            A_SPLITS = [(p[0:R], a[:, :, :]) for p, a in ((a1_p, a1_s), (a3_p, a3_s), (a2_p, a2_s))]
            W_SPLITS = [(p, w[:, :, :]) for p, w in ((w1_p, w1_s), (w3_p, w3_s), (w2_p, w2_s))]
            FOLDS = G + 3 * (E * C // 4)

            def fold_target(n, part):
                if n < G:
                    first = 2 * HG * (n // 2) + n % 2
                    return qk0[:, part, first:first + 2 * HG - 1:2, :]
                which, q = divmod(n - G, E * C // 4)
                return (up1, up3, down)[which][:, part, 4 * q:4 * q + 4, :]

            MID = G + 2
            JOBS = ([("turn", n) for n in range(G)] + [("fold", n) for n in range(G)]
                    + [("turn", n) for n in range(G, NT - 2)] + [("fold", n) for n in range(G, MID)]
                    + [("turn", NT - 2), ("turn", NT - 1)] + [("fold", n) for n in range(MID, FOLDS)])
            PLACE = {job: at for at, job in enumerate(JOBS)}

            def has_lo(job):
                return job[0] == "fold" or isinstance(TURNS[job[1]][1], list)

            LO_BEFORE = [sum(map(has_lo, JOBS[:at])) for at in range(len(JOBS) + 1)]

            def parts(job):
                place = bank[PLACE[job] % 8]
                if job[0] == "fold":
                    return [fold_target(job[1], w) for w in range(2)], place[:, :].rearrange("p (c d) -> p c d", d=P)
                dst = TURNS[job[1]][1]
                dst = dst if isinstance(dst, list) else [dst]
                return dst, place[0:dst[0].shape[0], 0:dst[0].shape[1]]

            heads = stage_sb("heads", [P, H])
            block = prep.enter_context(nc.Block())

            @block.sync
            def _(sp):
                sp.dma_start(wq0_s[:, :], wq0).then_inc(qk_loaded, 16)
                sp.dma_start(wk0_s[:, :], wk0).then_inc(qk_loaded, 16)
                sp.dma_start(bb1_s[:, :, :], bb1.rearrange("e (c p) r -> p (e c) r", p=P)).then_inc(lora_loaded, 16)
                sp.dma_start(bb3_s[:, :, :], bb3.rearrange("e (c p) r -> p (e c) r", p=P)).then_inc(lora_loaded, 16)
                sp.dma_start(bb2_s[:, :, :], bb2.rearrange("e d r -> d e r")).then_inc(lora_loaded, 16)
                sp.dma_start(a1_s[:, :, :], a1.rearrange("e r d -> r e d")).then_inc(lora_loaded, 16)
                sp.dma_start(a3_s[:, :, :], a3.rearrange("e r d -> r e d")).then_inc(lora_loaded, 16)
                sp.dma_start(a2_s[:, :, :], a2.rearrange("e r h -> r e h")).then_inc(lora_loaded, 16)
                sp.dma_start(w1_s[:, :, :], w1.rearrange("e (c p) d -> p (e c) d", p=P)).then_inc(up_loaded, 16)
                sp.dma_start(w3_s[:, :, :], w3.rearrange("e (c p) d -> p (e c) d", p=P)).then_inc(up_loaded, 16)
                sp.dma_start(w2_s[:, :, :], w2.rearrange("e d h -> d e h")).then_inc(up_loaded, 16)
                sp.dma_start(xs[:, :, :], x.rearrange("b s d -> s b d")).then_inc(x_loaded, 16)
                sp.dma_start(wg_s[:, :], wg).then_inc(small_loaded, 16)
                for i, v in enumerate((g_xattn, g_ffn)):
                    sp.dma_start(gains_in[:, 2 * i:2 * i + 2], v.rearrange("(a n) -> a n", a=1).broadcast_to([P, 2]))\
                      .then_inc(small_loaded, 16)
                for i, v in enumerate((b1, b3)):
                    sp.dma_start(rows_s[E * C * i:E * C * (i + 1), :], v.rearrange("e (c p) -> (e c) p", p=P))\
                      .then_inc(small_loaded, 16)
                for i, v in enumerate((bq1, bk1, bv1, mu_r, mu_k)):
                    sp.dma_start(rows_s[2 * E * C + i:2 * E * C + i + 1, :], v.rearrange("(a n) -> a n", a=1))\
                      .then_inc(small_loaded, 16)
                for i, w in enumerate((wq1, wk1, wv1, wo1)):
                    sp.dma_start(att1_s[:, i, :], w).then_inc(mats_loaded, 16)
                sp.dma_start(bo_row[:, :], bo1.rearrange("(a n) -> a n", a=1)).then_inc(small_loaded, 16)
                sp.dma_start(b2_row[:, :], b2).then_inc(small_loaded, 16)
                for c in range(2):
                    load_ctx(sp, ctx_in, c, c, ctx_loaded)
                for c in range(2):
                    load_ctx(sp, ctx1, c, c, c_loaded)

            @block.scalar
            def _(act):
                for i, w in enumerate((w_r, w_k, w_v)):
                    act.dma_start(mix_s[:, i, :], w).then_inc(mats_loaded, 16)
                act.dma_start(wv0_s[:, :], wv0).then_inc(vo_loaded, 16)
                act.dma_start(wo0_s[:, :, :], wo0.rearrange("(c p) d -> p c d", p=P)).then_inc(vo_loaded, 16)
                def take_hi(job):
                    act.wait_ge(filled, PLACE[job] + 1)
                    to, src = parts(job)
                    act.activation(to[0], src, ACT.Copy).then_inc(taken_hi, 1)

                for n in range(G):
                    take_hi(("turn", n))
                for n in range(G):
                    take_hi(("fold", n))
                act.wait_ge(padded, 1)
                for n in range(G, NT - 2):
                    take_hi(("turn", n))
                act.wait_ge(lora_loaded, LORA)
                act.wait_ge(up_loaded, UP)
                for pair_, src in W_SPLITS[:1]:
                    act.activation(pair_[:, 0], src, ACT.Copy).then_inc(w_hi, 1)
                for pair_, src in A_SPLITS:
                    act.activation(pair_[:, 0], src, ACT.Copy).then_inc(a_hi, 1)
                for pair_, src in W_SPLITS[1:]:
                    act.activation(pair_[:, 0], src, ACT.Copy).then_inc(w_hi, 1)
                for n in range(G, MID):
                    take_hi(("fold", n))
                act.wait_ge(vo_loaded, 32)
                act.activation(v0[:, 0, :], wv0_s[:, :], ACT.Copy).then_inc(raw_hi, 1)
                take_hi(("turn", NT - 2))
                take_hi(("turn", NT - 1))
                act.wait_ge(small_loaded, SMALL)
                act.activation(gain[:, :], gains_in[:, :], ACT.Tanh).then_inc(gain_ready, 1)
                act.wait_ge(mats_loaded, MATS)
                act.activation(att1[:, 0, 0:3, :], att1_s[:, 0:3, :], ACT.Copy).then_inc(raw_hi, 1)
                act.wait_ge(taken_hi, PLACE["turn", NT - 1] + 1)
                act.activation(router[:, 0, :], mix_T[:, 3 * P:3 * P + E], ACT.Copy).then_inc(raw_hi, 1)
                for n in range(MID, FOLDS):
                    take_hi(("fold", n))

            @block.gpsimd
            def _(pool):
                pool.memset(ident[:, :], 0.0).then_inc(const_step, 1)
                pool.wait_ge(const_step, 1)
                pool.affine_select(out=ident[:, :], in_=ident[:, :], compare_op=ALU.not_equal, fill=1.0,
                                   base=0, pattern=[[-1, P]], channel_multiplier=1).then_inc(ident_ready, 1)
                pool.memset(minus_half[:, :], -0.5).then_inc(const_step, 1)
                pool.memset(ones16[:, :], 1.0).then_inc(const_step, 1)
                pool.iota(experts[:, :], pattern=[[1, E]], base=0, channel_multiplier=0,
                          allow_small_or_imprecise_dtypes=True).then_inc(const_step, 1)
                pool.memset(minus_one_at[:, :, :], 0.0).then_inc(const_step, 1)
                pool.wait_ge(const_step, 5)
                for n, row in enumerate((0, 32)):
                    pool.wait_ge(const_step, 5 + n)
                    pool.affine_select(out=minus_one_at[:, :, :], in_=minus_one_at[:, :, :],
                                       compare_op=ALU.not_equal, fill=-1.0, base=-row,
                                       pattern=[[-1, H], [0, P]], channel_multiplier=1).then_inc(const_step, 1)
                pool.memset(heads[:, :], 1.0).then_inc(const_step, 1)
                pool.wait_ge(const_step, 8)
                pool.affine_select(out=heads[:, :], in_=heads[:, :], compare_op=ALU.is_ge, fill=0.0,
                                   base=0, pattern=[[-D1, H]], channel_multiplier=1).then_inc(const_step, 1)
                pool.wait_ge(const_step, 9)
                pool.affine_select(out=heads[:, :], in_=heads[:, :], compare_op=ALU.is_ge, fill=0.0,
                                   base=D1 - 1, pattern=[[D1, H]], channel_multiplier=-1).then_inc(const_step, 1)
                for to, value in ((half, 0.5), (one_in_p, 1.0 / P), (eps, EPS)):
                    pool.memset(to[:, :], value).then_inc(const_step, 1)
                pool.wait_ge(const_step, 13)
                for n, (pair_, src) in enumerate(W_SPLITS):
                    pool.wait_ge(w_hi, n + 1)
                    pool.tensor_tensor(pair_[:, 1], src, pair_[:, 0], ALU.subtract).then_inc(w_lo, 1)
                pool.wait_ge(stats_ready, B)
                layer_norm(pool, 0, 0, 0, B)

            @block.vector
            def _(dve):
                dve.wait_ge(ident_ready, 1)
                for i in range(HG):
                    last = dve.tensor_copy(ident4[:, i, :], ident[:, :])
                last.then_inc(prep_end, 1)
                dve.tensor_copy(ident16[:, :], ident[:, :]).then_inc(prep_end, 1)

                def take_lo(job):
                    dve.wait_ge(taken_hi, PLACE[job] + 1)
                    to, src = parts(job)
                    dve.tensor_tensor(to[1], src, to[0], ALU.subtract).then_inc(taken_lo, 1)

                for t in (bb1_T, bb3_T, bb2_T, a1_p, a3_p, a2_p):
                    last = dve.memset(t[:, :, :, :], 0.0)
                last.then_inc(padded, 1)
                for n in range(G):
                    take_lo(("fold", n))
                for n in range(G, NT - 2):
                    take_lo(("turn", n))
                for n, (pair_, src) in enumerate(A_SPLITS):
                    dve.wait_ge(a_hi, n + 1)
                    dve.tensor_tensor(pair_[:, 1], src, pair_[:, 0], ALU.subtract).then_inc(a_lo, 1)
                dve.wait_ge(x_loaded, 16)
                with dve.Fori(0, B // 8) as i:
                    for j in range(8):
                        dve.bn_stats(stat[:, bass.ds(8 * i + j, 1), :], xs[:, bass.ds(8 * i + j, 1), :])\
                           .then_inc(stats_ready, 1)
                for n in range(G, MID):
                    take_lo(("fold", n))
                dve.wait_ge(gain_ready, 1)
                dve.wait_ge(taken_hi, PLACE["turn", NT - 1] + 1)
                dve.tensor_scalar(half_gain[:, :], gain[:, :], 0.5, None, ALU.mult).then_inc(scales_ready, 1)
                dve.tensor_scalar(minus_half_gain[:, :], gain[:, :], -0.5, None, ALU.mult).then_inc(scales_ready, 1)
                dve.tensor_scalar(one_minus_mu[:, :], mu, -1.0, 1.0, ALU.mult, ALU.add).then_inc(scales_ready, 1)
                dve.wait_ge(const_step, 10)
                dve.tensor_reduce(slot_of[:, :], heads[:, :].rearrange("p (j i) -> p i j", i=HG), AX.X, ALU.add)\
                   .then_inc(scales_ready, 1)
                dve.wait_ge(scales_ready, 4)
                dve.wait_ge(vo_loaded, 32)
                dve.wait_ge(mats_loaded, MATS)
                scaled = [(mix[:, :, 0, :], mix_T[:, 0:P], mu[:, 0:1]),
                          (mix[:, :, 1, :], mix_T[:, 0:P], one_minus_mu[:, 0:1]),
                          (mix[:, :, 2, :], mix_T[:, P:2 * P], mu[:, 1:2]),
                          (mix[:, :, 3, :], mix_T[:, P:2 * P], one_minus_mu[:, 1:2]),
                          (mix[:, :, 4, :], mix_T[:, 2 * P:3 * P], half_gain[:, 2:3]),
                          (o0[:, :, :, :].rearrange("p a c d -> p a (c d)"),
                           wo0_s[:, :, :].rearrange("p c d -> p (c d)"), gain[:, 0:1]),
                          (att1[:, :, 3, :], att1_s[:, 3, :], gain[:, 1:2])]
                for n, (to, w, by) in enumerate(scaled):
                    dve.tensor_scalar(to[:, 0], w, by, None, ALU.mult).then_inc(gained_hi, 1)
                for n, (to, w, by) in enumerate(scaled):
                    dve.wait_ge(gained_hi, n + 1)
                    dve.scalar_tensor_tensor(out=to[:, 1], in0=w, scalar=by, in1=to[:, 0],
                                             op0=ALU.mult, op1=ALU.subtract).then_inc(prep_end, 1)
                dve.wait_ge(raw_hi, 3)
                dve.tensor_tensor(v0[:, 1, :], wv0_s[:, :], v0[:, 0, :], ALU.subtract).then_inc(prep_end, 1)
                dve.tensor_tensor(att1[:, 1, 0:3, :], att1_s[:, 0:3, :], att1[:, 0, 0:3, :], ALU.subtract).then_inc(prep_end, 1)
                dve.tensor_tensor(router[:, 1, :], mix_T[:, 3 * P:3 * P + E], router[:, 0, :], ALU.subtract).then_inc(prep_end, 1)
                for n in range(MID, FOLDS):
                    take_lo(("fold", n))
                dve.wait_ge(bias_done, 1)
                dve.tensor_tensor(bias1_s[:, 0, :], bank[len(JOBS) % 8][0:1, 0:P], bo_row[:, :], ALU.add).then_inc(bias_step, 1)
                dve.wait_ge(bias_step, 1)
                dve.tensor_scalar(bias1_s[:, 1, :], bias1_s[:, 0, :], gain[0:1, 1:2], None, ALU.mult).then_inc(bias_step, 1)
                dve.wait_ge(bias_step, 2)
                dve.tensor_copy(bias1[:, 0, :], bias1_s[:, 1, :]).then_inc(bias_step, 1)
                dve.wait_ge(bias_step, 3)
                dve.tensor_tensor(bias1[:, 1, :], bias1_s[:, 1, :], bias1[:, 0, :], ALU.subtract).then_inc(prep_end, 1)
            @block.tensor
            def _(pe):
                pe.wait_ge(ident_ready, 1)

                def turn(n, to):
                    srcs = TURNS[n][0]
                    for i, w in enumerate(srcs):
                        rows, cols_ = w.shape
                        last = pe.transpose(to[0:cols_, i * P:i * P + rows], w, ident[0:rows, 0:rows])
                    last.then_inc(filled, 1)

                def fold(n, to):
                    for i in range(4):
                        where = to[:, i * P:(i + 1) * P]
                        if n < G:
                            h = 2 * HG * (n // 2) + n % 2 + 2 * i
                            rows = slice(D0 * (h % 2), D0 * (h % 2) + D0)
                            last = pe.matmul(where, qT[rows, h // 2, :], kT[rows, h // 2, :], start=True, stop=True)
                            continue
                        which, q = divmod(n - G, E * C // 4)
                        u = 4 * q + i
                        e, c = divmod(u, C)
                        if which == 2:
                            w, a, bT = ([p[:, part, e, c * P:(c + 1) * P] for part in range(2)] for p in (w2_p, a2_p, a2_p))
                            bT = [bb2_T[:, part, e, :] for part in range(2)]
                        else:
                            w_pair, a_pair, b_pair = ((w1_p, a1_p, bb1_T), (w3_p, a3_p, bb3_T))[which]
                            w = [w_pair[:, part, u, :] for part in range(2)]
                            a = [a_pair[:, part, e, :] for part in range(2)]
                            bT = [b_pair[:, part, u, :] for part in range(2)]
                        pe.matmul(where, w[0], ident16[:, :], start=True, stop=False)
                        pe.matmul(where, w[1], ident16[:, :], start=False, stop=False)
                        last = product(pe, where, a, bT, start=False)
                    last.then_inc(filled, 1)

                pe.wait_ge(qk_loaded, 32)
                for at, (kind, n) in enumerate(JOBS):
                    if at >= 8:
                        pe.wait_ge(taken_hi, at - 7)
                        if LO_BEFORE[at - 7]:
                            pe.wait_ge(taken_lo, LO_BEFORE[at - 7])
                    if (kind, n) == ("turn", G):
                        pe.wait_ge(lora_loaded, LORA)
                    if (kind, n) == ("turn", NT - 2):
                        pe.wait_ge(mats_loaded, MATS)
                        pe.wait_ge(small_loaded, SMALL)
                    if (kind, n) == ("fold", 0):
                        pe.wait_ge(taken_hi, G)
                    if (kind, n) == ("fold", G):
                        pe.wait_ge(prep_end, 2)
                        pe.wait_ge(taken_hi, PLACE["turn", NT - 3] + 1)
                        pe.wait_ge(taken_lo, LO_BEFORE[PLACE["turn", NT - 3] + 1])
                        pe.wait_ge(a_lo, len(A_SPLITS))
                    if kind == "fold" and n >= G and (n - G) % (E * C // 4) == 0:
                        pe.wait_ge(w_lo, (n - G) // (E * C // 4) + 1)
                    (turn if kind == "turn" else fold)(n, bank[at % 8])
                pe.wait_ge(taken_hi, PLACE["turn", NT - 1] + 1)
                pe.wait_ge(taken_lo, LO_BEFORE[len(JOBS) - 7])
                pe.matmul(bank[len(JOBS) % 8][0:1, 0:P], bv_col, att1_s[:, 3, :], start=True, stop=True).then_inc(bias_done, 1)


        masks = sb("masks", [P, B, P], I32)

        with ExitStack() as att:
            def a_sb(name, shape, dt=F32):
                return sb(name, shape, dt, att)

            xn = a_sb("xn", [P, P])
            xcT = a_sb("xcT", [P, 2, 2, 2 * P], F16)
            t_s = a_sb("t_s", [P, 2, 2, H, P], F16)
            v_s = a_sb("v_s", [P, 2, 2, H, D0 + 1], F16)
            peak = a_sb("peak", [P, H])
            peakT = a_sb("peakT", [P, 2, P], BF16)
            prob = a_sb("prob", [P, 2, HG * P])
            prob_hi = a_sb("prob_hi", [P, 2, HG * P], F16)
            prob_lo = a_sb("prob_lo", [P, 2, HG * P], F16)
            inv = a_sb("inv", [P, 2, HG])
            o_s = a_sb("o_s", [P, 2, HG, D0])
            oT = a_sb("oT", [P, 2, G * 2, P], F16)

            blanks_ready = sem("blanks_ready")
            xn_ready = sem("xn_ready")
            turn_done = sem("turn_done")
            turn_hi = sem("turn_hi")
            turn_lo = sem("turn_lo")
            proj_done = sem("proj_done")
            proj_hi = sem("proj_hi")
            proj_lo = sem("proj_lo")
            rough_done = sem("rough_done")
            peak_done = sem("peak_done")
            peak_turned = sem("peak_turned")
            peakT_hi = sem("peakT_hi")
            peakT_lo = sem("peakT_lo")
            score_done = sem("score_done")
            exp_done = sem("exp_done")
            problo_done = sem("problo_done")
            pv_done = sem("pv_done")
            inv_done = sem("inv_done")
            norm_done = sem("norm_done")
            oturn_done = sem("oturn_done")
            oturn_hi = sem("oturn_hi")
            oturn_lo = sem("oturn_lo")
            out_done = sem("out_done")
            res_done = sem("res_done")
            stat_done = sem("stat_done")

            TURN, OUTB, ROUGH, PVB = bank[0], bank[7], bank[3], bank[6]
            QUADS = (B - 4) // 4

            def pair(t, part):
                return [t[:, part, i] for i in range(2)]

            block = att.enter_context(nc.Block())

            @block.sync
            def _(sp):
                def load(c, par):
                    ahead(sp, turn_done, c - 1)
                    load_ctx(sp, ctx_in, c, par, ctx_loaded)
                sp.dma_start(masks[:, :, :], mask.rearrange("b q k -> q b k")).then_inc(masks_loaded, 16)
                with sp.Fori(0, B // 2 - 1) as i:
                    load(2 * i + 2, 0)
                    load(2 * i + 3, 1)

            @block.gpsimd
            def _(pool):
                pool.memset(peakT[:, :, :], 0.0).then_inc(blanks_ready, 1)
                pool.memset(v_s[:, :, 0, :, D0:D0 + 1], 1.0).then_inc(blanks_ready, 1)
                pool.memset(v_s[:, :, 1, :, D0:D0 + 1], 0.0).then_inc(blanks_ready, 1)

                def group(n, par):
                    pool.wait_ge(exp_done, n + 1)
                    ahead(pool, pv_done, n - 1)
                    pool.tensor_tensor(prob_lo[:, par, :], prob[:, par, :], prob_hi[:, par, :],
                                       ALU.subtract).then_inc(problo_done, 1)
                for n in range(G):
                    group(n, n % 2)
                with pool.Fori(1, B) as b:
                    for g in range(G):
                        group(G * b + g, g % 2)
                    wait_beside(pool, stat_done, b)
                    layer_norm(pool, 1, b - 1, b - 1, 1)
                pool.wait_ge(stat_done, B)
                layer_norm(pool, 1, B - 1, B - 1, 1)

            @block.scalar
            def _(act):
                def hi_turned(a, par):
                    act.wait_ge(turn_done, a + 1)
                    act.activation(xcT[:, par, 0, :], TURN[:, 0:2 * P], ACT.Copy).then_inc(turn_hi, 1)

                def hi_peak(a, par):
                    act.wait_ge(peak_turned, a + 1)
                    act.activation(peakT[0:H, par, :], TURN[0:H, 0:P], ACT.Copy).then_inc(peakT_hi, 1)

                def hi_t(a, par, g):
                    act.wait_ge(proj_done, 6 * a + g + 1)
                    act.activation(t_s[:, par, 0, HG * g:HG * g + HG, :].rearrange("p h q -> p (h q)"),
                                   bank[1 + g % 2][:, :], ACT.Copy).then_inc(proj_hi, 1)

                def hi_v(a, par, j):
                    act.wait_ge(proj_done, 6 * a + G + j + 1)
                    act.activation(v_s[:, par, 0, 8 * j:8 * j + 8, 0:D0],
                                   bank[1 + j][:, :].rearrange("p (h d) -> p h d", d=D0), ACT.Copy).then_inc(proj_hi, 1)

                def exps(b, g):
                    n = G * b + g
                    act.wait_ge(score_done, n + 1)
                    ahead(act, problo_done, n - 1)
                    ahead(act, pv_done, n - 1)
                    act.activation(prob[:, g % 2, :], bank[4 + g % 2][:, :], ACT.Exp, scale=float(D0) ** -0.5)
                    act.activation(prob_hi[:, g % 2, :], bank[4 + g % 2][:, :], ACT.Exp, scale=float(D0) ** -0.5)\
                       .then_inc(exp_done, 1)

                def hi_o(b, g):
                    act.wait_ge(oturn_done, G * b + g + 1)
                    act.activation(oT[:, 0, 2 * g:2 * g + 2, :].rearrange("p c q -> p (c q)"),
                                   OUTB[:, 0:2 * P], ACT.Copy).then_inc(oturn_hi, 1)

                def step(b, par, first=False, after=2):
                    a, ap = b + 1, 1 - par
                    if after >= 1:
                        hi_t(a, ap, 0)
                    exps(b, 0)
                    if not first:
                        hi_o(b - 1, 2)
                    if after >= 1:
                        hi_t(a, ap, 1)
                    if not first:
                        hi_o(b - 1, 3)
                    exps(b, 1)
                    if after >= 1:
                        hi_t(a, ap, 2)
                    exps(b, 2)
                    hi_o(b, 0)
                    if after >= 1:
                        hi_t(a, ap, 3)
                    exps(b, 3)
                    if after >= 2:
                        hi_turned(b + 2, par)
                    if after >= 1:
                        hi_v(a, ap, 0)
                    hi_o(b, 1)
                    if after >= 1:
                        hi_peak(a, ap)
                        hi_v(a, ap, 1)

                hi_turned(0, 0)
                for g in range(G):
                    hi_t(0, 0, g)
                act.wait_ge(blanks_ready, 3)
                hi_v(0, 0, 0)
                hi_v(0, 0, 1)
                hi_turned(1, 1)
                hi_peak(0, 0)
                step(0, 0, first=True)
                with act.Fori(0, QUADS) as i:
                    for j in range(1, 5):
                        step(4 * i + j, j % 2)
                step(B - 3, 1)
                step(B - 2, 0, after=1)
                step(B - 1, 1, after=0)
                hi_o(B - 1, 2)
                hi_o(B - 1, 3)

            @block.vector
            def _(dve):
                def normalize(a):
                    ahead(dve, turn_done, a)
                    dve.tensor_scalar(xn[:, :], xs[:, bass.ds(a, 1), :].rearrange("p a d -> p (a d)"),
                                      mean[:, bass.ds(a, 1)],
                                      rstd[:, bass.ds(a, 1)], ALU.subtract, ALU.mult).then_inc(xn_ready, 1)

                def lo_turned(a, par):
                    dve.wait_ge(turn_hi, a + 1)
                    dve.tensor_tensor(xcT[:, par, 1, :], TURN[:, 0:2 * P], xcT[:, par, 0, :], ALU.subtract)\
                       .then_inc(turn_lo, 1)

                def lo_peak(a, par):
                    dve.wait_ge(peakT_hi, a + 1)
                    dve.tensor_tensor(peakT[32:32 + H, par, :], TURN[0:H, 0:P], peakT[0:H, par, :], ALU.subtract)\
                       .then_inc(peakT_lo, 1)

                def lo_t(a, par, g):
                    dve.wait_ge(proj_hi, 6 * a + g + 1)
                    hs = slice(HG * g, HG * g + HG)
                    dve.tensor_tensor(t_s[:, par, 1, hs, :].rearrange("p h q -> p (h q)"), bank[1 + g % 2][:, :],
                                      t_s[:, par, 0, hs, :].rearrange("p h q -> p (h q)"), ALU.subtract)\
                       .then_inc(proj_lo, 1)

                def lo_v(a, par, j):
                    dve.wait_ge(proj_hi, 6 * a + G + j + 1)
                    hs = slice(8 * j, 8 * j + 8)
                    dve.tensor_tensor(v_s[:, par, 1, hs, 0:D0], bank[1 + j][:, :].rearrange("p (h d) -> p h d", d=D0),
                                      v_s[:, par, 0, hs, 0:D0], ALU.subtract).then_inc(proj_lo, 1)

                def maxima(a, g):
                    dve.wait_ge(rough_done, G * a + g + 1)
                    dve.tensor_reduce(peak[:, HG * g:HG * g + HG], ROUGH[:, :].rearrange("p (h k) -> p h k", k=P),
                                      AX.X, ALU.max).then_inc(peak_done, 1)

                def norm(b, g):
                    n = G * b + g
                    dve.wait_ge(pv_done, n + 1)
                    o = PVB[:, 0:HG * (D0 + 1)].rearrange("p (h d) -> p h d", d=D0 + 1)
                    dve.reciprocal(inv[:, g % 2, :], o[:, :, D0]).then_inc(inv_done, 1)
                    dve.wait_ge(inv_done, n + 1)
                    ahead(dve, oturn_done, n - 1)
                    dve.tensor_tensor(o_s[:, g % 2, :, :], o[:, :, 0:D0],
                                      inv[:, g % 2, :].unsqueeze(2).broadcast_to([P, HG, D0]), ALU.mult)\
                       .then_inc(norm_done, 1)

                def lo_o(b, g):
                    dve.wait_ge(oturn_hi, G * b + g + 1)
                    cs = slice(2 * g, 2 * g + 2)
                    dve.tensor_tensor(oT[:, 1, cs, :].rearrange("p c q -> p (c q)"), OUTB[:, 0:2 * P],
                                      oT[:, 0, cs, :].rearrange("p c q -> p (c q)"), ALU.subtract).then_inc(oturn_lo, 1)

                def residual(b):
                    dve.wait_ge(out_done, b + 1)
                    here = xs[:, bass.ds(b, 1), :].rearrange("p a d -> p (a d)")
                    dve.tensor_tensor(here, OUTB[:, 0:P], here, ALU.add).then_inc(res_done, 1)

                def statistics(b):
                    dve.wait_ge(res_done, b + 1)
                    dve.bn_stats(stat[:, bass.ds(b, 1), :], xs[:, bass.ds(b, 1), :]).then_inc(stat_done, 1)

                def step(b, par, first=False, after=2):
                    a, ap = b + 1, 1 - par
                    if after >= 2:
                        normalize(b + 2)
                    if after >= 1:
                        lo_t(a, ap, 0)
                    if not first:
                        norm(b - 1, 3)
                        lo_o(b - 1, 2)
                    if after >= 1:
                        maxima(a, 0)
                    if not first:
                        lo_o(b - 1, 3)
                    if after >= 1:
                        lo_t(a, ap, 1)
                    if after >= 1:
                        maxima(a, 1)
                    norm(b, 0)
                    if not first:
                        residual(b - 1)
                        statistics(b - 1)
                    if after >= 1:
                        lo_t(a, ap, 2)
                    norm(b, 1)
                    if after >= 1:
                        maxima(a, 2)
                    lo_o(b, 0)
                    if after >= 1:
                        lo_t(a, ap, 3)
                        maxima(a, 3)
                    if after >= 2:
                        lo_turned(b + 2, par)
                    if after >= 1:
                        lo_v(a, ap, 0)
                    lo_o(b, 1)
                    norm(b, 2)
                    if after >= 1:
                        lo_peak(a, ap)
                        lo_v(a, ap, 1)

                normalize(0)
                lo_turned(0, 0)
                normalize(1)
                for g in range(G):
                    lo_t(0, 0, g)
                dve.wait_ge(blanks_ready, 3)
                lo_v(0, 0, 0)
                lo_v(0, 0, 1)
                lo_turned(1, 1)
                for g in range(G):
                    maxima(0, g)
                lo_peak(0, 0)
                step(0, 0, first=True)
                with dve.Fori(0, QUADS) as i:
                    for j in range(1, 5):
                        step(4 * i + j, j % 2)
                step(B - 3, 1)
                step(B - 2, 0, after=1)
                step(B - 1, 1, after=0)
                norm(B - 1, 3)
                lo_o(B - 1, 2)
                lo_o(B - 1, 3)
                residual(B - 1)
                statistics(B - 1)

            @block.tensor
            def _(pe):
                def turn(a, par, ctx_count):
                    pe.wait_ge(xn_ready, a + 1)
                    pe.wait_ge(ctx_loaded[par], ctx_count)
                    ahead(pe, peakT_lo, a - 1)
                    pe.transpose(TURN[:, 0:P], xn[:, :], ident[:, :])
                    pe.transpose(TURN[:, P:2 * P], ctx_in[:, par, :], ident[:, :]).then_inc(turn_done, 1)

                def project_t(a, par, g):
                    ahead(pe, proj_lo, 6 * a + g - 1)
                    if g == 0:
                        pe.wait_ge(turn_lo, a + 1)
                    for i in range(HG):
                        last = product(pe, bank[1 + g % 2][:, i * P:(i + 1) * P],
                                       [qk0[:, s, HG * g + i, :] for s in range(2)],
                                       [xcT[:, par, s, 0:P] for s in range(2)])
                    last.then_inc(proj_done, 1)

                def project_v(a, par, j):
                    pe.wait_ge(proj_lo, 6 * a + G + j - 1)
                    product(pe, bank[1 + j][:, :], [xcT[:, par, s, P:2 * P] for s in range(2)],
                            [v0[:, s, 512 * j:512 * j + 512] for s in range(2)]).then_inc(proj_done, 1)

                def rough(a, par, g):
                    pe.wait_ge(proj_hi, 6 * a + g + 1)
                    ahead(pe, peak_done, G * a + g)
                    for i in range(HG):
                        last = pe.matmul(ROUGH[:, i * P:(i + 1) * P], t_s[:, par, 0, HG * g + i, :],
                                         xcT[:, par, 0, P:2 * P], start=True, stop=True)
                    last.then_inc(rough_done, 1)

                def turn_peak(a, split):
                    pe.wait_ge(peak_done, G * a + G)
                    pe.wait_ge(turn_lo, split)
                    pe.transpose(TURN[0:H, 0:P], peak[:, :], ident[:, :]).then_inc(peak_turned, 1)

                def scores(b, par, g):
                    n = G * b + g
                    to = bank[4 + g % 2]
                    pe.wait_ge(proj_lo, 6 * b + g + 1)
                    ahead(pe, exp_done, n - 1)
                    product(pe, to[:, :], [xcT[:, par, s, P:2 * P] for s in range(2)],
                            [t_s[:, par, s, HG * g:HG * g + HG, :].rearrange("p h q -> p (h q)") for s in range(2)],
                            stop=False)
                    pe.wait_ge(peakT_lo, b + 1)
                    for i in range(HG):
                        last = pe.matmul(to[:, i * P:(i + 1) * P], minus_one_at[:, HG * g + i, :],
                                         peakT[:, par, :], start=False, stop=(i == HG - 1))
                    last.then_inc(score_done, 1)

                def times_v(b, par, g):
                    n = G * b + g
                    pe.wait_ge(exp_done, n + 1)
                    pe.wait_ge(problo_done, n + 1)
                    pe.wait_ge(proj_lo, 6 * b + 6)
                    ahead(pe, norm_done, n)
                    for i in range(HG):
                        last = product(pe, PVB[:, i * (D0 + 1):(i + 1) * (D0 + 1)],
                                       [p[:, g % 2, i * P:(i + 1) * P] for p in (prob_hi, prob_lo)],
                                       [v_s[:, par, s, HG * g + i, :] for s in range(2)])
                    last.then_inc(pv_done, 1)

                def turn_o(b, g):
                    n = G * b + g
                    pe.wait_ge(norm_done, n + 1)
                    ahead(pe, oturn_lo, n)
                    if g == 0:
                        ahead(pe, res_done, b)
                    o = o_s[:, g % 2, :, :].rearrange("p h d -> p (h d)")
                    pe.transpose(OUTB[:, 0:P], o[:, 0:P], ident[:, :])
                    pe.transpose(OUTB[:, P:2 * P], o[:, P:2 * P], ident[:, :]).then_inc(oturn_done, 1)

                def output(b):
                    pe.wait_ge(oturn_lo, G * b + G)
                    for c in range(2 * G):
                        last = product(pe, OUTB[:, 0:P], [oT[:, s, c, :] for s in range(2)],
                                       [o0[:, s, c, :] for s in range(2)], start=(c == 0), stop=(c == 2 * G - 1))
                    last.then_inc(out_done, 1)

                def step(b, par, ctx_count=0, first=False, after=2):
                    a, ap = b + 1, 1 - par
                    if after >= 1:
                        project_t(a, ap, 0)
                    scores(b, par, 0)
                    if not first:
                        turn_o(b - 1, 2)
                        times_v(b - 1, ap, 3)
                    if after >= 1:
                        project_t(a, ap, 1)
                        rough(a, ap, 0)
                    scores(b, par, 1)
                    if not first:
                        turn_o(b - 1, 3)
                    if after >= 1:
                        project_t(a, ap, 2)
                        rough(a, ap, 1)
                    times_v(b, par, 0)
                    if not first:
                        output(b - 1)
                    scores(b, par, 2)
                    turn_o(b, 0)
                    times_v(b, par, 1)
                    if after >= 1:
                        project_t(a, ap, 3)
                        rough(a, ap, 2)
                    scores(b, par, 3)
                    if after >= 2:
                        turn(b + 2, par, ctx_count)
                    if after >= 1:
                        rough(a, ap, 3)
                        project_v(a, ap, 0)
                    turn_o(b, 1)
                    times_v(b, par, 2)
                    if after >= 1:
                        project_v(a, ap, 1)
                        turn_peak(a, b + 3 if after >= 2 else B)

                turn(0, 0, 16)
                for g in range(G):
                    project_t(0, 0, g)
                project_v(0, 0, 0)
                project_v(0, 0, 1)
                turn(1, 1, 16)
                for g in range(G):
                    rough(0, 0, g)
                turn_peak(0, 2)
                pe.wait_ge(blanks_ready, 3)
                step(0, 0, 32, first=True)
                with pe.Fori(0, QUADS) as i:
                    for j in range(1, 5):
                        step(4 * i + j, j % 2, 32 * i + 16 * (j // 2) + 32)
                step(B - 3, 1, 16 * (B // 2))
                step(B - 2, 0, after=1)
                step(B - 1, 1, after=0)
                turn_o(B - 1, 2)
                times_v(B - 1, 1, 3)
                turn_o(B - 1, 3)
                output(B - 1)


        with ExitStack() as ffn:
            def f_sb(name, shape, dt=F32):
                return sb(name, shape, dt, ffn)

            T = TILES
            SETS = B // T
            f_xn = f_sb("f_xn", [P, T, P])
            xT = f_sb("xT", [P, 2, 2, T, P + 1], F16)
            tanh_r = f_sb("tanh_r", [P, 2, T * P])
            relu_k = f_sb("relu_k", [P, 2, T * P])
            k_sq = f_sb("k_sq", [P, 2, T * P])
            k_s = f_sb("k_s", [P, 2, 2, T * P], F16)
            gated = f_sb("gated", [P, T * P])

            f_blank = sem("f_blank")
            f_xn_ready = sem("f_xn_ready")
            f_turn = sem("f_turn")
            f_turn_hi = sem("f_turn_hi")
            f_turn_lo = sem("f_turn_lo")
            f_r = sem("f_r")
            f_k = sem("f_k")
            f_tanh = sem("f_tanh")
            f_relu = sem("f_relu")
            f_sq = sem("f_sq")
            f_k_hi = sem("f_k_hi")
            f_k_lo = sem("f_k_lo")
            f_v = sem("f_v")
            f_gated = sem("f_gated")
            f_res = sem("f_res")
            f_stat = sem("f_stat")
            FT, FR, FK, FV = bank[0:2], bank[2:4], bank[4:6], bank[6:8]
            F_PAIRS = (SETS - 4) // 2

            def rows_of(s):
                return xs[:, bass.ds(T * s, T), :].rearrange("p t d -> p (t d)")

            with nc.Block() as block:
                @block.gpsimd
                def _(pool):
                    pool.memset(xT[:, :, :, :, 0:1], 0.0).then_inc(f_blank, 1)

                    def residual(s):
                        wait_beside(pool, f_gated, s + 1)
                        pool.tensor_tensor(rows_of(s), gated[:, :], rows_of(s), ALU.add).then_inc(f_res, 1)

                    def next_norm(i):
                        wait_beside(pool, f_stat, 2 * i + 2)
                        layer_norm(pool, 2, i, 2 * T * i, 2 * T)

                    residual(0)
                    residual(1)
                    with pool.Fori(1, SETS // 2) as i:
                        residual(2 * i)
                        next_norm(i - 1)
                        residual(2 * i + 1)
                    next_norm(SETS // 2 - 1)

                @block.scalar
                def _(act):
                    def hi_turned(a, par):
                        act.wait_ge(f_turn, a + 1)
                        act.activation(xT[:, par, 0, :, 1:P + 1], FT[par][:, :].rearrange("p (t q) -> p t q", q=P),
                                       ACT.Copy).then_inc(f_turn_hi, 1)

                    def tanh(s, par):
                        act.wait_ge(f_r, s + 1)
                        ahead(act, f_gated, s - 1)
                        act.activation(tanh_r[:, par, :], FR[par][:, :], ACT.Tanh, scale=0.5).then_inc(f_tanh, 1)

                    def relu(s, par):
                        act.wait_ge(f_k, s + 1)
                        ahead(act, f_sq, s - 1)
                        act.activation(relu_k[:, par, :], FK[par][:, :], ACT.Relu).then_inc(f_relu, 1)

                    def square(s, par):
                        act.wait_ge(f_relu, s + 1)
                        ahead(act, f_k_lo, s - 1)
                        act.activation(k_sq[:, par, :], relu_k[:, par, :], ACT.Square).then_inc(f_sq, 1)

                    def hi_k(s, par):
                        act.wait_ge(f_sq, s + 1)
                        act.activation(k_s[:, par, 0, :], k_sq[:, par, :], ACT.Copy).then_inc(f_k_hi, 1)

                    def step(s, par, last=False):
                        tanh(s, par)
                        if not last:
                            hi_turned(s + 1, 1 - par)
                        relu(s, par)
                        square(s, par)
                        hi_k(s, par)

                    act.wait_ge(f_blank, 1)
                    hi_turned(0, 0)
                    step(0, 0)
                    with act.Fori(0, (SETS - 2) // 2) as i:
                        step(2 * i + 1, 1)
                        step(2 * i + 2, 0)
                    step(SETS - 1, 1, last=True)

                @block.vector
                def _(dve):
                    def normalize(a):
                        ahead(dve, f_turn, a)
                        for t in range(T):
                            last = dve.tensor_scalar(f_xn[:, t, :],
                                                     xs[:, bass.ds(T * a + t, 1), :].rearrange("p a d -> p (a d)"),
                                                     mean[:, bass.ds(T * a + t, 1)],
                                                     rstd[:, bass.ds(T * a + t, 1)], ALU.subtract, ALU.mult)
                        last.then_inc(f_xn_ready, 1)

                    def lo_turned(a, par):
                        dve.wait_ge(f_turn_hi, a + 1)
                        dve.tensor_tensor(xT[:, par, 1, :, 1:P + 1], FT[par][:, :].rearrange("p (t q) -> p t q", q=P),
                                          xT[:, par, 0, :, 1:P + 1], ALU.subtract).then_inc(f_turn_lo, 1)

                    def lo_k(s, par):
                        dve.wait_ge(f_k_hi, s + 1)
                        dve.tensor_tensor(k_s[:, par, 1, :], k_sq[:, par, :], k_s[:, par, 0, :],
                                          ALU.subtract).then_inc(f_k_lo, 1)

                    def gate(s, par):
                        dve.wait_ge(f_v, s + 1)
                        ahead(dve, f_res, s)
                        dve.scalar_tensor_tensor(out=gated[:, :], in0=tanh_r[:, par, :], scalar=1.0,
                                                 in1=FV[par][:, :], op0=ALU.add, op1=ALU.mult).then_inc(f_gated, 1)

                    def statistics(s):
                        dve.wait_ge(f_res, s + 1)
                        for t in range(T):
                            last = dve.bn_stats(stat[:, bass.ds(T * s + t, 1), :], xs[:, bass.ds(T * s + t, 1), :])
                        last.then_inc(f_stat, 1)

                    def step(s, par, before=2, after=2):
                        if before >= 1:
                            lo_k(s - 1, 1 - par)
                        if after >= 1:
                            lo_turned(s + 1, 1 - par)
                        if after >= 2:
                            normalize(s + 2)
                        if before >= 2:
                            statistics(s - 2)
                        if before >= 1:
                            gate(s - 1, 1 - par)

                    dve.wait_ge(f_blank, 1)
                    normalize(0)
                    lo_turned(0, 0)
                    normalize(1)
                    step(0, 0, before=0)
                    step(1, 1, before=1)
                    with dve.Fori(0, F_PAIRS) as i:
                        step(2 * i + 2, 0)
                        step(2 * i + 3, 1)
                    step(SETS - 2, 0, after=1)
                    step(SETS - 1, 1, after=0)
                    lo_k(SETS - 1, 1)
                    statistics(SETS - 2)
                    gate(SETS - 1, 1)
                    statistics(SETS - 1)

                @block.tensor
                def _(pe):
                    def turn(a, par):
                        pe.wait_ge(f_xn_ready, a + 1)
                        ahead(pe, f_turn_lo, a - 1)
                        for t in range(T):
                            last = pe.transpose(FT[par][:, t * P:(t + 1) * P], f_xn[:, t, :], ident[:, :])
                        last.then_inc(f_turn, 1)

                    def weights(n):
                        return [mix[:, w, n, :] for w in range(2)]

                    def project_r(s, par):
                        pe.wait_ge(f_turn_lo, s + 1)
                        ahead(pe, f_tanh, s - 1)
                        for t in range(T):
                            to = FR[par][:, t * P:(t + 1) * P]
                            product(pe, to, [xT[:, par, w, t, 1:P + 1] for w in range(2)], weights(0), stop=False)
                            last = product(pe, to, [xT[:, par, w, t, 0:P] for w in range(2)], weights(1), start=False)
                        last.then_inc(f_r, 1)

                    def project_k(s, par):
                        ahead(pe, f_relu, s - 1)
                        to = FK[par][:, :].rearrange("p (t q) -> p t q", q=P)
                        product(pe, to, weights(2), [xT[:, par, w, :, 1:P + 1] for w in range(2)], stop=False)
                        product(pe, to, weights(3), [xT[:, par, w, :, 0:P] for w in range(2)], start=False).then_inc(f_k, 1)

                    def times_v(s, par):
                        pe.wait_ge(f_k_lo, s + 1)
                        for t in range(T):
                            last = product(pe, FV[par][:, t * P:(t + 1) * P],
                                           [k_s[:, par, w, t * P:(t + 1) * P] for w in range(2)], weights(4))
                        last.then_inc(f_v, 1)

                    def step(s, par, first=False, last=False):
                        project_r(s, par)
                        if not last:
                            turn(s + 1, 1 - par)
                        project_k(s, par)
                        if not first:
                            times_v(s - 1, 1 - par)

                    turn(0, 0)
                    step(0, 0, first=True)
                    with pe.Fori(0, (SETS - 2) // 2) as i:
                        step(2 * i + 1, 1)
                        step(2 * i + 2, 0)
                    step(SETS - 1, 1, last=True)
                    times_v(SETS - 1, 1)

        with ExitStack() as att:
            def b_sb(name, shape, dt=F32):
                return sb(name, shape, dt, att)

            yn = b_sb("yn", [P, P])
            ycT = b_sb("ycT", [P, 2, 2, 2 * P], F16)
            qk32 = b_sb("qk32", [P, 2, P])
            qk16 = b_sb("qk16", [P, 2, 2, P], F16)
            q_s = b_sb("q_s", [P, 2, 2, HG, P], F16)
            k_z = b_sb("k_z", [P, 2, G, 2, P], F16)
            v1 = b_sb("v1", [P, 2, 2, H, D1 + 1], F16)
            hide = b_sb("hide", [P, 2, P], BF16)
            peak1 = b_sb("peak1", [P, H])
            peak1c = b_sb("peak1c", [P, H])
            peak1T = b_sb("peak1T", [P, 2, P], BF16)
            pr = b_sb("pr", [P, 2, HG * P])
            pr_hi = b_sb("pr_hi", [P, 2, HG * P], F16)
            pr_lo = b_sb("pr_lo", [P, 2, HG * P], F16)
            inv1 = b_sb("inv1", [P, H])
            o1 = b_sb("o1", [P, H, D1])
            o1T = b_sb("o1T", [P, 2, P], F16)

            c_blank = sem("c_blank")
            c_xn = sem("c_xn")
            c_turn = sem("c_turn")
            c_turn_hi = sem("c_turn_hi")
            c_turn_lo = sem("c_turn_lo")
            c_qkv = sem("c_qkv")
            c_biased = sem("c_biased")
            c_v_hi = sem("c_v_hi")
            c_v_lo = sem("c_v_lo")
            c_qk_hi = sem("c_qk_hi")
            c_qk_lo = sem("c_qk_lo")
            c_slots = sem("c_slots")
            c_hide = sem("c_hide")
            c_rough = sem("c_rough")
            c_peak = sem("c_peak")
            c_peak_turn = sem("c_peak_turn")
            c_peak_hi = sem("c_peak_hi")
            c_peak_lo = sem("c_peak_lo")
            c_clip = sem("c_clip")
            c_score = sem("c_score")
            c_exp = sem("c_exp")
            c_lo = sem("c_lo")
            c_pv = sem("c_pv")
            c_inv = sem("c_inv")
            c_norm = sem("c_norm")
            c_oturn = sem("c_oturn")
            c_o_hi = sem("c_o_hi")
            c_o_lo = sem("c_o_lo")
            c_out = sem("c_out")
            c_res = sem("c_res")
            c_stat = sem("c_stat")
            TURN1, QKV, ROUGH1, PV1, OUT1 = bank[0], bank[1], bank[2:4], bank[6], bank[7]
            C_QUADS = (B - 4) // 4
            W = D1 + 1

            with nc.Block() as block:
                @block.sync
                def _(sp):
                    def load(c, par):
                        ahead(sp, c_turn, c - 1)
                        load_ctx(sp, ctx1, c, par, c_loaded)
                    with sp.Fori(0, B // 2 - 1) as i:
                        load(2 * i + 2, 0)
                        load(2 * i + 3, 1)

                @block.gpsimd
                def _(pool):
                    pool.memset(peak1T[:, :, :], 0.0).then_inc(c_blank, 1)
                    pool.memset(k_z[:, :, :, :, :], 0.0).then_inc(c_blank, 1)
                    pool.memset(v1[:, :, 0, :, D1:W], 1.0).then_inc(c_blank, 1)
                    pool.memset(v1[:, :, 1, :, D1:W], 0.0).then_inc(c_blank, 1)

                    def group(n, par):
                        pool.wait_ge(c_exp, n + 1)
                        ahead(pool, c_pv, n - 1)
                        pool.tensor_tensor(pr_lo[:, par, :], pr[:, par, :], pr_hi[:, par, :],
                                           ALU.subtract).then_inc(c_lo, 1)
                    for n in range(2 * G):
                        group(n, n % 2)
                    with pool.Fori(2, B) as b:
                        group(G * b, 0)
                        group(G * b + 1, 1)
                        group(G * b + 2, 0)
                        wait_beside(pool, c_stat, b - 1)
                        layer_norm_moments(pool, 3, b - 2, b - 2, 1)
                        group(G * b + 3, 1)
                        layer_norm_scale(pool, 3, b - 2, b - 2, 1)
                    for b in (B - 2, B - 1):
                        pool.wait_ge(c_stat, b + 1)
                        layer_norm(pool, 3, b, b, 1)

                @block.scalar
                def _(act):
                    def hi_turned(n, par):
                        act.wait_ge(c_turn, n + 1)
                        act.activation(ycT[:, par, 0, :], TURN1[:, 0:2 * P], ACT.Copy).then_inc(c_turn_hi, 1)

                    def hi_peak(a, par):
                        act.wait_ge(c_peak_turn, a + 1)
                        act.activation(peak1T[0:H, par, :], TURN1[0:H, 0:P], ACT.Copy).then_inc(c_peak_hi, 1)

                    def biased(a):
                        act.wait_ge(c_qkv, a + 1)
                        ahead(act, c_qk_lo, a)
                        act.activation(qk32[:, 0, :], QKV[:, 0:P], ACT.Identity, bias=bq_col)
                        act.activation(qk32[:, 1, :], QKV[:, P:2 * P], ACT.Identity, bias=bk_col).then_inc(c_biased, 1)

                    def hi_v(a, par):
                        act.wait_ge(c_qkv, a + 1)
                        ahead(act, c_pv, G * (a - 1))
                        act.activation(v1[:, par, 0, :, 0:D1], QKV[:, 2 * P:3 * P].rearrange("p (h d) -> p h d", d=D1),
                                       ACT.Copy).then_inc(c_v_hi, 1)

                    def exps(b, g):
                        n = G * b + g
                        act.wait_ge(c_score, n + 1)
                        ahead(act, c_lo, n - 1)
                        ahead(act, c_pv, n - 1)
                        act.activation(pr[:, g % 2, :], bank[4 + g % 2][:, :], ACT.Exp, scale=float(D1) ** -0.5)
                        act.activation(pr_hi[:, g % 2, :], bank[4 + g % 2][:, :], ACT.Exp, scale=float(D1) ** -0.5)\
                           .then_inc(c_exp, 1)

                    def hi_o(b):
                        act.wait_ge(c_oturn, b + 1)
                        act.activation(o1T[:, 0, :], OUT1[:, 0:P], ACT.Copy).then_inc(c_o_hi, 1)

                    def step(b, par, first=False, after=2):
                        a, ap = b + 1, 1 - par
                        if after >= 1:
                            biased(a)
                        exps(b, 0)
                        if after >= 1:
                            hi_v(a, ap)
                        exps(b, 1)
                        if after >= 2:
                            hi_turned(b + 2, par)
                        if not first:
                            hi_o(b - 1)
                        exps(b, 2)
                        exps(b, 3)
                        if after >= 1:
                            hi_peak(a, ap)

                    hi_turned(0, 0)
                    biased(0)
                    act.wait_ge(c_blank, 4)
                    hi_v(0, 0)
                    hi_turned(1, 1)
                    hi_peak(0, 0)
                    step(0, 0, first=True)
                    with act.Fori(0, C_QUADS) as i:
                        for j in range(1, 5):
                            step(4 * i + j, j % 2)
                    step(B - 3, 1)
                    step(B - 2, 0, after=1)
                    step(B - 1, 1, after=0)
                    hi_o(B - 1)

                @block.vector
                def _(dve):
                    def normalize(a):
                        ahead(dve, c_turn, a)
                        dve.tensor_scalar(yn[:, :], xs[:, bass.ds(a, 1), :].rearrange("p a d -> p (a d)"),
                                          mean[:, bass.ds(a, 1)],
                                          rstd[:, bass.ds(a, 1)], ALU.subtract, ALU.mult).then_inc(c_xn, 1)

                    def hide_masked(a, par):
                        ahead(dve, c_score, G * (a - 1))
                        dve.tensor_scalar(hide[:, par, :], masks[:, bass.ds(a, 1), :].rearrange("p a k -> p (a k)"),
                                          0, -BIG, ALU.is_equal, ALU.mult).then_inc(c_hide, 1)

                    def lo_turned(n, par):
                        dve.wait_ge(c_turn_hi, n + 1)
                        dve.tensor_tensor(ycT[:, par, 1, :], TURN1[:, 0:2 * P], ycT[:, par, 0, :], ALU.subtract).then_inc(c_turn_lo, 1)

                    def lo_peak(a, par):
                        dve.wait_ge(c_peak_hi, a + 1)
                        dve.tensor_tensor(peak1T[32:32 + H, par, :], TURN1[0:H, 0:P], peak1T[0:H, par, :],
                                          ALU.subtract).then_inc(c_peak_lo, 1)

                    def split_qk(a):
                        dve.wait_ge(c_biased, a + 1)
                        ahead(dve, c_slots, a)
                        dve.tensor_copy(qk16[:, :, 0, :], qk32[:, :, :]).then_inc(c_qk_hi, 1)

                    def split_qk_lo(a):
                        dve.wait_ge(c_qk_hi, a + 1)
                        dve.tensor_tensor(qk16[:, :, 1, :], qk32[:, :, :], qk16[:, :, 0, :], ALU.subtract).then_inc(c_qk_lo, 1)

                    def q_slots(a, par):
                        dve.wait_ge(c_qk_lo, a + 1)
                        for i in range(HG):
                            dve.tensor_scalar(q_s[:, par, :, i, :], qk16[:, 0, :, :], slot_of[:, i:i + 1], None, ALU.mult)

                    def k_slots(par):
                        for j in range(G):
                            rows = slice(32 * j, 32 * j + 32)
                            last = dve.tensor_copy(k_z[rows, par, j, :, :], qk16[rows, 1, :, :])
                        last.then_inc(c_slots, 1)

                    def lo_v(a, par):
                        dve.wait_ge(c_v_hi, a + 1)
                        dve.tensor_tensor(v1[:, par, 1, :, 0:D1], QKV[:, 2 * P:3 * P].rearrange("p (h d) -> p h d", d=D1),
                                          v1[:, par, 0, :, 0:D1], ALU.subtract).then_inc(c_v_lo, 1)

                    def maxima(a, g):
                        dve.wait_ge(c_rough, G * a + g + 1)
                        dve.tensor_reduce(peak1[:, HG * g:HG * g + HG],
                                          ROUGH1[g % 2][:, :].rearrange("p (h k) -> p h k", k=P),
                                          AX.X, ALU.max).then_inc(c_peak, 1)

                    def clip(a):
                        dve.wait_ge(c_peak, G * a + G)
                        dve.tensor_scalar(peak1c[:, :], peak1[:, :], -BIG / 16, None, ALU.max).then_inc(c_clip, 1)

                    def norm(b):
                        dve.wait_ge(c_pv, G * b + G)
                        o = PV1[:, 0:H * W].rearrange("p (h d) -> p h d", d=W)
                        dve.reciprocal(inv1[:, :], o[:, :, D1]).then_inc(c_inv, 1)
                        dve.wait_ge(c_inv, b + 1)
                        ahead(dve, c_oturn, b)
                        dve.tensor_tensor(o1[:, :, :], o[:, :, 0:D1],
                                          inv1[:, :].unsqueeze(2).broadcast_to([P, H, D1]), ALU.mult).then_inc(c_norm, 1)

                    def lo_o(b):
                        dve.wait_ge(c_o_hi, b + 1)
                        dve.tensor_tensor(o1T[:, 1, :], OUT1[:, 0:P], o1T[:, 0, :], ALU.subtract).then_inc(c_o_lo, 1)

                    def residual(b):
                        dve.wait_ge(c_out, b + 1)
                        here = xs[:, bass.ds(b, 1), :].rearrange("p a d -> p (a d)")
                        dve.tensor_tensor(here, OUT1[:, 0:P], here, ALU.add).then_inc(c_res, 1)
                        dve.wait_ge(c_res, b + 1)
                        dve.bn_stats(stat[:, bass.ds(b, 1), :], xs[:, bass.ds(b, 1), :]).then_inc(c_stat, 1)

                    def step(b, par, first=False, after=2):
                        a, ap = b + 1, 1 - par
                        if after >= 1:
                            split_qk(a)
                            split_qk_lo(a)
                            q_slots(a, ap)
                        if not first:
                            norm(b - 1)
                        if after >= 1:
                            k_slots(ap)
                            lo_v(a, ap)
                        if after >= 2:
                            lo_turned(b + 2, par)
                        if not first:
                            lo_o(b - 1)
                        if after >= 3:
                            normalize(b + 3)
                        if after >= 1:
                            for g in range(G):
                                maxima(a, g)
                            clip(a)
                        if not first:
                            residual(b - 1)
                        if after >= 1:
                            lo_peak(a, ap)
                        if after >= 2:
                            hide_masked(b + 2, par)

                    normalize(0)
                    dve.wait_ge(masks_loaded, 16)
                    hide_masked(0, 0)
                    lo_turned(0, 0)
                    normalize(1)
                    split_qk(0)
                    split_qk_lo(0)
                    q_slots(0, 0)
                    dve.wait_ge(c_blank, 4)
                    k_slots(0)
                    lo_v(0, 0)
                    lo_turned(1, 1)
                    hide_masked(1, 1)
                    normalize(2)
                    for g in range(G):
                        maxima(0, g)
                    clip(0)
                    lo_peak(0, 0)
                    step(0, 0, first=True, after=3)
                    with dve.Fori(0, C_QUADS) as i:
                        for j in range(1, 5):
                            step(4 * i + j, j % 2, after=3)
                    step(B - 3, 1)
                    step(B - 2, 0, after=1)
                    step(B - 1, 1, after=0)
                    norm(B - 1)
                    lo_o(B - 1)
                    residual(B - 1)

                @block.tensor
                def _(pe):
                    def turn(a, par, ctx_count):
                        pe.wait_ge(c_xn, a + 1)
                        pe.wait_ge(c_loaded[par], ctx_count)
                        ahead(pe, c_peak_lo, a - 1)
                        pe.transpose(TURN1[:, 0:P], yn[:, :], ident[:, :])
                        pe.transpose(TURN1[:, P:2 * P], ctx1[:, par, :], ident[:, :]).then_inc(c_turn, 1)

                    def project(a, par):
                        pe.wait_ge(c_turn_lo, a + 1)
                        ahead(pe, c_v_lo, a)
                        xT_, cT_ = ([ycT[:, par, s, w * P:(w + 1) * P] for s in range(2)] for w in range(2))
                        wq, wk, wv = ([att1[:, s, n, :] for s in range(2)] for n in range(3))
                        product(pe, QKV[:, 0:P], wq, xT_)
                        product(pe, QKV[:, P:2 * P], wk, cT_)
                        product(pe, QKV[:, 2 * P:3 * P], cT_, wv).then_inc(c_qkv, 1)

                    def rough(a, par, g):
                        pe.wait_ge(c_slots, a + 1)
                        pe.wait_ge(c_hide, a + 1)
                        ahead(pe, c_peak, G * a + g - 1)
                        to = ROUGH1[g % 2]
                        pe.matmul(to[:, :].rearrange("p (h k) -> p h k", k=P), ident4[:, 0, :],
                                  hide[:, par, :].unsqueeze(1).broadcast_to([P, HG, P]), start=True, stop=False)
                        for i in range(HG):
                            last = pe.matmul(to[:, i * P:(i + 1) * P], q_s[:, par, 0, i, :], k_z[:, par, g, 0, :],
                                             start=False, stop=(i == HG - 1))
                        last.then_inc(c_rough, 1)

                    def turn_peak(a, turned):
                        pe.wait_ge(c_clip, a + 1)
                        pe.wait_ge(c_turn_lo, turned)
                        pe.transpose(TURN1[0:H, 0:P], peak1c[:, :], ident[:, :]).then_inc(c_peak_turn, 1)

                    def scores(b, par, g):
                        n = G * b + g
                        to = bank[4 + g % 2]
                        ahead(pe, c_exp, n - 1)
                        product(pe, to[:, :], [k_z[:, par, g, s, :] for s in range(2)],
                                [q_s[:, par, s, :, :].rearrange("p i q -> p (i q)") for s in range(2)], stop=False)
                        pe.matmul(to[:, :], hide[:, par, :], ident4[:, :, :].rearrange("p i q -> p (i q)"),
                                  start=False, stop=False)
                        pe.wait_ge(c_peak_lo, b + 1)
                        for i in range(HG):
                            last = pe.matmul(to[:, i * P:(i + 1) * P], minus_one_at[:, HG * g + i, :],
                                             peak1T[:, par, :], start=False, stop=(i == HG - 1))
                        last.then_inc(c_score, 1)

                    def times_v(b, par, g):
                        n = G * b + g
                        pe.wait_ge(c_exp, n + 1)
                        pe.wait_ge(c_lo, n + 1)
                        if g == 0:
                            ahead(pe, c_norm, b)
                        for i in range(HG):
                            h = HG * g + i
                            last = product(pe, PV1[:, h * W:(h + 1) * W],
                                           [p[:, g % 2, i * P:(i + 1) * P] for p in (pr_hi, pr_lo)],
                                           [v1[:, par, s, h, :] for s in range(2)])
                        last.then_inc(c_pv, 1)

                    def turn_o(b):
                        pe.wait_ge(c_norm, b + 1)
                        ahead(pe, c_res, b)
                        pe.transpose(OUT1[:, 0:P], o1[:, :, :].rearrange("p h d -> p (h d)"), ident[:, :]).then_inc(c_oturn, 1)

                    def output(b):
                        pe.wait_ge(c_o_lo, b + 1)
                        product(pe, OUT1[:, 0:P], [o1T[:, s, :] for s in range(2)], [att1[:, s, 3, :] for s in range(2)],
                                stop=False)
                        pe.matmul(OUT1[:, 0:P], ones16[:, :], bias1[:, 0, :], start=False, stop=False)
                        pe.matmul(OUT1[:, 0:P], ones16[:, :], bias1[:, 1, :], start=False, stop=True).then_inc(c_out, 1)

                    def step(b, par, ctx_count=0, first=False, after=2):
                        a, ap = b + 1, 1 - par
                        if after >= 1:
                            project(a, ap)
                        scores(b, par, 0)
                        scores(b, par, 1)
                        if not first:
                            times_v(b - 1, ap, 3)
                        if after >= 2:
                            turn(b + 2, par, ctx_count)
                        scores(b, par, 2)
                        if not first:
                            turn_o(b - 1)
                        times_v(b, par, 0)
                        if after >= 1:
                            rough(a, ap, 0)
                            rough(a, ap, 1)
                        if not first:
                            output(b - 1)
                        times_v(b, par, 1)
                        if after >= 1:
                            rough(a, ap, 2)
                            rough(a, ap, 3)
                        scores(b, par, 3)
                        if after >= 1:
                            turn_peak(a, b + 3 if after >= 2 else B)
                        times_v(b, par, 2)

                    turn(0, 0, 16)
                    project(0, 0)
                    turn(1, 1, 16)
                    for g in range(G):
                        rough(0, 0, g)
                    turn_peak(0, 2)
                    step(0, 0, 32, first=True)
                    with pe.Fori(0, C_QUADS) as i:
                        for j in range(1, 5):
                            step(4 * i + j, j % 2, 32 * i + 16 * (j // 2) + 32)
                    step(B - 3, 1, 16 * (B // 2))
                    step(B - 2, 0, after=1)
                    step(B - 1, 1, after=0)
                    times_v(B - 1, 1, 3)
                    turn_o(B - 1)
                    output(B - 1)


        with ExitStack() as moe:
            def m_sb(name, shape, dt=F32):
                return sb(name, shape, dt, moe)

            T = TILES
            SETS = B // T
            zn = m_sb("zn", [P, T, P])
            zT = m_sb("zT", [P, 2, 2, T * P], F16)
            logits = m_sb("logits", [P, T, E])
            top = m_sb("top", [P, T, 8])
            top_at = m_sb("top_at", [P, T, 8], U32)
            two_at = m_sb("two_at", [P, T, 2])
            lead = m_sb("lead", [P, T])
            tanh_lead = m_sb("tanh_lead", [P, T])
            two_gates = m_sb("two_gates", [P, T, 2])
            picked = m_sb("picked", [P, T, 2, E])
            picked_gate = m_sb("picked_gate", [P, T, 2, E])
            gate = m_sb("gate", [P, 2, T, E])
            gateT = m_sb("gateT", [E, T * P])
            silu = m_sb("silu", [P, C, T * P])
            g32 = m_sb("g32", [P, C, T * P])
            g_s = m_sb("g_s", [P, 2, C, 2, T * P], F16)
            acc = m_sb("acc", [P, 2, T, P])

            z_norm = sem("z_norm")
            z_turn = sem("z_turn")
            z_hi = sem("z_hi")
            z_lo = sem("z_lo")
            z_logits = sem("z_logits")
            z_kept = sem("z_kept")
            z_ranked = sem("z_ranked")
            z_top = sem("z_top")
            z_at = sem("z_at")
            z_lead = sem("z_lead")
            z_tanh = sem("z_tanh")
            z_two = sem("z_two")
            z_picked = sem("z_picked")
            z_pgate = sem("z_pgate")
            z_gate = sem("z_gate")
            z_gturn = sem("z_gturn")
            z_gateT = sem("z_gateT")
            z_b2 = sem("z_b2")
            z_start = sem("z_start")
            h1_done = sem("h1_done")
            h3_done = sem("h3_done")
            silu_done = sem("silu_done")
            g_done = sem("g_done")
            g_hi = sem("g_hi")
            g_lo = sem("g_lo")
            y_done = sem("y_done")
            acc_done = sem("acc_done")
            set_stored = [sem(f"set_stored{i}") for i in range(2)]
            H1B, H3B, YB, TURNB, SMALLB = bank[0:2], bank[2:4], bank[4:6], bank[6], bank[7]
            S_PAIRS = (SETS - 2) // 2

            with nc.Block() as block:
                @block.sync
                def _(sp):
                    def store(s, par):
                        sp.wait_ge(acc_done, T * E * (s + 1))
                        sp.dma_start(out[bass.ds(T * s, T), :, :].rearrange("b s d -> s b d"), acc[:, par, :, :])\
                          .then_inc(set_stored[par], 16)
                    with sp.Fori(0, SETS // 2) as i:
                        store(2 * i, 0)
                        store(2 * i + 1, 1)
                    for par in range(2):
                        sp.wait_ge(set_stored[par], 16 * (SETS // 2))

                @block.gpsimd
                def _(pool):
                    def lo_g(s, e):
                        for c in range(C):
                            v = E * C * s + C * e + c
                            pool.wait_ge(g_hi, v + 1)
                            ahead(pool, y_done, E * s + e - 1)
                            pool.tensor_tensor(g_s[:, e % 2, c, 1, :], g32[:, c, :], g_s[:, e % 2, c, 0, :],
                                               ALU.subtract).then_inc(g_lo, 1)
                    for e in range(E):
                        lo_g(0, e)
                    with pool.Fori(1, SETS) as s:
                        for e in range(E):
                            lo_g(s, e)

                @block.scalar
                def _(act):
                    def hi_turned(a, par):
                        act.wait_ge(z_turn, a + 1)
                        act.activation(zT[:, par, 0, :], TURNB[:, :], ACT.Copy).then_inc(z_hi, 1)

                    def tanh(a):
                        act.wait_ge(z_lead, a + 1)
                        act.activation(tanh_lead[:, :], lead[:, :], ACT.Tanh, scale=0.5).then_inc(z_tanh, 1)

                    def keep_gateT(a):
                        act.wait_ge(z_gturn, a + 1)
                        act.activation(gateT[:, :], SMALLB[0:E, :], ACT.Copy).then_inc(z_gateT, 1)

                    def silu_h1(s, e, c):
                        v = E * C * s + C * e + c
                        act.wait_ge(h1_done, v + 1)
                        ahead(act, g_done, v - 1)
                        act.activation(silu[:, c, :], H1B[c][:, :], ACT.Silu,
                                       bias=b1_col[:, C * e + c:C * e + c + 1]).then_inc(silu_done, 1)

                    def hi_g(s, e, c):
                        v = E * C * s + C * e + c
                        act.wait_ge(g_done, v + 1)
                        ahead(act, y_done, E * s + e - 1)
                        act.activation(g_s[:, e % 2, c, 0, :], g32[:, c, :], ACT.Copy).then_inc(g_hi, 1)

                    def step(s, par, last=False):
                        for e in range(E):
                            silu_h1(s, e, 0)
                            silu_h1(s, e, 1)
                            hi_g(s, e, 0)
                            hi_g(s, e, 1)
                            if not last:
                                if e == 1:
                                    hi_turned(s + 1, 1 - par)
                                if e == 3:
                                    tanh(s + 1)
                                if e == 5:
                                    keep_gateT(s + 1)

                    hi_turned(0, 0)
                    tanh(0)
                    keep_gateT(0)
                    step(0, 0)
                    with act.Fori(0, S_PAIRS) as i:
                        step(2 * i + 1, 1)
                        step(2 * i + 2, 0)
                    step(SETS - 1, 1, last=True)

                @block.vector
                def _(dve):
                    def normalize(a):
                        ahead(dve, z_turn, a)
                        for t in range(T):
                            last = dve.tensor_scalar(zn[:, t, :], xs[:, bass.ds(T * a + t, 1), :].rearrange("p a d -> p (a d)"),
                                                     mean[:, bass.ds(T * a + t, 1)],
                                                     rstd[:, bass.ds(T * a + t, 1)], ALU.subtract, ALU.mult)
                        last.then_inc(z_norm, 1)

                    def lo_turned(a, par):
                        dve.wait_ge(z_hi, a + 1)
                        dve.tensor_tensor(zT[:, par, 1, :], TURNB[:, :], zT[:, par, 0, :], ALU.subtract).then_inc(z_lo, 1)

                    def rank(a):
                        dve.wait_ge(z_logits, a + 1)
                        ahead(dve, z_top, a)
                        dve.tensor_copy(logits[:, :, :].rearrange("p t e -> p (t e)"), SMALLB[:, 0:T * E]).then_inc(z_kept, 1)
                        dve.wait_ge(ln_ready[0], 1)
                        dve.wait_ge(z_kept, a + 1)
                        ahead(dve, z_pgate, a)
                        for t in range(T):
                            dve.max(top[:, t, :], logits[:, t, :]).then_inc(z_ranked, 1)
                        dve.wait_ge(z_ranked, T * (a + 1))
                        dve.tensor_tensor(lead[:, :], top[:, :, 0], top[:, :, 1], ALU.subtract).then_inc(z_lead, 1)
                        for t in range(T):
                            last = dve.max_index(top_at[:, t, :], top[:, t, :], logits[:, t, :])
                        last.then_inc(z_top, 1)
                        dve.wait_ge(z_top, a + 1)
                        ahead(dve, z_picked, a)
                        dve.tensor_copy(two_at[:, :, :], top_at[:, :, 0:2]).then_inc(z_at, 1)

                    def route(a, par):
                        dve.wait_ge(z_tanh, a + 1)
                        ahead(dve, z_pgate, a)
                        dve.tensor_scalar(two_gates[:, :, 0], tanh_lead[:, :], half_gain[:, 3:4], half_gain[:, 3:4],
                                          ALU.mult, ALU.add)
                        dve.tensor_scalar(two_gates[:, :, 1], tanh_lead[:, :], minus_half_gain[:, 3:4], half_gain[:, 3:4],
                                          ALU.mult, ALU.add).then_inc(z_two, 1)
                        dve.wait_ge(z_at, a + 1)
                        dve.tensor_tensor(picked[:, :, :, :],
                                          experts[:, :].unsqueeze(1).unsqueeze(1).broadcast_to([P, T, 2, E]),
                                          two_at[:, :, :].unsqueeze(3).broadcast_to([P, T, 2, E]), ALU.is_equal)\
                           .then_inc(z_picked, 1)
                        dve.wait_ge(z_two, a + 1)
                        dve.wait_ge(z_picked, a + 1)
                        ahead(dve, z_gate, a)
                        dve.tensor_tensor(picked_gate[:, :, :, :], picked[:, :, :, :],
                                          two_gates[:, :, :].unsqueeze(3).broadcast_to([P, T, 2, E]), ALU.mult)\
                           .then_inc(z_pgate, 1)
                        dve.wait_ge(z_pgate, a + 1)
                        ahead(dve, acc_done, T * E * (a - 1))
                        dve.tensor_tensor(gate[:, par, :, :], picked_gate[:, :, 0, :], picked_gate[:, :, 1, :], ALU.add)\
                           .then_inc(z_gate, 1)

                    def begin(a, par, stores):
                        dve.wait_ge(z_b2, a + 1)
                        ahead(dve, set_stored[par], stores)
                        dve.tensor_tensor(acc[:, par, :, :].rearrange("p t d -> p (t d)"), SMALLB[:, :],
                                          xs[:, bass.ds(T * a, T), :].rearrange("p t d -> p (t d)"), ALU.add)\
                           .then_inc(z_start, 1)

                    def gated(s, e):
                        for c in range(C):
                            v = E * C * s + C * e + c
                            dve.wait_ge(h3_done, v + 1)
                            dve.wait_ge(silu_done, v + 1)
                            ahead(dve, g_lo, v - 1)
                            dve.scalar_tensor_tensor(out=g32[:, c, :], in0=H3B[c][:, :],
                                                     scalar=b3_col[:, C * e + c:C * e + c + 1], in1=silu[:, c, :],
                                                     op0=ALU.add, op1=ALU.mult).then_inc(g_done, 1)

                    def accumulate(s, par, e):
                        u = E * s + e
                        dve.wait_ge(y_done, u + 1)
                        dve.wait_ge(z_start, s + 1)
                        ahead(dve, acc_done, T * u)
                        for t in range(T):
                            dve.scalar_tensor_tensor(out=acc[:, par, t, :], in0=YB[e % 2][:, t * P:(t + 1) * P],
                                                     scalar=gate[:, par, t, e:e + 1], in1=acc[:, par, t, :],
                                                     op0=ALU.mult, op1=ALU.add).then_inc(acc_done, 1)

                    def step(s, par, stores=0, first=False, last=False):
                        for e in range(E):
                            gated(s, e)
                            if e > 0:
                                accumulate(s, par, e - 1)
                            elif not first:
                                accumulate(s - 1, 1 - par, E - 1)
                            if not last:
                                if e == 0:
                                    normalize(s + 1)
                                if e == 2:
                                    lo_turned(s + 1, 1 - par)
                                if e == 3:
                                    rank(s + 1)
                                if e == 4:
                                    route(s + 1, 1 - par)
                                if e == 7:
                                    begin(s + 1, 1 - par, stores)

                    normalize(0)
                    lo_turned(0, 0)
                    rank(0)
                    route(0, 0)
                    begin(0, 0, 0)
                    step(0, 0, 0, first=True)
                    with dve.Fori(0, S_PAIRS) as i:
                        step(2 * i + 1, 1, 16 * i + 16)
                        step(2 * i + 2, 0, 16 * i + 16)
                    step(SETS - 1, 1, last=True)
                    accumulate(SETS - 1, 1, E - 1)

                @block.tensor
                def _(pe):
                    def turn(a):
                        pe.wait_ge(z_norm, a + 1)
                        ahead(pe, z_lo, a)
                        for t in range(T):
                            last = pe.transpose(TURNB[:, t * P:(t + 1) * P], zn[:, t, :], ident[:, :])
                        last.then_inc(z_turn, 1)

                    def score_experts(a, par):
                        pe.wait_ge(z_lo, a + 1)
                        ahead(pe, z_start, a)
                        for t in range(T):
                            last = product(pe, SMALLB[:, t * E:(t + 1) * E],
                                           [zT[:, par, w, t * P:(t + 1) * P] for w in range(2)],
                                           [router[:, w, :] for w in range(2)])
                        last.then_inc(z_logits, 1)

                    def turn_gates(a, par):
                        pe.wait_ge(z_gate, a + 1)
                        for t in range(T):
                            last = pe.transpose(SMALLB[0:E, t * P:(t + 1) * P], gate[:, par, t, :], ident[:, :])
                        last.then_inc(z_gturn, 1)

                    def gates_b2(a):
                        pe.wait_ge(z_gateT, a + 1)
                        for t in range(T):
                            last = pe.matmul(SMALLB[:, t * P:(t + 1) * P], gateT[:, t * P:(t + 1) * P], b2_row[:, :],
                                             start=True, stop=True)
                        last.then_inc(z_b2, 1)

                    def hidden(s, par, e):
                        for c in range(C):
                            v = E * C * s + C * e + c
                            z = [zT[:, par, w, :] for w in range(2)]
                            if c == 0 and e == 0:
                                pe.wait_ge(z_lo, s + 1)
                            ahead(pe, silu_done, v - 1)
                            product(pe, H1B[c][:, :], [up1[:, w, C * e + c, :] for w in range(2)], z).then_inc(h1_done, 1)
                            ahead(pe, g_done, v - 1)
                            product(pe, H3B[c][:, :], [up3[:, w, C * e + c, :] for w in range(2)], z).then_inc(h3_done, 1)

                    def down_project(s, e):
                        u = E * s + e
                        pe.wait_ge(g_lo, C * (u + 1))
                        ahead(pe, acc_done, T * (u - 1))
                        for c in range(C):
                            for t in range(T):
                                last = product(pe, YB[e % 2][:, t * P:(t + 1) * P],
                                               [g_s[:, e % 2, c, w, t * P:(t + 1) * P] for w in range(2)],
                                               [down[:, w, C * e + c, :] for w in range(2)],
                                               start=(c == 0 and t == 0), stop=(c == C - 1 and t == T - 1))
                        last.then_inc(y_done, 1)

                    def step(s, par, first=False, last=False):
                        for e in range(E):
                            hidden(s, par, e)
                            if e > 0:
                                down_project(s, e - 1)
                            elif not first:
                                down_project(s - 1, E - 1)
                            if not last:
                                if e == 1:
                                    turn(s + 1)
                                if e == 3:
                                    score_experts(s + 1, 1 - par)
                                if e == 5:
                                    turn_gates(s + 1, 1 - par)
                                if e == 6:
                                    gates_b2(s + 1)

                    turn(0)
                    score_experts(0, 0)
                    turn_gates(0, 0)
                    gates_b2(0)
                    step(0, 0, first=True)
                    with pe.Fori(0, S_PAIRS) as i:
                        step(2 * i + 1, 1)
                        step(2 * i + 2, 0)
                    step(SETS - 1, 1, last=True)
                    down_project(SETS - 1, E - 1)


_INS = ["x", "ctx_1024", "mask_BxSxS2_if1", "g_xattn", "g_ffn",
        "L0_xattn_w_q", "L0_xattn_w_k", "L0_xattn_w_v", "L0_xattn_w_o",
        "L0_ffn_W_r", "L0_ffn_W_k", "L0_ffn_W_v", "L0_ffn_mu_r", "L0_ffn_mu_k",
        "L1_xattn_Wq", "L1_xattn_bq", "L1_xattn_Wk", "L1_xattn_bk", "L1_xattn_Wv", "L1_xattn_bv",
        "L1_xattn_Wo", "L1_xattn_bo", "L1_ffn_Wg", "L1_ffn_W1", "L1_ffn_b1", "L1_ffn_A1", "L1_ffn_B1",
        "L1_ffn_W2", "L1_ffn_b2", "L1_ffn_A2", "L1_ffn_B2", "L1_ffn_W3", "L1_ffn_b3", "L1_ffn_A3",
        "L1_ffn_B3"]


def kernel(**inputs):
    import numpy as np
    import concourse.bacc as bacc
    from concourse.bass_utils import run_bass_kernel_spmd

    nc = bacc.Bacc("TRN2", target_bir_lowering=False, num_devices=1)
    arrays, args = {}, []
    for name in _INS:
        a = np.ascontiguousarray(inputs[name])
        arrays[name] = a
        args.append(nc.dram_tensor(name, a.shape, mybir.dt.from_np(a.dtype), kind="ExternalInput").ap())
    args.append(nc.dram_tensor("x_out", arrays["x"].shape, F32, kind="ExternalOutput").ap())
    gated_layers(nc, *args)
    result = run_bass_kernel_spmd(nc, [arrays], core_ids=[0])
    return result.results[0]["x_out"]
```
